# Optimizing a Trainium2 kernel written in Bass

```python
import numpy as np
import jax
import jax.numpy as jnp

def _softmax(x, axis=-1):
    return jax.nn.softmax(x, axis=axis)

def _gelu(x):
    return jax.nn.gelu(x, approximate=True)

def _silu(x):
    return jax.nn.silu(x)

def _sigmoid(x):
    return jax.nn.sigmoid(x)

def _layernorm(x, axis=-1, eps=1e-05):
    m = jnp.mean(x, axis=axis, keepdims=True)
    v = jnp.var(x, axis=axis, keepdims=True)
    return (x - m) / jnp.sqrt(v + eps)

def _scatter_add(tgt, idx, src, axis=0):
    return tgt.at[idx].add(src)

def _segment_sum(src, seg, n):
    return jax.ops.segment_sum(src, seg, n)
kernel_name = 'mk_xattn_ffn_d2_seqx_r8_39718b'

def setup_inputs(seed: int=0):
    np.random.seed(seed)
    _w = jnp.asarray

    def _rec_inputs():
        import jax
        import jax.numpy as jnp
        _rk = jax.random.key(seed)
        x = 7.22e-05 + 1 * jax.random.normal(jax.random.fold_in(_rk, 1), (64, 128, 128), jnp.float32)
        _lenS = 128 - jax.random.randint(jax.random.fold_in(_rk, 7), (64,), 0, max(1, 128 // 4) + 1, jnp.int32)
        _lenS2 = 77 - jax.random.randint(jax.random.fold_in(_rk, 8), (64,), 0, max(1, 77 // 4) + 1, jnp.int32)
        _ctx_1024P = jax.random.normal(jax.random.fold_in(_rk, 11), (64, 16, 128), jnp.float32)
        _ctx_1024c = jax.random.dirichlet(jax.random.fold_in(_rk, 511), 0.3 * jnp.ones((16,), jnp.float32), (64, 77))
        _ctx_1024t = jnp.einsum('bsk,bkd->bsd', _ctx_1024c, _ctx_1024P)
        _ctx_1024t = _ctx_1024t * jax.lax.rsqrt(jnp.mean(jnp.square(_ctx_1024t)) + 1e-12) * 0.953939
        ctx_1024 = 4.13588e-05 + 0.999923 * (_ctx_1024t + 0.3 * jax.random.normal(jax.random.fold_in(_rk, 611), (64, 77, 128), jnp.float32))
        return (x, ctx_1024)
    x, ctx_1024 = _rec_inputs()

    def _L0_xattn_setup():
        import jax, jax.numpy as jnp
        import numpy as np
        H = 16
        D_K = 128
        D_V = 128
        D_MODEL = 128
        B = 4
        S = 256

        def _split_heads(x):
            b, s, d = x.shape
            return x.reshape(b, s, H, d // H).transpose(0, 2, 1, 3)
        key = jax.random.key(seed)
        ks = jax.random.split(key, 11)
        sc_in = 1.0 / np.sqrt(D_MODEL).astype(np.float32)
        sc_k = 1.0 / np.sqrt(D_K).astype(np.float32)
        return {'queries': jax.random.normal(ks[0], (B, S, D_MODEL), jnp.float32), 'keys': jax.random.normal(ks[1], (B, S, D_MODEL), jnp.float32), 'values': jax.random.normal(ks[2], (B, S, D_MODEL), jnp.float32), 'Wq': jax.random.normal(ks[3], (D_MODEL, D_K), jnp.float32) * sc_in, 'bq': jnp.zeros((D_K,), jnp.float32), 'Wk': jax.random.normal(ks[4], (D_MODEL, D_K), jnp.float32) * sc_in, 'bk': jnp.zeros((D_K,), jnp.float32), 'Wv': jax.random.normal(ks[5], (D_MODEL, D_V), jnp.float32) * sc_in, 'bv': jnp.zeros((D_V,), jnp.float32), 'Wo': jax.random.normal(ks[6], (D_K, D_MODEL), jnp.float32) * sc_k, 'bo': jnp.zeros((D_MODEL,), jnp.float32)}
    _L0_xattn_all = _L0_xattn_setup()
    _L0_xattn_in = {k: v for k, v in _L0_xattn_all.items() if k in ('Wq', 'bq', 'Wk', 'bk', 'Wv', 'bv', 'Wo', 'bo')}
    del _L0_xattn_all

    def _L0_ffn_setup():
        import jax, jax.numpy as jnp
        import numpy as np
        EMB = 128
        FF = 4 * EMB

        def _ternary(w):
            scale = jnp.maximum(jnp.mean(jnp.abs(w)), 1e-08)
            w_t = jnp.clip(jnp.round(w / scale), -1.0, 1.0)
            return w + jax.lax.stop_gradient(w_t - w)
        key = jax.random.key(seed)
        kx, k1, k2, kb1, kb2 = jax.random.split(key, 5)
        x = jax.random.normal(kx, (4, 256, EMB), dtype=jnp.float32)
        lim1 = 1.0 / np.sqrt(EMB)
        lim2 = 1.0 / np.sqrt(FF)
        W1 = jax.random.uniform(k1, (FF, EMB), jnp.float32, -lim1, lim1)
        b1 = jax.random.uniform(kb1, (FF,), jnp.float32, -lim1, lim1)
        W2 = jax.random.uniform(k2, (EMB, FF), jnp.float32, -lim2, lim2)
        b2 = jax.random.uniform(kb2, (EMB,), jnp.float32, -lim2, lim2)
        return {'x': x, 'W1': W1, 'b1': b1, 'W2': W2, 'b2': b2}
    _L0_ffn_all = _L0_ffn_setup()
    _L0_ffn_in = {k: v for k, v in _L0_ffn_all.items() if k in ('W1', 'b1', 'W2', 'b2')}
    del _L0_ffn_all

    def _L1_xattn_setup():
        import jax, jax.numpy as jnp
        import numpy as np
        IN_CH = 128
        ATT_DIM = 128
        B, L1, L2 = (8, 256, 256)
        key = jax.random.key(seed)
        ks = jax.random.split(key, 8)
        s = 1.0 / np.sqrt(IN_CH)
        return {'input_1': jax.random.normal(ks[0], (B, L1, IN_CH), dtype=jnp.float32), 'input_2': jax.random.normal(ks[1], (B, L2, IN_CH), dtype=jnp.float32), 'Wq': jax.random.uniform(ks[2], (IN_CH, ATT_DIM), jnp.float32, -s, s), 'bq': jnp.zeros((ATT_DIM,), jnp.float32), 'Wk': jax.random.uniform(ks[3], (IN_CH, ATT_DIM), jnp.float32, -s, s), 'bk': jnp.zeros((ATT_DIM,), jnp.float32), 'Wv': jax.random.uniform(ks[4], (IN_CH, ATT_DIM), jnp.float32, -s, s), 'bv': jnp.zeros((ATT_DIM,), jnp.float32)}
    _L1_xattn_all = _L1_xattn_setup()
    _L1_xattn_in = {k: v for k, v in _L1_xattn_all.items() if k in ('Wq', 'bq', 'Wk', 'bk', 'Wv', 'bv')}
    del _L1_xattn_all

    def _L1_ffn_setup():
        import jax, jax.numpy as jnp
        import numpy as np
        TOP_K = 2
        key = jax.random.key(seed)
        ks = jax.random.split(key, 6)
        B, S, D, U, E = (4, 128, 128, 512, 8)
        return {'x': jax.random.normal(ks[0], (B, S, D), dtype=jnp.float32), 'w_up': jax.random.normal(ks[1], (E, U, D), dtype=jnp.float32), 'w_down': jax.random.normal(ks[2], (E, D, U), dtype=jnp.float32), 'b_up': jax.random.normal(ks[3], (E, U), dtype=jnp.float32), 'b_down': jax.random.normal(ks[4], (E, D), dtype=jnp.float32), 'w_router': jax.random.normal(ks[5], (E, D), dtype=jnp.float32)}
    _L1_ffn_all = _L1_ffn_setup()
    _L1_ffn_in = {k: v for k, v in _L1_ffn_all.items() if k in ('w_up', 'w_down', 'b_up', 'b_down', 'w_router')}
    del _L1_ffn_all
    return {'x': x, 'ctx_1024': ctx_1024, 'L0_xattn_Wq': _L0_xattn_in['Wq'], 'L0_xattn_bq': _L0_xattn_in['bq'], 'L0_xattn_Wk': _L0_xattn_in['Wk'], 'L0_xattn_bk': _L0_xattn_in['bk'], 'L0_xattn_Wv': _L0_xattn_in['Wv'], 'L0_xattn_bv': _L0_xattn_in['bv'], 'L0_xattn_Wo': _L0_xattn_in['Wo'], 'L0_xattn_bo': _L0_xattn_in['bo'], 'L0_ffn_W1': _L0_ffn_in['W1'], 'L0_ffn_b1': _L0_ffn_in['b1'], 'L0_ffn_W2': _L0_ffn_in['W2'], 'L0_ffn_b2': _L0_ffn_in['b2'], 'L1_xattn_Wq': _L1_xattn_in['Wq'], 'L1_xattn_bq': _L1_xattn_in['bq'], 'L1_xattn_Wk': _L1_xattn_in['Wk'], 'L1_xattn_bk': _L1_xattn_in['bk'], 'L1_xattn_Wv': _L1_xattn_in['Wv'], 'L1_xattn_bv': _L1_xattn_in['bv'], 'L1_ffn_w_up': _L1_ffn_in['w_up'], 'L1_ffn_w_down': _L1_ffn_in['w_down'], 'L1_ffn_b_up': _L1_ffn_in['b_up'], 'L1_ffn_b_down': _L1_ffn_in['b_down'], 'L1_ffn_w_router': _L1_ffn_in['w_router']}

def reference(x, ctx_1024, L0_xattn_Wq, L0_xattn_bq, L0_xattn_Wk, L0_xattn_bk, L0_xattn_Wv, L0_xattn_bv, L0_xattn_Wo, L0_xattn_bo, L0_ffn_W1, L0_ffn_b1, L0_ffn_W2, L0_ffn_b2, L1_xattn_Wq, L1_xattn_bq, L1_xattn_Wk, L1_xattn_bk, L1_xattn_Wv, L1_xattn_bv, L1_ffn_w_up, L1_ffn_w_down, L1_ffn_b_up, L1_ffn_b_down, L1_ffn_w_router):
    import jax
    import jax.numpy as jnp

    def _L0_xattn_ref(queries, keys, values, Wq, bq, Wk, bk, Wv, bv, Wo, bo):
        import jax, jax.numpy as jnp
        import numpy as np
        H = 16
        D_K = 128
        D_V = 128
        D_MODEL = 128
        B = 4
        S = 256

        def _split_heads(x):
            b, s, d = x.shape
            return x.reshape(b, s, H, d // H).transpose(0, 2, 1, 3)
        q = _split_heads(queries @ Wq + bq)
        k = _split_heads(keys @ Wk + bk)
        v = _split_heads(values @ Wv + bv)
        scores = jnp.einsum('bhqd,bhkd->bhqk', q, k) / jnp.sqrt(jnp.float32(D_K))
        weights = jax.nn.softmax(scores, axis=-1)
        o = jnp.einsum('bhqk,bhkd->bhqd', weights, v)
        b_, h_, s_, dh = o.shape
        o = o.transpose(0, 2, 1, 3).reshape(b_, s_, D_K)
        return o @ Wo + bo

    def _L0_ffn_ref(x, W1, b1, W2, b2):
        import jax, jax.numpy as jnp
        import numpy as np
        EMB = 128
        FF = 4 * EMB

        def _ternary(w):
            scale = jnp.maximum(jnp.mean(jnp.abs(w)), 1e-08)
            w_t = jnp.clip(jnp.round(w / scale), -1.0, 1.0)
            return w + jax.lax.stop_gradient(w_t - w)
        h = jnp.einsum('bsd,fd->bsf', x, _ternary(W1)) + b1
        h = jax.nn.gelu(h, approximate=False)
        out = jnp.einsum('bsf,df->bsd', h, _ternary(W2)) + b2
        return out

    def _L1_xattn_ref(input_1, input_2, Wq, bq, Wk, bk, Wv, bv):
        import jax, jax.numpy as jnp
        import numpy as np
        IN_CH = 128
        ATT_DIM = 128
        B, L1, L2 = (8, 256, 256)
        scale = 1.0 / np.sqrt(ATT_DIM).astype(np.float32)
        Q = jnp.einsum('bld,de->ble', input_1, Wq) + bq
        K = jnp.einsum('bld,de->ble', input_2, Wk) + bk
        V = jnp.einsum('bld,de->ble', input_2, Wv) + bv
        scores = jnp.einsum('bqd,bkd->bqk', Q, K) * scale
        scores = jnp.clip(scores, -100.0, 100.0)
        weights = jax.nn.softmax(scores, axis=-1)
        return jnp.einsum('bqk,bkd->bqd', weights, V)

    def _L1_ffn_ref(x, w_up, w_down, b_up, b_down, w_router):
        import jax, jax.numpy as jnp
        import numpy as np
        TOP_K = 2
        logits = jnp.einsum('bsd,ed->bse', x, w_router)
        top_vals, top_idx = jax.lax.top_k(logits, TOP_K)
        router_weights = jax.nn.softmax(top_vals, axis=-1)
        up = jnp.einsum('eud,bsd->bseu', w_up, x) + b_up
        h = jax.nn.gelu(up, approximate=False)
        down = jnp.einsum('edu,bseu->bsed', w_down, h) + b_down
        sel = jnp.take_along_axis(down, top_idx[..., None], axis=2)
        return jnp.einsum('bskd,bsk->bsd', sel, router_weights)
    x = x + _L0_xattn_ref(_layernorm(x, axis=-1), ctx_1024, ctx_1024, L0_xattn_Wq, L0_xattn_bq, L0_xattn_Wk, L0_xattn_bk, L0_xattn_Wv, L0_xattn_bv, L0_xattn_Wo, L0_xattn_bo)
    x = x + _L0_ffn_ref(_layernorm(x, axis=-1), L0_ffn_W1, L0_ffn_b1, L0_ffn_W2, L0_ffn_b2)
    x = x + _L1_xattn_ref(_layernorm(x, axis=-1), ctx_1024, L1_xattn_Wq, L1_xattn_bq, L1_xattn_Wk, L1_xattn_bk, L1_xattn_Wv, L1_xattn_bv)
    x = x + _L1_ffn_ref(_layernorm(x, axis=-1), L1_ffn_w_up, L1_ffn_w_down, L1_ffn_b_up, L1_ffn_b_down, L1_ffn_w_router)
    return x

_drawn_inputs = setup_inputs


def setup_inputs(seed=0):
    import zlib

    import numpy as np

    out = dict(_drawn_inputs(seed))
    spreads = {'L0_xattn_bq': (0.0, 0.399),
     'L0_xattn_bk': (0.0, 2.0),
     'L0_xattn_bv': (0.0, 0.1),
     'L0_xattn_bo': (0.0, 0.1),
     'L1_xattn_bq': (0.0, 0.8),
     'L1_xattn_bk': (0.0, 2.0),
     'L1_xattn_bv': (0.0, 2.0)}
    factors = {'L0_ffn_b1': 4.394,
     'L0_ffn_b2': 64.0,
     'L1_xattn_Wq': 8.0,
     'L1_xattn_Wk': 8.0,
     'L1_xattn_Wv': 6.229,
     'L1_ffn_b_down': 8.0}
    for name, (base, spread) in spreads.items():
        noise = np.random.default_rng([zlib.crc32(name.encode()), seed]).standard_normal(out[name].shape)
        drawn = base * np.exp(spread * noise) if base else spread * noise
        out[name] = jnp.asarray(drawn.astype(out[name].dtype))
    for name, factor in factors.items():
        out[name] = (out[name] * factor).astype(out[name].dtype)
    return out
```

```python
from contextlib import ExitStack

import numpy as np
import concourse.bass as bass
from concourse import mybir

F32 = mybir.dt.float32
BF16 = mybir.dt.bfloat16
U32 = mybir.dt.uint32
ALU = mybir.AluOpType
ACT = mybir.ActivationFunctionType
AX_X = mybir.AxisListType.X

B, S, D = 64, 128, 128
KEYS = 77
HEADS, DH = 16, 8
FF = 512
E = 8
GB = 4
G = B // GB
HH = HEADS // 2
CH = 5
UNITS = 2 * GB
FLAT = CH * 128
SLOTS = 3
FC = FF // 128
EPS = 1e-5
SCALE = 1.0 / float(np.sqrt(np.float32(128.0)))


def hold(engine, sem, value, passed):
    engine.wait_ge(sem, value)
    engine.sem_inc(passed)


def later(n, least):
    return type(n) is not int or n >= least


def first_head(c):
    return c * 128 // KEYS


PACK = {}
_at = 0
for _name, _n in (("Wq0", D), ("Wk0", D), ("Wv0", D), ("Wo0", D), ("W1T", FF), ("W2T", FF), ("Wq1", D),
                  ("Wk1", D), ("Wv1", D), ("router", E), ("bq0", 1), ("bk0", 1), ("bv0", 1), ("b1", FC), ("bq1", 1),
                  ("bk1", 1), ("ident", 128), ("kmask", HH), ("vmask", CH * SLOTS), ("rowsel", CH * 128), ("ones", 128),
                  ("bo0", D), ("b2", D), ("bv1", D), ("bup", E * FC), ("eidx", E)):
    PACK[_name] = (_at, _n)
    _at += _n
PACK_COLS = _at


def build(nc, x, ctxT, pack, sel, identb, wupT, wdnT, bdn, out, phases="ABCD"):
    with ExitStack() as stack:
        def sb(name, shape, dt=F32):
            return stack.enter_context(nc.sbuf_tensor(name, shape, dt))

        def sem(name):
            return stack.enter_context(nc.semaphore(name))

        X = sb("X", [128, B, D])
        par = sb("par", [128, PACK_COLS])

        def P(name):
            at, n = PACK[name]
            return par[:, at:at + n]

        selm = sb("selm", [HH, FLAT], BF16)
        idb = sb("idb", [128, 128], BF16)
        halves = sb("halves", [128, GB])
        epsilons = sb("epsilons", [128, GB])
        passed = sem("passed")
        params_in = sem("params_in")
        params2_in = sem("params2_in")
        halves_set = sem("halves_set")

        def xg(g, b=None):
            if b is None:
                return X[:, bass.ds(g * GB, GB), :]
            return X[:, bass.ds(g * GB + b, 1), :].rearrange("p a d -> p (a d)")

        prologue(nc, sem, pack, sel, identb, par, selm, idb, halves, epsilons, passed, params_in, params2_in, halves_set)
        attention0(nc, sem, x, ctxT, X, xg, P, selm, idb, halves, epsilons, passed, params_in)
        if "B" in phases:
            feed_forward0(nc, sem, X, xg, P, halves, epsilons, passed)
        if "C" in phases:
            gates = sb("gates", [128, B, E])
            xnT_all = sb("xnT_all", [128, B * S])
            attention1(nc, sem, ctxT, X, xg, P, halves, epsilons, passed, gates, xnT_all)
        if "D" in phases:
            experts(nc, sem, X, xg, P, wupT, wdnT, bdn, gates, xnT_all)
        with ExitStack() as st2:
            blk = st2.enter_context(nc.Block())
            stored = sem("stored")

            @blk.sync
            def _(sp):
                sp.dma_start(out.rearrange("b p d -> p b d"), X[:]).then_inc(stored, 16)
                sp.wait_ge(stored, 16)


def prologue(nc, sem, pack, sel, identb, par, selm, idb, halves, epsilons, passed, params_in, params2_in, halves_set):
    with nc.Block() as block:
        @block.sync
        def _(sp):
            sp.dma_start(par[:], pack).then_inc(params_in, 16)
            sp.dma_start(selm[:], sel).then_inc(params2_in, 16)
            sp.dma_start(idb[:], identb).then_inc(params2_in, 16)
            sp.wait_ge(params_in, 16)
            sp.wait_ge(params2_in, 32)

        @block.gpsimd
        def _(pool):
            nc.gpsimd.memset(halves[:], -0.5).then_inc(halves_set, 1)
            nc.gpsimd.memset(epsilons[:], EPS).then_inc(halves_set, 1)
            pool.wait_ge(halves_set, 2)


def attention0(nc, sem, x, ctxT, X, xg, P, selm, idb, halves, epsilons, passed, params_in):
    with ExitStack() as stack:
        def sb(name, shape, dt=F32):
            return stack.enter_context(nc.sbuf_tensor(name, shape, dt))

        def ps(name, shape, dt=F32):
            return stack.enter_context(nc.psum_tensor(name, shape, dt))

        ctx = sb("a_ctx", [128, 2, GB, KEYS])
        stats = sb("a_stats", [128, GB, 6])
        mv = sb("a_mv", [128, GB, 2])
        veps = sb("a_veps", [128, GB])
        rstd = sb("a_rstd", [128, GB])
        xn = sb("a_xn", [128, GB, D])
        xnT = sb("a_xnT", [128, GB * S])
        qT = [sb(f"a_qT{p}", [128, GB * S]) for p in range(2)]
        kT = sb("a_kT", [128, GB, KEYS])
        kbd = [sb(f"a_kbd{p}", [128, GB, FLAT]) for p in range(2)]
        vals = sb("a_vals", [KEYS, GB, D + DH])
        vx = [sb(f"a_vx{p}", [128, CH, GB * 2, 128]) for p in range(2)]
        negmax = [sb(f"a_negmax{p}", [128, HH], BF16) for p in range(2)]
        negmaxT = [sb(f"a_negmaxT{p}", [HH, 128], BF16) for p in range(2)]
        probs = [sb(f"a_probs{p}", [128, FLAT]) for p in range(2)]
        rden = sb("a_rden", [128, 2, HH])
        o = sb("a_o", [128, GB, D])
        oT = sb("a_oT", [128, GB * S])

        psS = ps("a_psS", [128, 2, 512])
        psT = [ps(f"a_psT{p}", [128, 1024]) for p in range(2)]
        psO = ps("a_psO", [128, 512])
        psM = ps("a_psM", [128, 512])
        psMax = [psT[p][0:HH, 768:832].bitcast(BF16) for p in range(2)]

        x_in = [sem(f"a_x_in{p}") for p in range(2)]
        ctx_in = [sem(f"a_ctx_in{p}") for p in range(2)]
        consts = sem("a_consts")
        ones_set = sem("a_ones_set")
        vals_done = sem("a_vals_done")
        vals_kept = sem("a_vals_kept")
        stats_done = sem("a_stats_done")
        aggr_done = sem("a_aggr_done")
        veps_done = sem("a_veps_done")
        rstd_done = sem("a_rstd_done")
        xn_done = sem("a_xn_done")
        bo_added = sem("a_bo_added")
        xT_done = sem("a_xT_done")
        xT_kept = sem("a_xT_kept")
        q_done = sem("a_q_done")
        q_kept = sem("a_q_kept")
        k_done = sem("a_k_done")
        k_kept = sem("a_k_kept")
        kbd_done = sem("a_kbd_done")
        v_done = sem("a_v_done")
        v_kept = sem("a_v_kept")
        s_done = sem("a_s_done")
        max_done = sem("a_max_done")
        maxT_done = sem("a_maxT_done")
        maxT_kept = sem("a_maxT_kept")
        t_done = sem("a_t_done")
        exp_done = sem("a_exp_done")
        pv_done = sem("a_pv_done")
        rden_done = sem("a_rden_done")
        o_done = sem("a_o_done")
        oT_done = sem("a_oT_done")
        oT_kept = sem("a_oT_kept")
        wo_done = sem("a_wo_done")
        x_done = sem("a_x_done")

        def over_groups(eng, first, step, last):
            first(0)
            with eng.Fori(0, G // 2 - 1) as h:
                step(2 * h + 1, 1)
                step(2 * h + 2, 0)
            last(G - 1)

        with nc.Block() as block:
            @block.sync
            def _(sp):
                def load(g, p, before):
                    if before is not None:
                        sp.wait_ge(x_in[p], 16 * before)
                        sp.wait_ge(ctx_in[p], 16 * before)
                        sp.wait_ge(vals_done, g - 1)
                    sp.dma_start(xg(g), x[bass.ds(g * GB, GB)].rearrange("b p d -> p b d")).then_inc(x_in[p], 16)
                    sp.dma_start(ctx[:, p], ctxT[:, bass.ds(g * GB, GB), :]).then_inc(ctx_in[p], 16)

                load(0, 0, None)
                load(1, 1, None)
                with sp.Fori(1, G // 2) as h:
                    load(2 * h, 0, h)
                    load(2 * h + 1, 1, h)
                for p in range(2):
                    sp.wait_ge(x_in[p], 16 * (G // 2))
                    sp.wait_ge(ctx_in[p], 16 * (G // 2))

            @block.gpsimd
            def _(pool):
                for p in range(2):
                    nc.gpsimd.memset(kbd[p][:], 0.0).then_inc(consts, 1)
                    nc.gpsimd.memset(vx[p][:], 0.0).then_inc(consts, 1)
                nc.gpsimd.memset(vals[:], 0.0).then_inc(consts, 1)
                pool.wait_ge(consts, 5)

                def norm(g):
                    pool.wait_ge(aggr_done, GB * g + GB)
                    nc.gpsimd.tensor_tensor(veps[:], mv[:, :, 1], epsilons[:], ALU.add).then_inc(veps_done, 1)
                    pool.wait_ge(veps_done, g + 1)
                    nc.gpsimd.tensor_tensor(rstd[:], veps[:], halves[:], ALU.pow).then_inc(rstd_done, 1)
                    pool.wait_ge(xn_done, GB * g + GB)
                    nc.gpsimd.tensor_tensor(xg(g), xg(g), P("bo0").unsqueeze(1).to_broadcast([128, GB, D]),
                                            ALU.add).then_inc(bo_added, 1)

                def spread_keys(g, p):
                    for b in range(GB):
                        pool.wait_ge(k_kept, g + 1)
                        nc.gpsimd.tensor_tensor(
                            kbd[p][:, b, 0:HH * KEYS].rearrange("p (h k) -> p h k", h=HH),
                            kT[:, b, :].unsqueeze(1).to_broadcast([128, HH, KEYS]),
                            P("kmask").unsqueeze(2).to_broadcast([128, HH, KEYS]), ALU.mult).then_inc(kbd_done, 1)

                norm(0)
                spread_keys(0, 0)

                def step(g, p):
                    norm(g + 1)
                    spread_keys(g + 1, 1 - p)
                over_groups(pool, lambda g: step(g, 0), step, lambda g: None)

            @block.vector
            def _(dve):
                for p in range(2):
                    dve.wait_ge(consts, 4)
                    for c in range(CH):
                        at = (DH + 1) * first_head(c)
                        ones = vx[p][:, c, :, at:at + SLOTS * (DH + 1)].rearrange("p n (s e) -> p n s e", e=DH + 1)
                        nc.vector.tensor_copy(ones[:, :, :, DH], P("vmask")[:, c * SLOTS:(c + 1) * SLOTS].unsqueeze(1)
                                              .to_broadcast([128, GB * 2, SLOTS])).then_inc(ones_set, 1)

                def stats_of(g, p, again):
                    hold(dve, x_in[p], 16 * (again + 1), passed)
                    for b in range(GB):
                        nc.vector.bn_stats(stats[:, b, :], xg(g, b)).then_inc(stats_done, 1)
                    hold(dve, stats_done, GB * g + GB, passed)
                    for b in range(GB):
                        nc.vector.bn_aggr(mv[:, b, :], stats[:, b, :]).then_inc(aggr_done, 1)

                def normalise(g):
                    dve.wait_ge(rstd_done, g + 1)
                    if later(g, 1):
                        dve.wait_ge(xT_done, g)
                    for b in range(GB):
                        nc.vector.tensor_scalar(xn[:, b, :], xg(g, b), mv[:, b, 0:1], rstd[:, b:b + 1],
                                                ALU.subtract, ALU.mult).then_inc(xn_done, 1)

                def keep_values(g, p, part):
                    dve.wait_ge(v_done, 3 * g + part + 1)
                    if later(g, 2) and part == 0:
                        dve.wait_ge(pv_done, UNITS * (g - 1))
                    for k, c in enumerate(range(2 * part, min(2 * part + 2, CH))):
                        at = (DH + 1) * first_head(c)
                        nc.vector.tensor_tensor(
                            vx[p][:, c, :, at:at + SLOTS * (DH + 1)].rearrange("p n (s e) -> p n s e", e=DH + 1)[:, :, :, 0:DH],
                            psM[:, k * 192:(k + 1) * 192].rearrange("p (n s e) -> p n s e", s=SLOTS, e=DH),
                            P("vmask")[:, c * SLOTS:(c + 1) * SLOTS].unsqueeze(1).unsqueeze(3)
                            .to_broadcast([128, GB * 2, SLOTS, DH]), ALU.mult).then_inc(v_kept, 1)

                def find_max(g, u):
                    n = UNITS * g + u
                    dve.wait_ge(s_done, n + 1)
                    if later(n, 2):
                        dve.wait_ge(maxT_done, n - 1)
                    nc.vector.tensor_reduce(negmax[u % 2][:], psS[:, :, 0:HH // 2 * KEYS].rearrange(
                        "p a (h k) -> p a h k", k=KEYS), AX_X, ALU.max, negate=True).then_inc(max_done, 1)

                def keep_max(g, u):
                    n = UNITS * g + u
                    dve.wait_ge(maxT_done, n + 1)
                    if later(n, 2):
                        dve.wait_ge(t_done, n - 1)
                    nc.vector.tensor_copy(negmaxT[u % 2][:], psMax[u % 2]).then_inc(maxT_kept, 1)

                def divide(g, b):
                    k = GB * g + b
                    dve.wait_ge(pv_done, 2 * k + 2)
                    acc = psO[:, 0:256].rearrange("p (a c) -> p a c", a=2)[:, :, 0:HH * (DH + 1)].rearrange(
                        "p a (h e) -> p a h e", e=DH + 1)
                    nc.vector.reciprocal(rden[:], acc[:, :, :, DH]).then_inc(rden_done, 1)
                    dve.wait_ge(rden_done, k + 1)
                    if later(g, 1):
                        dve.wait_ge(oT_done, g)
                    nc.vector.tensor_tensor(o[:, b, :].rearrange("p (a h e) -> p a h e", a=2, e=DH),
                                            acc[:, :, :, 0:DH],
                                            rden[:].unsqueeze(3).to_broadcast([128, 2, HH, DH]),
                                            ALU.mult).then_inc(o_done, 1)

                def residual(g):
                    dve.wait_ge(wo_done, g + 1)
                    dve.wait_ge(bo_added, g + 1)
                    nc.vector.tensor_tensor(xg(g), xg(g), psM[:].rearrange("p (b d) -> p b d", d=D),
                                            ALU.add).then_inc(x_done, 1)

                stats_of(0, 0, 0)
                normalise(0)
                for part in range(3):
                    keep_values(0, 0, part)

                def step(g, p, again_next, prev=True, nxt=True):
                    for u in range(UNITS):
                        find_max(g, u)
                        if u % 2 == 0 and (prev or u):
                            divide(g if u else g - 1, (u // 2 - 1) % GB)
                        keep_max(g, u)
                        if u == 0 and nxt:
                            stats_of(g + 1, 1 - p, again_next)
                        if u == 1 and nxt:
                            normalise(g + 1)
                        if u == 3 and prev:
                            residual(g - 1)
                        if u == 6 and nxt:
                            keep_values(g + 1, 1 - p, 0)
                            keep_values(g + 1, 1 - p, 1)
                        if u == 7 and nxt:
                            keep_values(g + 1, 1 - p, 2)

                step(0, 0, 0, prev=False)
                with dve.Fori(0, G // 2 - 1) as h:
                    step(2 * h + 1, 1, h + 1)
                    step(2 * h + 2, 0, h + 1)
                step(G - 1, 1, 0, nxt=False)
                divide(G - 1, GB - 1)
                residual(G - 1)

            @block.scalar
            def _(act):
                def keep_xT(g):
                    act.wait_ge(xT_done, g + 1)
                    if later(g, 1):
                        act.wait_ge(q_done, g)
                    nc.scalar.copy(xnT[:], psM[:]).then_inc(xT_kept, 1)

                def keep_q(g, p):
                    act.wait_ge(q_done, g + 1)
                    nc.scalar.activation(qT[p][:], psM[:], ACT.Identity, bias=P("bq0")).then_inc(q_kept, 1)

                def keep_k(g):
                    act.wait_ge(k_done, g + 1)
                    if later(g, 1):
                        act.wait_ge(kbd_done, GB * g)
                    nc.scalar.activation(kT[:], psM[:, 0:GB * KEYS].rearrange("p (b k) -> p b k", k=KEYS),
                                         ACT.Identity, bias=P("bk0")).then_inc(k_kept, 1)

                def keep_vals(g):
                    act.wait_ge(vals_done, g + 1)
                    if later(g, 1):
                        act.wait_ge(v_done, 3 * g)
                    nc.scalar.copy(vals[:, :, 0:D], psM[0:KEYS, :].rearrange("p (b d) -> p b d", d=D)).then_inc(vals_kept, 1)

                def exponentials(g, u):
                    n = UNITS * g + u
                    act.wait_ge(t_done, n + 1)
                    if later(n, 2):
                        act.wait_ge(pv_done, n - 1)
                    nc.scalar.activation(probs[u % 2][:], psT[u % 2][:, 0:FLAT], ACT.Exp,
                                         scale=SCALE).then_inc(exp_done, 1)

                def keep_oT(g):
                    act.wait_ge(oT_done, g + 1)
                    if later(g, 1):
                        act.wait_ge(wo_done, g)
                    nc.scalar.activation(oT[:], psM[:], ACT.Identity, bias=P("bv0")).then_inc(oT_kept, 1)

                keep_xT(0)
                keep_q(0, 0)
                keep_k(0)
                keep_vals(0)

                def step(g, p, prev=True, nxt=True):
                    for u in range(UNITS):
                        exponentials(g, u)
                        if u == 1 and prev:
                            keep_oT(g - 1)
                        if u == 2 and nxt:
                            keep_xT(g + 1)
                        if u == 4 and nxt:
                            keep_q(g + 1, 1 - p)
                        if u == 5 and nxt:
                            keep_k(g + 1)
                            keep_vals(g + 1)
                over_groups(act, lambda g: step(g, 0, prev=False), step, lambda g: step(g, 1, nxt=False))
                keep_oT(G - 1)

            @block.tensor
            def _(pe):
                mm = nc.tensor.matmul

                def transpose_x(g):
                    pe.wait_ge(xn_done, GB * g + GB)
                    for b in range(GB):
                        last = nc.tensor.transpose(psM[:, b * S:(b + 1) * S], xn[:, b, :], P("ident"))
                    last.then_inc(xT_done, 1)

                def queries(g):
                    pe.wait_ge(xT_kept, g + 1)
                    mm(psM[:], P("Wq0"), xnT[:], start=True, stop=True).then_inc(q_done, 1)

                def keys(g, p, again):
                    pe.wait_ge(q_kept, g + 1)
                    pe.wait_ge(ctx_in[p], 16 * (again + 1))
                    mm(psM[:, 0:GB * KEYS], P("Wk0"), ctx[:, p], start=True, stop=True).then_inc(k_done, 1)

                def project_values(g, p):
                    pe.wait_ge(k_kept, g + 1)
                    for b in range(GB):
                        last = mm(psM[0:KEYS, b * D:(b + 1) * D], ctx[:, p, b, :], P("Wv0"), start=True, stop=True)
                    last.then_inc(vals_done, 1)

                def values(g, part):
                    pe.wait_ge(vals_kept, g + 1)
                    if part:
                        pe.wait_ge(v_kept, CH * g + 2 * part)
                    for k, c in enumerate(range(2 * part, min(2 * part + 2, CH))):
                        for half in range(2):
                            at = D // 2 * half + DH * first_head(c)
                            last = mm(psM[:, k * 192:(k + 1) * 192].rearrange("p (b a e) -> p b a e", b=GB, a=2)[:, :, half, :],
                                      P("rowsel")[0:KEYS, c * 128:(c + 1) * 128], vals[:, :, at:at + SLOTS * DH],
                                      start=True, stop=True)
                    last.then_inc(v_done, 1)

                def scores(g, p, u):
                    n = UNITS * g + u
                    b, lo = u // 2, 64 * (u % 2)
                    if u == 0:
                        pe.wait_ge(q_kept, g + 1)
                    if u % 2 == 0:
                        pe.wait_ge(kbd_done, GB * g + b + 1)
                    if later(n, 1):
                        pe.wait_ge(max_done, n)
                    for a in range(2):
                        last = mm(psS[:, a, 0:HH // 2 * KEYS], qT[p][lo:lo + 64, b * S:(b + 1) * S],
                                  kbd[p][lo:lo + 64, b, a * HH // 2 * KEYS:(a + 1) * HH // 2 * KEYS],
                                  start=True, stop=True)
                    last.then_inc(s_done, 1)

                def scores_t(g, p, u):
                    n = UNITS * g + u
                    b, lo = u // 2, 64 * (u % 2)
                    if later(n, 2):
                        pe.wait_ge(exp_done, n - 1)
                    for c in range(CH - 1):
                        mm(psT[u % 2][:, c * 128:(c + 1) * 128], kbd[p][lo:lo + 64, b, c * 128:(c + 1) * 128],
                           qT[p][lo:lo + 64, b * S:(b + 1) * S], start=c == 0, stop=False, skip_group_check=True)

                def transpose_max(g, u):
                    n = UNITS * g + u
                    pe.wait_ge(max_done, n + 1)
                    nc.tensor.transpose(psMax[u % 2], negmax[u % 2][:], idb[:]).then_inc(maxT_done, 1)

                def subtract_max(g, p, u):
                    n = UNITS * g + u
                    b, lo, c = u // 2, 64 * (u % 2), CH - 1
                    pe.wait_ge(maxT_kept, n + 1)
                    mm(psT[u % 2][:, c * 128:(c + 1) * 128], kbd[p][lo:lo + 64, b, c * 128:(c + 1) * 128],
                       qT[p][lo:lo + 64, b * S:(b + 1) * S], start=True, stop=False, skip_group_check=True)
                    for c in range(CH):
                        last = mm(psT[u % 2][:, c * 128:(c + 1) * 128], selm[:, c * 128:(c + 1) * 128],
                                  negmaxT[u % 2][:], start=False, stop=True, skip_group_check=True)
                    last.then_inc(t_done, 1)

                def weigh(g, p, u):
                    n = UNITS * g + u
                    b, half = u // 2, u % 2
                    pe.wait_ge(exp_done, n + 1)
                    if half == 0:
                        if b == 0:
                            pe.wait_ge(v_kept, CH * g + CH)
                        if later(n, 1):
                            pe.wait_ge(o_done, GB * g + b)
                    for c in range(CH):
                        last = mm(psO[:, half * 128:(half + 1) * 128], probs[u % 2][:, c * 128:(c + 1) * 128],
                                  vx[p][:, c, 2 * b + half, :], start=c == 0, stop=c == CH - 1)
                    last.then_inc(pv_done, 1)

                def transpose_o(g):
                    pe.wait_ge(o_done, GB * g + GB)
                    for b in range(GB):
                        last = nc.tensor.transpose(psM[:, b * S:(b + 1) * S], o[:, b, :], P("ident"))
                    last.then_inc(oT_done, 1)

                def project(g):
                    pe.wait_ge(oT_kept, g + 1)
                    for b in range(GB):
                        last = mm(psM[:, b * D:(b + 1) * D], oT[:, b * S:(b + 1) * S], P("Wo0"), start=True, stop=True)
                    last.then_inc(wo_done, 1)

                pe.wait_ge(consts, 5)
                pe.wait_ge(ones_set, 2 * CH)
                transpose_x(0)
                queries(0)
                keys(0, 0, 0)
                project_values(0, 0)
                for part in range(3):
                    values(0, part)
                scores(0, 0, 0)

                def step(g, p, again_next, prev=True, nxt=True):
                    for u in range(UNITS):
                        scores_t(g, p, u)
                        if u:
                            weigh(g, p, u - 1)
                        elif prev:
                            weigh(g - 1, 1 - p, UNITS - 1)
                        transpose_max(g, u)
                        if u < UNITS - 1:
                            scores(g, p, u + 1)
                        elif nxt:
                            scores(g + 1, 1 - p, 0)
                        subtract_max(g, p, u)
                        if u == 1 and prev:
                            pe.wait_ge(v_kept, CH * g + CH)
                            transpose_o(g - 1)
                        if u == 2 and nxt:
                            if prev:
                                pe.wait_ge(oT_kept, g)
                            else:
                                pe.wait_ge(v_kept, CH)
                            transpose_x(g + 1)
                        if u == 3 and prev:
                            if nxt:
                                pe.wait_ge(xT_kept, g + 2)
                            project(g - 1)
                        if u == 4 and nxt:
                            if prev:
                                pe.wait_ge(x_done, g)
                            queries(g + 1)
                        if u == 5 and nxt:
                            keys(g + 1, 1 - p, again_next)
                            project_values(g + 1, 1 - p)
                        if u == 6 and nxt:
                            values(g + 1, 0)
                            values(g + 1, 1)
                        if u == 7 and nxt:
                            values(g + 1, 2)

                step(0, 0, 0, prev=False)
                with pe.Fori(0, G // 2 - 1) as h:
                    step(2 * h + 1, 1, h + 1)
                    step(2 * h + 2, 0, h + 1)
                step(G - 1, 1, 0, nxt=False)
                weigh(G - 1, 1, UNITS - 1)
                transpose_o(G - 1)
                project(G - 1)


def ternary(nc, sem, sb, P):
    absum = sb("t_absum", [128, 2])
    half = sb("t_half", [128, 2])
    neg = sb("t_neg", [128, 2])
    up = sb("t_up", [128, FF])
    down = sb("t_down", [128, FF])
    step_done = sem("t_step_done")
    summed = sem("t_summed")
    with ExitStack() as stack:
        total = stack.enter_context(nc.psum_tensor("t_total", [128, 2], F32))
        with nc.Block() as block:
            @block.tensor
            def _(pe):
                pe.wait_ge(step_done, 2)
                nc.tensor.matmul(total[:], P("ones"), absum[:], start=True, stop=True).then_inc(summed, 1)

            @block.vector
            def _(dve):
                for j, name in enumerate(("W1T", "W2T")):
                    nc.vector.tensor_reduce(absum[:, j:j + 1], P(name), AX_X, ALU.add,
                                            apply_absolute_value=True).then_inc(step_done, 1)
                dve.wait_ge(summed, 1)
                nc.vector.tensor_scalar(half[:], total[:], 1.0 / (D * FF), 1e-8, ALU.mult, ALU.max).then_inc(step_done, 1)
                dve.wait_ge(step_done, 3)
                nc.vector.tensor_scalar(neg[:], half[:], -0.5, None, ALU.mult).then_inc(step_done, 1)
                dve.wait_ge(step_done, 4)
                nc.vector.tensor_scalar(half[:], half[:], 0.5, None, ALU.mult).then_inc(step_done, 1)
                n = 5
                for j, name in enumerate(("W1T", "W2T")):
                    w = P(name)
                    dve.wait_ge(step_done, n)
                    nc.vector.tensor_scalar(up[:], w, half[:, j:j + 1], None, ALU.is_gt).then_inc(step_done, 1)
                    nc.vector.tensor_scalar(down[:], w, neg[:, j:j + 1], None, ALU.is_lt).then_inc(step_done, 1)
                    dve.wait_ge(step_done, n + 2)
                    nc.vector.tensor_tensor(up[:], up[:], down[:], ALU.subtract).then_inc(step_done, 1)
                    dve.wait_ge(step_done, n + 3)
                    nc.vector.tensor_tensor(up[:], up[:], w, ALU.subtract).then_inc(step_done, 1)
                    dve.wait_ge(step_done, n + 4)
                    nc.vector.tensor_tensor(w, w, up[:], ALU.add).then_inc(step_done, 1)
                    n += 5
                dve.wait_ge(step_done, n)


def feed_forward0(nc, sem, X, xg, P, halves, epsilons, passed):
    with ExitStack() as stack:
        def sb(name, shape, dt=F32):
            return stack.enter_context(nc.sbuf_tensor(name, shape, dt))

        def ps(name, shape, dt=F32):
            return stack.enter_context(nc.psum_tensor(name, shape, dt))

        ternary(nc, sem, sb, P)
        stats = sb("b_stats", [128, GB, 6])
        mv = sb("b_mv", [128, GB, 2])
        veps = sb("b_veps", [128, GB])
        rstd = sb("b_rstd", [128, GB])
        xn = sb("b_xn", [128, GB, D])
        xnT = [sb(f"b_xnT{p}", [128, GB * S]) for p in range(2)]
        hT = [sb(f"b_hT{p}", [128, FC, GB * S]) for p in range(2)]
        psX = ps("b_psX", [128, 512])
        psU = [ps(f"b_psU{c}", [128, 512]) for c in range(FC)]
        psY = [ps(f"b_psY{p}", [128, 512]) for p in range(2)]

        stats_done = sem("b_stats_done")
        aggr_done = sem("b_aggr_done")
        veps_done = sem("b_veps_done")
        rstd_done = sem("b_rstd_done")
        xn_done = sem("b_xn_done")
        b2_added = sem("b_b2_added")
        xT_done = sem("b_xT_done")
        xT_kept = sem("b_xT_kept")
        up_done = sem("b_up_done")
        gelu_done = sem("b_gelu_done")
        down_done = sem("b_down_done")
        x_done = sem("b_x_done")

        def over_groups(eng, step):
            step(0, 0)
            with eng.Fori(0, (G - 4) // 2) as h:
                step(2 * h + 1, 1)
                step(2 * h + 2, 0)
            for g in range(G - 3, G):
                step(g, g % 2)

        def has(g, ahead):
            return type(g) is not int or g + ahead < G

        with nc.Block() as block:
            @block.gpsimd
            def _(pool):
                def norm(g):
                    pool.wait_ge(aggr_done, GB * g + GB)
                    nc.gpsimd.tensor_tensor(veps[:], mv[:, :, 1], epsilons[:], ALU.add).then_inc(veps_done, 1)
                    pool.wait_ge(veps_done, g + 1)
                    nc.gpsimd.tensor_tensor(rstd[:], veps[:], halves[:], ALU.pow).then_inc(rstd_done, 1)
                    pool.wait_ge(xn_done, GB * g + GB)
                    nc.gpsimd.tensor_tensor(xg(g), xg(g), P("b2").unsqueeze(1).to_broadcast([128, GB, D]),
                                            ALU.add).then_inc(b2_added, 1)

                for g in range(3):
                    norm(g)
                over_groups(pool, lambda g, p: norm(g + 3) if has(g, 3) else None)

            @block.vector
            def _(dve):
                def stats_of(g):
                    for b in range(GB):
                        nc.vector.bn_stats(stats[:, b, :], xg(g, b)).then_inc(stats_done, 1)
                    hold(dve, stats_done, GB * g + GB, passed)
                    for b in range(GB):
                        nc.vector.bn_aggr(mv[:, b, :], stats[:, b, :]).then_inc(aggr_done, 1)

                def normalise(g):
                    dve.wait_ge(rstd_done, g + 1)
                    if later(g, 1):
                        dve.wait_ge(xT_done, g)
                    for b in range(GB):
                        nc.vector.tensor_scalar(xn[:, b, :], xg(g, b), mv[:, b, 0:1], rstd[:, b:b + 1],
                                                ALU.subtract, ALU.mult).then_inc(xn_done, 1)

                for g in range(2):
                    stats_of(g)
                    normalise(g)
                stats_of(2)

                def step(g, p):
                    if has(g, 2):
                        normalise(g + 2)
                    if has(g, 3):
                        stats_of(g + 3)
                    dve.wait_ge(down_done, g + 1)
                    dve.wait_ge(b2_added, g + 1)
                    nc.vector.tensor_tensor(xg(g), xg(g), psY[p][:].rearrange("p (b d) -> p b d", d=D),
                                            ALU.add).then_inc(x_done, 1)
                over_groups(dve, step)
                dve.wait_ge(x_done, G)

            @block.scalar
            def _(act):
                def keep_xT(g, p):
                    act.wait_ge(xT_done, g + 1)
                    if later(g, 2):
                        act.wait_ge(up_done, FC * (g - 1))
                    nc.scalar.copy(xnT[p][:], psX[:]).then_inc(xT_kept, 1)

                def gelu(g, p, c):
                    act.wait_ge(up_done, FC * g + c + 1)
                    if later(g, 2) and c == 0:
                        act.wait_ge(down_done, g - 1)
                    nc.scalar.activation(hT[p][:, c, :], psU[c][:], ACT.Gelu, bias=P("b1")[:, c:c + 1]).then_inc(gelu_done, 1)

                keep_xT(0, 0)
                for c in range(FC):
                    gelu(0, 0, c)
                keep_xT(1, 1)

                def step(g, p):
                    if has(g, 1):
                        for c in range(FC):
                            gelu(g + 1, 1 - p, c)
                    if has(g, 2):
                        keep_xT(g + 2, p)
                over_groups(act, step)

            @block.tensor
            def _(pe):
                mm = nc.tensor.matmul

                def transpose_x(g):
                    pe.wait_ge(xn_done, GB * g + GB)
                    if later(g, 1):
                        pe.wait_ge(xT_kept, g)
                    for b in range(GB):
                        last = nc.tensor.transpose(psX[:, b * S:(b + 1) * S], xn[:, b, :], P("ident"))
                    last.then_inc(xT_done, 1)

                def up(g, p, c):
                    if c == 0:
                        pe.wait_ge(xT_kept, g + 1)
                    if later(g, 1):
                        pe.wait_ge(gelu_done, FC * (g - 1) + c + 1)
                    mm(psU[c][:], P("W1T")[:, c * 128:(c + 1) * 128], xnT[p][:], start=True, stop=True).then_inc(up_done, 1)

                def down(g, p, b):
                    if b == 0:
                        pe.wait_ge(gelu_done, FC * g + FC)
                        if later(g, 2):
                            pe.wait_ge(x_done, g - 1)
                    for c in range(FC):
                        last = mm(psY[p][:, b * D:(b + 1) * D], hT[p][:, c, b * S:(b + 1) * S],
                                  P("W2T")[:, c * D:(c + 1) * D], start=c == 0, stop=c == FC - 1)
                    if b == GB - 1:
                        last.then_inc(down_done, 1)

                transpose_x(0)
                for c in range(FC):
                    up(0, 0, c)
                transpose_x(1)

                def step(g, p):
                    for k in range(FC):
                        if has(g, 1):
                            up(g + 1, 1 - p, k)
                        down(g, p, k)
                    if has(g, 2):
                        transpose_x(g + 2)
                over_groups(pe, step)


def attention1(nc, sem, ctxT, X, xg, P, halves, epsilons, passed, gates, xnT_all):
    with ExitStack() as stack:
        def sb(name, shape, dt=F32):
            return stack.enter_context(nc.sbuf_tensor(name, shape, dt))

        def ps(name, shape, dt=F32):
            return stack.enter_context(nc.psum_tensor(name, shape, dt))

        ctx = sb("c_ctx", [128, 2, GB, KEYS])
        bq = sb("c_bq", [128, 1])
        stats = sb("c_stats", [128, GB, 6])
        mv = sb("c_mv", [128, GB, 2])
        veps = sb("c_veps", [128, GB])
        rstd = sb("c_rstd", [128, GB])
        xn = sb("c_xn", [128, GB, D])
        xnT = sb("c_xnT", [128, GB * S])
        qT = sb("c_qT", [128, GB * S])
        kT = sb("c_kT", [128, GB, KEYS])
        v = [sb(f"c_v{p}", [KEYS, GB * D]) for p in range(2)]
        clipped = sb("c_clipped", [128, GB, KEYS])
        negmax = sb("c_negmax", [128, GB])
        probs = sb("c_probs", [128, GB, KEYS])
        den = sb("c_den", [128, GB])
        rden = sb("c_rden", [128, GB])
        probsT = sb("c_probsT", [KEYS, GB * S])
        stats2 = sb("c_stats2", [128, GB, 6])
        mv2 = sb("c_mv2", [128, GB, 2])
        veps2 = sb("c_veps2", [128, GB])
        rstd2 = sb("c_rstd2", [128, GB])
        xn2 = sb("c_xn2", [128, GB, D])
        xn2T = sb("c_xn2T", [128, GB * S])
        logits = sb("c_logits", [128, GB, E])
        top = sb("c_top", [128, GB, 8])
        topi = sb("c_topi", [128, GB, 8], U32)
        topf = sb("c_topf", [128, GB, 8])
        gap = sb("c_gap", [128, GB])
        egap = sb("c_egap", [128, GB])
        egap1 = sb("c_egap1", [128, GB])
        w1 = sb("c_w1", [128, GB])
        w2 = sb("c_w2", [128, GB])
        hot1 = sb("c_hot1", [128, GB, E])
        hot2 = sb("c_hot2", [128, GB, E])

        psX = ps("c_psX", [128, 512])
        psQ = ps("c_psQ", [128, 512])
        psK = ps("c_psK", [128, 512])
        psV = ps("c_psV", [KEYS, 512])
        psS = ps("c_psS", [128, 512])
        psP = ps("c_psP", [KEYS, 512])
        psY = ps("c_psY", [128, 512])
        psL = ps("c_psL", [128, 512])

        names = ("bq_done stats_done aggr_done veps_done rstd_done xn_done xT_done xT_kept q_done q_kept k_done k_kept "
                 "v_done v_kept s_done clip_done max_done exp_done rden_done pT_done pT_kept y_done x_done stats2_done "
                 "aggr2_done veps2_done rstd2_done xn2_done x2T_done x2T_kept l_done l_kept top_done topi_done topf_done "
                 "gap_done egap_done egap1_done w1_done w2_done hot_done hotw_done gates_done").split()
        (bq_done, stats_done, aggr_done, veps_done, rstd_done, xn_done, xT_done, xT_kept, q_done, q_kept, k_done,
         k_kept, v_done, v_kept, s_done, clip_done, max_done, exp_done, rden_done, pT_done, pT_kept, y_done, x_done,
         stats2_done, aggr2_done, veps2_done, rstd2_done, xn2_done, x2T_done, x2T_kept, l_done, l_kept, top_done,
         topi_done, topf_done, gap_done, egap_done, egap1_done, w1_done, w2_done, hot_done, hotw_done,
         gates_done) = [sem("c_" + name) for name in names]
        ctx_in = [sem(f"c_ctx_in{p}") for p in range(2)]

        def over_groups(eng, step):
            step(0, 0, True, False)
            with eng.Fori(0, G // 2 - 1) as h:
                step(2 * h + 1, 1, True, True)
                step(2 * h + 2, 0, True, True)
            step(G - 1, 1, True, True)
            step(G, 0, False, True)

        with nc.Block() as block:
            @block.sync
            def _(sp):
                def load(g, p, before):
                    if before is not None:
                        sp.wait_ge(ctx_in[p], 16 * before)
                        sp.wait_ge(v_done, g - 1)
                    sp.dma_start(ctx[:, p], ctxT[:, bass.ds(g * GB, GB), :]).then_inc(ctx_in[p], 16)

                load(0, 0, None)
                load(1, 1, None)
                with sp.Fori(1, G // 2) as h:
                    load(2 * h, 0, h)
                    load(2 * h + 1, 1, h)
                for p in range(2):
                    sp.wait_ge(ctx_in[p], 16 * (G // 2))

            @block.gpsimd
            def _(pool):
                def step(g, p, here, before):
                    if here:
                        pool.wait_ge(aggr_done, GB * g + GB)
                        nc.gpsimd.tensor_tensor(veps[:], mv[:, :, 1], epsilons[:], ALU.add).then_inc(veps_done, 1)
                        pool.wait_ge(veps_done, g + 1)
                        nc.gpsimd.tensor_tensor(rstd[:], veps[:], halves[:], ALU.pow).then_inc(rstd_done, 1)
                    if before:
                        pool.wait_ge(aggr2_done, GB * g)
                        nc.gpsimd.tensor_tensor(veps2[:], mv2[:, :, 1], epsilons[:], ALU.add).then_inc(veps2_done, 1)
                        pool.wait_ge(veps2_done, g)
                        nc.gpsimd.tensor_tensor(rstd2[:], veps2[:], halves[:], ALU.pow).then_inc(rstd2_done, 1)
                over_groups(pool, step)

            @block.vector
            def _(dve):
                nc.vector.tensor_scalar(bq[:], P("bq1"), SCALE, None, ALU.mult).then_inc(bq_done, 1)

                def stats_of(g):
                    for b in range(GB):
                        nc.vector.bn_stats(stats[:, b, :], xg(g, b)).then_inc(stats_done, 1)
                    hold(dve, stats_done, GB * g + GB, passed)
                    for b in range(GB):
                        nc.vector.bn_aggr(mv[:, b, :], stats[:, b, :]).then_inc(aggr_done, 1)

                def normalise(g):
                    dve.wait_ge(rstd_done, g + 1)
                    if later(g, 1):
                        dve.wait_ge(xT_done, g)
                    for b in range(GB):
                        nc.vector.tensor_scalar(xn[:, b, :], xg(g, b), mv[:, b, 0:1], rstd[:, b:b + 1],
                                                ALU.subtract, ALU.mult).then_inc(xn_done, 1)

                def finish_attention(g, p):
                    dve.wait_ge(exp_done, GB * g + GB)
                    nc.vector.reciprocal(rden[:], den[:]).then_inc(rden_done, 1)
                    dve.wait_ge(rden_done, g + 1)
                    dve.wait_ge(y_done, g + 1)
                    for b in range(GB):
                        nc.vector.scalar_tensor_tensor(xg(g, b), psY[:, b * D:(b + 1) * D], rden[:, b:b + 1], xg(g, b),
                                                       ALU.mult, ALU.add).then_inc(x_done, 1)

                def second_stats(g):
                    hold(dve, x_done, GB * g + GB, passed)
                    for b in range(GB):
                        nc.vector.bn_stats(stats2[:, b, :], xg(g, b)).then_inc(stats2_done, 1)
                    hold(dve, stats2_done, GB * g + GB, passed)
                    for b in range(GB):
                        nc.vector.bn_aggr(mv2[:, b, :], stats2[:, b, :]).then_inc(aggr2_done, 1)

                def second_normalise(g):
                    dve.wait_ge(rstd2_done, g + 1)
                    for b in range(GB):
                        nc.vector.tensor_scalar(xn2[:, b, :], xg(g, b), mv2[:, b, 0:1], rstd2[:, b:b + 1],
                                                ALU.subtract, ALU.mult).then_inc(xn2_done, 1)

                def route(g):
                    dve.wait_ge(l_done, g + 1)
                    nc.vector.tensor_copy(logits[:], psL[:, 0:GB * E].rearrange("p (b e) -> p b e", e=E)).then_inc(l_kept, 1)
                    hold(dve, l_kept, g + 1, passed)
                    for b in range(GB):
                        nc.vector.max(top[:, b, :], logits[:, b, :]).then_inc(top_done, 1)
                    hold(dve, top_done, GB * g + GB, passed)
                    for b in range(GB):
                        nc.vector.max_index(topi[:, b, :], top[:, b, :], logits[:, b, :]).then_inc(topi_done, 1)
                    nc.vector.tensor_tensor(gap[:], top[:, :, 1], top[:, :, 0], ALU.subtract).then_inc(gap_done, 1)
                    dve.wait_ge(topi_done, GB * g + GB)
                    nc.vector.tensor_copy(topf[:], topi[:]).then_inc(topf_done, 1)
                    dve.wait_ge(topf_done, g + 1)
                    for hot, k in ((hot1, 0), (hot2, 1)):
                        nc.vector.tensor_tensor(hot[:], P("eidx").unsqueeze(1).to_broadcast([128, GB, E]),
                                                topf[:, :, k:k + 1].to_broadcast([128, GB, E]),
                                                ALU.is_equal).then_inc(hot_done, 1)
                    dve.wait_ge(egap_done, g + 1)
                    nc.vector.tensor_scalar(egap1[:], egap[:], 1.0, None, ALU.add).then_inc(egap1_done, 1)
                    dve.wait_ge(egap1_done, g + 1)
                    nc.vector.reciprocal(w1[:], egap1[:]).then_inc(w1_done, 1)
                    dve.wait_ge(w1_done, g + 1)
                    nc.vector.tensor_tensor(w2[:], w1[:], egap[:], ALU.mult).then_inc(w2_done, 1)
                    dve.wait_ge(w2_done, g + 1)
                    dve.wait_ge(hot_done, 2 * g + 2)
                    for hot, w in ((hot1, w1), (hot2, w2)):
                        nc.vector.tensor_tensor(hot[:], hot[:], w[:].unsqueeze(2).to_broadcast([128, GB, E]),
                                                ALU.mult).then_inc(hotw_done, 1)
                    dve.wait_ge(hotw_done, 2 * g + 2)
                    nc.vector.tensor_tensor(gates[:, bass.ds(g * GB, GB), :], hot1[:], hot2[:], ALU.add).then_inc(gates_done, 1)

                def step(g, p, here, before):
                    if here:
                        stats_of(g)
                    if before:
                        finish_attention(g - 1, 1 - p)
                    if here:
                        normalise(g)
                    if before:
                        second_stats(g - 1)
                    if here:
                        dve.wait_ge(k_done, g + 1)
                        nc.vector.tensor_scalar(kT[:], psK[:, 0:GB * KEYS].rearrange("p (b k) -> p b k", k=KEYS), P("bk1"),
                                                None, ALU.add).then_inc(k_kept, 1)
                        dve.wait_ge(v_done, g + 1)
                        nc.vector.tensor_tensor(v[p][:].rearrange("k (b d) -> k b d", d=D),
                                                psV[:].rearrange("k (b d) -> k b d", d=D),
                                                P("bv1")[0:KEYS, :].unsqueeze(1).to_broadcast([KEYS, GB, D]),
                                                ALU.add).then_inc(v_kept, 1)
                    if before:
                        second_normalise(g - 1)
                    if here:
                        dve.wait_ge(s_done, g + 1)
                        nc.vector.tensor_scalar(clipped[:], psS[:, 0:GB * KEYS].rearrange("p (b k) -> p b k", k=KEYS),
                                                100.0, -100.0, ALU.min, ALU.max).then_inc(clip_done, 1)
                        dve.wait_ge(clip_done, g + 1)
                        nc.vector.tensor_reduce(negmax[:], clipped[:], AX_X, ALU.max, negate=True).then_inc(max_done, 1)
                    if before:
                        route(g - 1)
                over_groups(dve, step)
                dve.wait_ge(gates_done, G)

            @block.scalar
            def _(act):
                act.wait_ge(bq_done, 1)

                def step(g, p, here, before):
                    if here:
                        act.wait_ge(xT_done, g + 1)
                        nc.scalar.copy(xnT[:], psX[:]).then_inc(xT_kept, 1)
                        act.wait_ge(q_done, g + 1)
                        nc.scalar.activation(qT[:], psQ[:], ACT.Identity, bias=bq[:], scale=SCALE).then_inc(q_kept, 1)
                    if before:
                        act.wait_ge(x2T_done, g)
                        nc.scalar.copy(xnT_all[:, bass.ds((g - 1) * GB * S, GB * S)], psX[:]).then_inc(x2T_kept, 1)
                        nc.scalar.copy(xn2T[:], psX[:]).then_inc(x2T_kept, 1)
                    if here:
                        act.wait_ge(max_done, g + 1)
                        for b in range(GB):
                            nc.scalar.activation(probs[:, b, :], clipped[:, b, :], ACT.Exp, bias=negmax[:, b:b + 1],
                                                 accum_out=den[:, b:b + 1]).then_inc(exp_done, 1)
                    if before:
                        act.wait_ge(gap_done, g)
                        nc.scalar.activation(egap[:], gap[:], ACT.Exp).then_inc(egap_done, 1)
                    if here:
                        act.wait_ge(pT_done, g + 1)
                        nc.scalar.copy(probsT[:], psP[:]).then_inc(pT_kept, 1)
                over_groups(act, step)
                act.wait_ge(x2T_kept, 2 * G)

            @block.tensor
            def _(pe):
                mm = nc.tensor.matmul

                def step(g, p, here, before):
                    if before:
                        pe.wait_ge(pT_kept, g)
                        pe.wait_ge(v_kept, g)
                        for b in range(GB):
                            last = mm(psY[:, b * D:(b + 1) * D], probsT[:, b * S:(b + 1) * S],
                                      v[1 - p][:, b * D:(b + 1) * D], start=True, stop=True)
                        last.then_inc(y_done, 1)
                    if here:
                        pe.wait_ge(xn_done, GB * g + GB)
                        if before:
                            if later(g, 2):
                                pe.wait_ge(x2T_kept, 2 * (g - 1))
                        for b in range(GB):
                            last = nc.tensor.transpose(psX[:, b * S:(b + 1) * S], xn[:, b, :], P("ident"))
                        last.then_inc(xT_done, 1)
                        pe.wait_ge(ctx_in[p], 16 * (half_of(g, p) + 1))
                        if before:
                            pe.wait_ge(k_kept, g)
                            pe.wait_ge(v_kept, g)
                        mm(psK[:, 0:GB * KEYS], P("Wk1"), ctx[:, p], start=True, stop=True).then_inc(k_done, 1)
                        for b in range(GB):
                            last = mm(psV[:, b * D:(b + 1) * D], ctx[:, p, b, :], P("Wv1"), start=True, stop=True)
                        last.then_inc(v_done, 1)
                        pe.wait_ge(xT_kept, g + 1)
                        mm(psQ[:], P("Wq1"), xnT[:], start=True, stop=True).then_inc(q_done, 1)
                    if before:
                        pe.wait_ge(xn2_done, GB * g)
                        if here:
                            pe.wait_ge(xT_kept, g + 1)
                        for b in range(GB):
                            last = nc.tensor.transpose(psX[:, b * S:(b + 1) * S], xn2[:, b, :], P("ident"))
                        last.then_inc(x2T_done, 1)
                    if here:
                        pe.wait_ge(q_kept, g + 1)
                        pe.wait_ge(k_kept, g + 1)
                        if before:
                            pe.wait_ge(clip_done, g)
                        for b in range(GB):
                            last = mm(psS[:, b * KEYS:(b + 1) * KEYS], qT[:, b * S:(b + 1) * S], kT[:, b, :],
                                      start=True, stop=True)
                        last.then_inc(s_done, 1)
                    if before:
                        pe.wait_ge(x2T_kept, 2 * g)
                        if later(g, 2):
                            pe.wait_ge(l_kept, g - 1)
                        for b in range(GB):
                            last = mm(psL[:, b * E:(b + 1) * E], xn2T[:, b * S:(b + 1) * S], P("router"),
                                      start=True, stop=True)
                        last.then_inc(l_done, 1)
                    if here:
                        pe.wait_ge(exp_done, GB * g + GB)
                        for b in range(GB):
                            last = nc.tensor.transpose(psP[:, b * S:(b + 1) * S], probs[:, b, :], P("ident"))
                        last.then_inc(pT_done, 1)

                def half_of(g, p):
                    return halfg[0] if type(g) is not int else g // 2

                halfg = [None]
                step(0, 0, True, False)
                with pe.Fori(0, G // 2 - 1) as h:
                    halfg[0] = h
                    step(2 * h + 1, 1, True, True)
                    halfg[0] = h + 1
                    step(2 * h + 2, 0, True, True)
                step(G - 1, 1, True, True)
                step(G, 0, False, True)


def experts(nc, sem, X, xg, P, wupT, wdnT, bdn, gates, xnT_all):
    with ExitStack() as stack:
        def sb(name, shape, dt=F32):
            return stack.enter_context(nc.sbuf_tensor(name, shape, dt))

        def ps(name, shape, dt=F32):
            return stack.enter_context(nc.psum_tensor(name, shape, dt))

        wup = sb("d_wup", [128, 2, FF])
        wdn = sb("d_wdn", [128, 2, FC, D])
        bdr = sb("d_bdn", [128, E, D])
        hT = [sb(f"d_hT{p}", [128, FC, GB * S]) for p in range(2)]
        psU = [ps(f"d_psU{c}", [128, 512]) for c in range(FC)]
        psY = [ps(f"d_psY{p}", [128, 512]) for p in range(2)]
        w_in = [sem(f"d_w_in{p}") for p in range(2)]
        bdn_in = sem("d_bdn_in")
        up_done = sem("d_up_done")
        gelu_done = sem("d_gelu_done")
        down_done = sem("d_down_done")
        x_done = sem("d_x_done")

        with nc.Block() as block:
            @block.sync
            def _(sp):
                sp.dma_start(bdr[:], bdn).then_inc(bdn_in, 16)
                for e in range(E):
                    if e >= 2:
                        sp.wait_ge(down_done, G * (e - 1))
                    sp.dma_start(wup[:, e % 2], wupT[:, e]).then_inc(w_in[e % 2], 16)
                    sp.dma_start(wdn[:, e % 2], wdnT[:, e]).then_inc(w_in[e % 2], 16)
                sp.wait_ge(bdn_in, 16)

            @block.vector
            def _(dve):
                def step(e, g, p):
                    k = G * e + g
                    dve.wait_ge(down_done, k + 1)
                    if e:
                        dve.wait_ge(x_done, GB * (k + 1 - G))
                    for b in range(GB):
                        nc.vector.scalar_tensor_tensor(xg(g, b), psY[p][:, b * D:(b + 1) * D],
                                                       gates[:, bass.ds(g * GB + b, 1), e], xg(g, b),
                                                       ALU.mult, ALU.add).then_inc(x_done, 1)
                for e in range(E):
                    with dve.Fori(0, G // 2) as h:
                        step(e, 2 * h, 0)
                        step(e, 2 * h + 1, 1)
                dve.wait_ge(x_done, E * G * GB)

            @block.scalar
            def _(act):
                def step(e, g, p):
                    for c in range(FC):
                        act.wait_ge(up_done, FC * (G * e + g) + c + 1)
                        nc.scalar.activation(hT[p][:, c, :], psU[c][:], ACT.Gelu,
                                             bias=P("bup")[:, e * FC + c:e * FC + c + 1]).then_inc(gelu_done, 1)
                for e in range(E):
                    with act.Fori(0, G // 2) as h:
                        step(e, 2 * h, 0)
                        step(e, 2 * h + 1, 1)

            @block.tensor
            def _(pe):
                mm = nc.tensor.matmul

                def up(e, g, p, c):
                    k = G * e + g
                    if later(k, 1):
                        pe.wait_ge(gelu_done, FC * (k - 1) + c + 1)
                    mm(psU[c][:], wup[:, e % 2, c * 128:(c + 1) * 128], xnT_all[:, bass.ds(g * GB * S, GB * S)],
                       start=True, stop=True).then_inc(up_done, 1)

                def down(e, g, p, b):
                    k = G * e + g
                    if b == 0:
                        pe.wait_ge(gelu_done, FC * k + FC)
                        if later(k, 2):
                            pe.wait_ge(x_done, GB * (k - 1))
                    for c in range(FC):
                        mm(psY[p][:, b * D:(b + 1) * D], hT[p][:, c, b * S:(b + 1) * S], wdn[:, e % 2, c, :],
                           start=c == 0, stop=False)
                    last = mm(psY[p][:, b * D:(b + 1) * D], P("ones")[0:1, :], bdr[0:1, e, :], start=False, stop=True)
                    if b == GB - 1:
                        last.then_inc(down_done, 1)

                pe.wait_ge(bdn_in, 16)
                for e in range(E):
                    pe.wait_ge(w_in[e % 2], 32 * (e // 2 + 1))
                    for c in range(FC):
                        up(e, 0, 0, c)

                    def step(g, p):
                        for k in range(FC):
                            if type(g) is not int or g < G - 1:
                                up(e, g + 1, 1 - p, k)
                            down(e, g, p, k)
                    step(0, 0)
                    with pe.Fori(0, G // 2 - 1) as h:
                        step(2 * h + 1, 1)
                        step(2 * h + 2, 0)
                    step(G - 1, 1)


def host_consts():
    f = np.arange(CH)[None, :] * 128 + np.arange(128)[:, None]
    head = f // KEYS
    vm = np.zeros((128, CH, SLOTS), np.float32)
    for c in range(CH):
        for slot in range(SLOTS):
            if first_head(c) + slot < HH:
                vm[:, c, slot] = head[:, c] == first_head(c) + slot
    rowsel = np.zeros((128, CH, 128), np.float32)
    rowsel[:KEYS] = (f.T % KEYS)[None] == np.arange(KEYS)[:, None, None]
    km = ((np.arange(128)[:, None] // DH) % HH == np.arange(HH)[None, :]).astype(np.float32)
    sel = (np.arange(FLAT)[None, :] // KEYS == np.arange(HH)[:, None]).astype(np.float32)
    return vm.reshape(128, -1), rowsel.reshape(128, -1), km, sel


def kernel(x, ctx_1024, L0_xattn_Wq, L0_xattn_bq, L0_xattn_Wk, L0_xattn_bk, L0_xattn_Wv, L0_xattn_bv, L0_xattn_Wo,
           L0_xattn_bo, L0_ffn_W1, L0_ffn_b1, L0_ffn_W2, L0_ffn_b2, L1_xattn_Wq, L1_xattn_bq, L1_xattn_Wk,
           L1_xattn_bk, L1_xattn_Wv, L1_xattn_bv, L1_ffn_w_up, L1_ffn_w_down, L1_ffn_b_up, L1_ffn_b_down,
           L1_ffn_w_router, _phases="ABCD", _raw=False):
    import ml_dtypes
    import concourse.bacc as _bacc
    from concourse import mybir as _mybir
    from concourse.bass_utils import run_bass_kernel_spmd as _run

    def f(a):
        return np.asarray(a)

    vm, rowsel, km, sel = host_consts()
    col = lambda v: f(v).reshape(-1, 128).T
    rows = lambda v: np.broadcast_to(f(v)[None, :], (128, f(v).shape[0]))
    cols = {
        "Wq0": f(L0_xattn_Wq), "Wk0": f(L0_xattn_Wk),
        "Wv0": f(L0_xattn_Wv), "Wo0": f(L0_xattn_Wo),
        "W1T": f(L0_ffn_W1).T, "W2T": f(L0_ffn_W2).T.reshape(FC, 128, D).transpose(1, 0, 2).reshape(128, FF),
        "Wq1": f(L1_xattn_Wq), "Wk1": f(L1_xattn_Wk), "Wv1": f(L1_xattn_Wv), "router": f(L1_ffn_w_router).T,
        "bq0": col(L0_xattn_bq), "bk0": col(L0_xattn_bk), "bv0": col(L0_xattn_bv), "b1": col(L0_ffn_b1),
        "bq1": col(L1_xattn_bq), "bk1": col(L1_xattn_bk), "ident": np.eye(128, dtype=np.float32),
        "kmask": km, "vmask": vm, "rowsel": rowsel, "ones": np.ones((128, 128), np.float32), "bo0": rows(L0_xattn_bo),
        "b2": rows(L0_ffn_b2), "bv1": rows(L1_xattn_bv),
        "bup": f(L1_ffn_b_up).reshape(E * FC, 128).T, "eidx": rows(np.arange(E, dtype=np.float32)),
    }
    pack = np.concatenate([cols[n].reshape(128, PACK[n][1]) for n in PACK], 1)
    ctxT = f(ctx_1024).transpose(2, 0, 1)
    arrays = {
        "x_in": f(x), "ctxT": ctxT, "pack": pack,
        "sel": sel.astype(ml_dtypes.bfloat16), "identb": np.eye(128).astype(ml_dtypes.bfloat16),
        "wupT": f(L1_ffn_w_up).transpose(2, 0, 1),
        "wdnT": f(L1_ffn_w_down).transpose(2, 0, 1).reshape(FC, 128, E, D).transpose(1, 2, 0, 3),
        "bdn": np.broadcast_to(f(L1_ffn_b_down)[None], (128, E, D)),
    }
    arrays = {k: np.ascontiguousarray(v) for k, v in arrays.items()}
    nc = _bacc.Bacc("TRN2", target_bir_lowering=False, num_devices=1)
    aps = [nc.dram_tensor(k, v.shape, _mybir.dt.from_np(v.dtype), kind="ExternalInput").ap() for k, v in arrays.items()]
    out = nc.dram_tensor("out", (B, S, D), F32, kind="ExternalOutput").ap()
    build(nc, *aps, out, phases=_phases)
    if _raw:
        return nc, arrays
    r = _run(nc, [arrays], core_ids=[0])
    return r.results[0]["out"]
```

```python
from contextlib import ExitStack

import numpy as np
import concourse.bass as bass
from concourse import mybir

F32 = mybir.dt.float32
BF16 = mybir.dt.bfloat16
U32 = mybir.dt.uint32
I32 = mybir.dt.int32
ALU = mybir.AluOpType
ACT = mybir.ActivationFunctionType
AX_X = mybir.AxisListType.X

B, S, D = 64, 128, 128
KEYS = 77
HEADS, DH = 16, 8
FF = 512
E = 8
GB = 4
G = B // GB
HH = HEADS // 2
CH = 5
UNITS = 2 * GB
FLAT = CH * 128
SLOTS = 3
FC = FF // 128
EPS = 1e-5
ROW = D + 2
TT = 256
TB = TT // 128
TILES = (2 * B * S + E * (TT - 1)) // TT // 2 * 2 + 2
REGION = B * S + TT
SPARE = E * REGION
KMAX = B * S // TT
WCOLS = 2 * FF + FC + D
SCALE = 1.0 / float(np.sqrt(np.float32(128.0)))


def hold(engine, sem, value, passed):
    engine.wait_ge(sem, value)
    engine.sem_inc(passed)


def later(n, least):
    return type(n) is not int or n >= least


def first_head(c):
    return c * 128 // KEYS


PACK = {}
_at = 0
for _name, _n in (("Wq0", D), ("Wk0", D), ("Wv0", D), ("Wo0", D), ("W1T", FF), ("W2T", FF), ("Wq1", D),
                  ("Wk1", D), ("Wv1", D), ("router", E), ("bq0", 1), ("bk0", 1), ("bv0", 1), ("b1", FC), ("bq1", 1),
                  ("bk1", 1), ("ident", 128), ("kmask", HH), ("vmask", CH * SLOTS), ("rowsel", CH * 128), ("ones", 128),
                  ("bo0", D), ("b2", D), ("bv1", D), ("eidx", E), ("steps", KMAX), ("part", 1)):
    PACK[_name] = (_at, _n)
    _at += _n
PACK_COLS = _at


def build(nc, x, ctxT, pack, sel, identb, weights, before, tokens, padding, out, phases="ABCD"):
    with ExitStack() as stack:
        def sb(name, shape, dt=F32):
            return stack.enter_context(nc.sbuf_tensor(name, shape, dt))

        def sem(name):
            return stack.enter_context(nc.semaphore(name))

        X = sb("X", [128, B, D])
        par = sb("par", [128, PACK_COLS])

        def P(name):
            at, n = PACK[name]
            return par[:, at:at + n]

        selm = sb("selm", [HH, FLAT], BF16)
        idb = sb("idb", [128, 128], BF16)
        halves = sb("halves", [128, GB])
        epsilons = sb("epsilons", [128, GB])
        passed = sem("passed")
        params_in = sem("params_in")
        params2_in = sem("params2_in")
        halves_set = sem("halves_set")

        def xg(g, b=None):
            if b is None:
                return X[:, bass.ds(g * GB, GB), :]
            return X[:, bass.ds(g * GB + b, 1), :].rearrange("p a d -> p (a d)")

        prologue(nc, sem, pack, sel, identb, par, selm, idb, halves, epsilons, passed, params_in, params2_in, halves_set)
        attention0(nc, sem, x, ctxT, X, xg, P, selm, idb, halves, epsilons, passed, params_in)
        if "B" in phases:
            feed_forward0(nc, sem, X, xg, P, halves, epsilons, passed)
        if "C" in phases:
            rows = nc.dram_tensor("rows", (SPARE + TT, ROW), F32, kind="Internal").ap()
            fill = sb("fill", [128, E])
            attention1(nc, sem, ctxT, X, xg, P, halves, epsilons, passed, before, tokens, padding, rows, fill, out)
        if "D" in phases:
            experts(nc, sem, P, passed, weights, padding, rows, fill, out)
        if "C" not in phases:
            with nc.Block() as blk:
                stored = sem("stored")

                @blk.sync
                def _(sp):
                    sp.dma_start(out[0:B * S].rearrange("(b p) d -> p b d", p=128), X[:]).then_inc(stored, 16)
                    sp.wait_ge(stored, 16)


def prologue(nc, sem, pack, sel, identb, par, selm, idb, halves, epsilons, passed, params_in, params2_in, halves_set):
    with nc.Block() as block:
        @block.sync
        def _(sp):
            sp.dma_start(par[:], pack).then_inc(params_in, 16)
            sp.dma_start(selm[:], sel).then_inc(params2_in, 16)
            sp.dma_start(idb[:], identb).then_inc(params2_in, 16)
            sp.wait_ge(params_in, 16)
            sp.wait_ge(params2_in, 32)

        @block.gpsimd
        def _(pool):
            nc.gpsimd.memset(halves[:], -0.5).then_inc(halves_set, 1)
            nc.gpsimd.memset(epsilons[:], EPS).then_inc(halves_set, 1)
            pool.wait_ge(halves_set, 2)


def attention0(nc, sem, x, ctxT, X, xg, P, selm, idb, halves, epsilons, passed, params_in):
    with ExitStack() as stack:
        def sb(name, shape, dt=F32):
            return stack.enter_context(nc.sbuf_tensor(name, shape, dt))

        def ps(name, shape, dt=F32):
            return stack.enter_context(nc.psum_tensor(name, shape, dt))

        ctx = sb("a_ctx", [128, 2, GB, KEYS])
        stats = sb("a_stats", [128, GB, 6])
        mv = sb("a_mv", [128, GB, 2])
        veps = sb("a_veps", [128, GB])
        rstd = sb("a_rstd", [128, GB])
        xn = sb("a_xn", [128, GB, D])
        xnT = sb("a_xnT", [128, GB * S])
        qT = [sb(f"a_qT{p}", [128, GB * S]) for p in range(2)]
        kT = sb("a_kT", [128, GB, KEYS])
        kbd = [sb(f"a_kbd{p}", [128, GB, FLAT]) for p in range(2)]
        vals = sb("a_vals", [KEYS, GB, D + DH])
        vx = [sb(f"a_vx{p}", [128, CH, GB * 2, 128]) for p in range(2)]
        negmax = [sb(f"a_negmax{p}", [128, HH], BF16) for p in range(2)]
        negmaxT = [sb(f"a_negmaxT{p}", [HH, 128], BF16) for p in range(2)]
        probs = [sb(f"a_probs{p}", [128, FLAT]) for p in range(2)]
        rden = sb("a_rden", [128, 2, HH])
        o = sb("a_o", [128, GB, D])
        oT = sb("a_oT", [128, GB * S])

        psS = ps("a_psS", [128, 2, 512])
        psT = [ps(f"a_psT{p}", [128, 1024]) for p in range(2)]
        psO = ps("a_psO", [128, 512])
        psM = ps("a_psM", [128, 512])
        psMax = [psT[p][0:HH, 768:832].bitcast(BF16) for p in range(2)]

        x_in = [sem(f"a_x_in{p}") for p in range(2)]
        ctx_in = [sem(f"a_ctx_in{p}") for p in range(2)]
        consts = sem("a_consts")
        ones_set = sem("a_ones_set")
        vals_done = sem("a_vals_done")
        vals_kept = sem("a_vals_kept")
        stats_done = sem("a_stats_done")
        aggr_done = sem("a_aggr_done")
        veps_done = sem("a_veps_done")
        rstd_done = sem("a_rstd_done")
        xn_done = sem("a_xn_done")
        bo_added = sem("a_bo_added")
        xT_done = sem("a_xT_done")
        xT_kept = sem("a_xT_kept")
        q_done = sem("a_q_done")
        q_kept = sem("a_q_kept")
        k_done = sem("a_k_done")
        k_kept = sem("a_k_kept")
        kbd_done = sem("a_kbd_done")
        v_done = sem("a_v_done")
        v_kept = sem("a_v_kept")
        s_done = sem("a_s_done")
        max_done = sem("a_max_done")
        maxT_done = sem("a_maxT_done")
        maxT_kept = sem("a_maxT_kept")
        t_done = sem("a_t_done")
        exp_done = sem("a_exp_done")
        pv_done = sem("a_pv_done")
        rden_done = sem("a_rden_done")
        o_done = sem("a_o_done")
        oT_done = sem("a_oT_done")
        oT_kept = sem("a_oT_kept")
        wo_done = sem("a_wo_done")
        x_done = sem("a_x_done")

        def over_groups(eng, first, step, last):
            first(0)
            with eng.Fori(0, G // 2 - 1) as h:
                step(2 * h + 1, 1)
                step(2 * h + 2, 0)
            last(G - 1)

        with nc.Block() as block:
            @block.sync
            def _(sp):
                def load(g, p, before):
                    if before is not None:
                        sp.wait_ge(x_in[p], 16 * before)
                        sp.wait_ge(ctx_in[p], 16 * before)
                        sp.wait_ge(vals_done, g - 1)
                    sp.dma_start(xg(g), x[bass.ds(g * GB, GB)].rearrange("b p d -> p b d")).then_inc(x_in[p], 16)
                    sp.dma_start(ctx[:, p], ctxT[:, bass.ds(g * GB, GB), :]).then_inc(ctx_in[p], 16)

                load(0, 0, None)
                load(1, 1, None)
                with sp.Fori(1, G // 2) as h:
                    load(2 * h, 0, h)
                    load(2 * h + 1, 1, h)
                for p in range(2):
                    sp.wait_ge(x_in[p], 16 * (G // 2))
                    sp.wait_ge(ctx_in[p], 16 * (G // 2))

            @block.gpsimd
            def _(pool):
                for p in range(2):
                    nc.gpsimd.memset(kbd[p][:], 0.0).then_inc(consts, 1)
                    nc.gpsimd.memset(vx[p][:], 0.0).then_inc(consts, 1)
                nc.gpsimd.memset(vals[:], 0.0).then_inc(consts, 1)
                pool.wait_ge(consts, 5)

                def norm(g):
                    pool.wait_ge(aggr_done, GB * g + GB)
                    nc.gpsimd.tensor_tensor(veps[:], mv[:, :, 1], epsilons[:], ALU.add).then_inc(veps_done, 1)
                    pool.wait_ge(veps_done, g + 1)
                    nc.gpsimd.tensor_tensor(rstd[:], veps[:], halves[:], ALU.pow).then_inc(rstd_done, 1)
                    pool.wait_ge(xn_done, GB * g + GB)
                    nc.gpsimd.tensor_tensor(xg(g), xg(g), P("bo0").unsqueeze(1).to_broadcast([128, GB, D]),
                                            ALU.add).then_inc(bo_added, 1)

                def spread_keys(g, p):
                    for b in range(GB):
                        pool.wait_ge(k_kept, g + 1)
                        nc.gpsimd.tensor_tensor(
                            kbd[p][:, b, 0:HH * KEYS].rearrange("p (h k) -> p h k", h=HH),
                            kT[:, b, :].unsqueeze(1).to_broadcast([128, HH, KEYS]),
                            P("kmask").unsqueeze(2).to_broadcast([128, HH, KEYS]), ALU.mult).then_inc(kbd_done, 1)

                norm(0)
                spread_keys(0, 0)

                def step(g, p):
                    norm(g + 1)
                    spread_keys(g + 1, 1 - p)
                over_groups(pool, lambda g: step(g, 0), step, lambda g: None)

            @block.vector
            def _(dve):
                for p in range(2):
                    dve.wait_ge(consts, 4)
                    for c in range(CH):
                        at = (DH + 1) * first_head(c)
                        ones = vx[p][:, c, :, at:at + SLOTS * (DH + 1)].rearrange("p n (s e) -> p n s e", e=DH + 1)
                        nc.vector.tensor_copy(ones[:, :, :, DH], P("vmask")[:, c * SLOTS:(c + 1) * SLOTS].unsqueeze(1)
                                              .to_broadcast([128, GB * 2, SLOTS])).then_inc(ones_set, 1)

                def stats_of(g, p, again):
                    hold(dve, x_in[p], 16 * (again + 1), passed)
                    for b in range(GB):
                        nc.vector.bn_stats(stats[:, b, :], xg(g, b)).then_inc(stats_done, 1)
                    hold(dve, stats_done, GB * g + GB, passed)
                    for b in range(GB):
                        nc.vector.bn_aggr(mv[:, b, :], stats[:, b, :]).then_inc(aggr_done, 1)

                def normalise(g):
                    dve.wait_ge(rstd_done, g + 1)
                    if later(g, 1):
                        dve.wait_ge(xT_done, g)
                    for b in range(GB):
                        nc.vector.tensor_scalar(xn[:, b, :], xg(g, b), mv[:, b, 0:1], rstd[:, b:b + 1],
                                                ALU.subtract, ALU.mult).then_inc(xn_done, 1)

                def keep_values(g, p, part):
                    dve.wait_ge(v_done, 3 * g + part + 1)
                    if later(g, 2) and part == 0:
                        dve.wait_ge(pv_done, UNITS * (g - 1))
                    for k, c in enumerate(range(2 * part, min(2 * part + 2, CH))):
                        at = (DH + 1) * first_head(c)
                        nc.vector.tensor_tensor(
                            vx[p][:, c, :, at:at + SLOTS * (DH + 1)].rearrange("p n (s e) -> p n s e", e=DH + 1)[:, :, :, 0:DH],
                            psM[:, k * 192:(k + 1) * 192].rearrange("p (n s e) -> p n s e", s=SLOTS, e=DH),
                            P("vmask")[:, c * SLOTS:(c + 1) * SLOTS].unsqueeze(1).unsqueeze(3)
                            .to_broadcast([128, GB * 2, SLOTS, DH]), ALU.mult).then_inc(v_kept, 1)

                def find_max(g, u):
                    n = UNITS * g + u
                    dve.wait_ge(s_done, n + 1)
                    if later(n, 2):
                        dve.wait_ge(maxT_done, n - 1)
                    nc.vector.tensor_reduce(negmax[u % 2][:], psS[:, :, 0:HH // 2 * KEYS].rearrange(
                        "p a (h k) -> p a h k", k=KEYS), AX_X, ALU.max, negate=True).then_inc(max_done, 1)

                def keep_max(g, u):
                    n = UNITS * g + u
                    dve.wait_ge(maxT_done, n + 1)
                    if later(n, 2):
                        dve.wait_ge(t_done, n - 1)
                    nc.vector.tensor_copy(negmaxT[u % 2][:], psMax[u % 2]).then_inc(maxT_kept, 1)

                def divide(g, b):
                    k = GB * g + b
                    dve.wait_ge(pv_done, 2 * k + 2)
                    acc = psO[:, 0:256].rearrange("p (a c) -> p a c", a=2)[:, :, 0:HH * (DH + 1)].rearrange(
                        "p a (h e) -> p a h e", e=DH + 1)
                    nc.vector.reciprocal(rden[:], acc[:, :, :, DH]).then_inc(rden_done, 1)
                    dve.wait_ge(rden_done, k + 1)
                    if later(g, 1):
                        dve.wait_ge(oT_done, g)
                    nc.vector.tensor_tensor(o[:, b, :].rearrange("p (a h e) -> p a h e", a=2, e=DH),
                                            acc[:, :, :, 0:DH],
                                            rden[:].unsqueeze(3).to_broadcast([128, 2, HH, DH]),
                                            ALU.mult).then_inc(o_done, 1)

                def residual(g):
                    dve.wait_ge(wo_done, g + 1)
                    dve.wait_ge(bo_added, g + 1)
                    nc.vector.tensor_tensor(xg(g), xg(g), psM[:].rearrange("p (b d) -> p b d", d=D),
                                            ALU.add).then_inc(x_done, 1)

                stats_of(0, 0, 0)
                normalise(0)
                for part in range(3):
                    keep_values(0, 0, part)

                def step(g, p, again_next, prev=True, nxt=True):
                    for u in range(UNITS):
                        find_max(g, u)
                        if u % 2 == 0 and (prev or u):
                            divide(g if u else g - 1, (u // 2 - 1) % GB)
                        keep_max(g, u)
                        if u == 0 and nxt:
                            stats_of(g + 1, 1 - p, again_next)
                        if u == 1 and nxt:
                            normalise(g + 1)
                        if u == 3 and prev:
                            residual(g - 1)
                        if u == 6 and nxt:
                            keep_values(g + 1, 1 - p, 0)
                            keep_values(g + 1, 1 - p, 1)
                        if u == 7 and nxt:
                            keep_values(g + 1, 1 - p, 2)

                step(0, 0, 0, prev=False)
                with dve.Fori(0, G // 2 - 1) as h:
                    step(2 * h + 1, 1, h + 1)
                    step(2 * h + 2, 0, h + 1)
                step(G - 1, 1, 0, nxt=False)
                divide(G - 1, GB - 1)
                residual(G - 1)

            @block.scalar
            def _(act):
                def keep_xT(g):
                    act.wait_ge(xT_done, g + 1)
                    if later(g, 1):
                        act.wait_ge(q_done, g)
                    nc.scalar.copy(xnT[:], psM[:]).then_inc(xT_kept, 1)

                def keep_q(g, p):
                    act.wait_ge(q_done, g + 1)
                    nc.scalar.activation(qT[p][:], psM[:], ACT.Identity, bias=P("bq0")).then_inc(q_kept, 1)

                def keep_k(g):
                    act.wait_ge(k_done, g + 1)
                    if later(g, 1):
                        act.wait_ge(kbd_done, GB * g)
                    nc.scalar.activation(kT[:], psM[:, 0:GB * KEYS].rearrange("p (b k) -> p b k", k=KEYS),
                                         ACT.Identity, bias=P("bk0")).then_inc(k_kept, 1)

                def keep_vals(g):
                    act.wait_ge(vals_done, g + 1)
                    if later(g, 1):
                        act.wait_ge(v_done, 3 * g)
                    nc.scalar.copy(vals[:, :, 0:D], psM[0:KEYS, :].rearrange("p (b d) -> p b d", d=D)).then_inc(vals_kept, 1)

                def exponentials(g, u):
                    n = UNITS * g + u
                    act.wait_ge(t_done, n + 1)
                    if later(n, 2):
                        act.wait_ge(pv_done, n - 1)
                    nc.scalar.activation(probs[u % 2][:], psT[u % 2][:, 0:FLAT], ACT.Exp,
                                         scale=SCALE).then_inc(exp_done, 1)

                def keep_oT(g):
                    act.wait_ge(oT_done, g + 1)
                    if later(g, 1):
                        act.wait_ge(wo_done, g)
                    nc.scalar.activation(oT[:], psM[:], ACT.Identity, bias=P("bv0")).then_inc(oT_kept, 1)

                keep_xT(0)
                keep_q(0, 0)
                keep_k(0)
                keep_vals(0)

                def step(g, p, prev=True, nxt=True):
                    for u in range(UNITS):
                        exponentials(g, u)
                        if u == 1 and prev:
                            keep_oT(g - 1)
                        if u == 2 and nxt:
                            keep_xT(g + 1)
                        if u == 4 and nxt:
                            keep_q(g + 1, 1 - p)
                        if u == 5 and nxt:
                            keep_k(g + 1)
                            keep_vals(g + 1)
                over_groups(act, lambda g: step(g, 0, prev=False), step, lambda g: step(g, 1, nxt=False))
                keep_oT(G - 1)

            @block.tensor
            def _(pe):
                mm = nc.tensor.matmul

                def transpose_x(g):
                    pe.wait_ge(xn_done, GB * g + GB)
                    for b in range(GB):
                        last = nc.tensor.transpose(psM[:, b * S:(b + 1) * S], xn[:, b, :], P("ident"))
                    last.then_inc(xT_done, 1)

                def queries(g):
                    pe.wait_ge(xT_kept, g + 1)
                    mm(psM[:], P("Wq0"), xnT[:], start=True, stop=True).then_inc(q_done, 1)

                def keys(g, p, again):
                    pe.wait_ge(q_kept, g + 1)
                    pe.wait_ge(ctx_in[p], 16 * (again + 1))
                    mm(psM[:, 0:GB * KEYS], P("Wk0"), ctx[:, p], start=True, stop=True).then_inc(k_done, 1)

                def project_values(g, p):
                    pe.wait_ge(k_kept, g + 1)
                    for b in range(GB):
                        last = mm(psM[0:KEYS, b * D:(b + 1) * D], ctx[:, p, b, :], P("Wv0"), start=True, stop=True)
                    last.then_inc(vals_done, 1)

                def values(g, part):
                    pe.wait_ge(vals_kept, g + 1)
                    if part:
                        pe.wait_ge(v_kept, CH * g + 2 * part)
                    for k, c in enumerate(range(2 * part, min(2 * part + 2, CH))):
                        for half in range(2):
                            at = D // 2 * half + DH * first_head(c)
                            last = mm(psM[:, k * 192:(k + 1) * 192].rearrange("p (b a e) -> p b a e", b=GB, a=2)[:, :, half, :],
                                      P("rowsel")[0:KEYS, c * 128:(c + 1) * 128], vals[:, :, at:at + SLOTS * DH],
                                      start=True, stop=True)
                    last.then_inc(v_done, 1)

                def scores(g, p, u):
                    n = UNITS * g + u
                    b, lo = u // 2, 64 * (u % 2)
                    if u == 0:
                        pe.wait_ge(q_kept, g + 1)
                    if u % 2 == 0:
                        pe.wait_ge(kbd_done, GB * g + b + 1)
                    if later(n, 1):
                        pe.wait_ge(max_done, n)
                    for a in range(2):
                        last = mm(psS[:, a, 0:HH // 2 * KEYS], qT[p][lo:lo + 64, b * S:(b + 1) * S],
                                  kbd[p][lo:lo + 64, b, a * HH // 2 * KEYS:(a + 1) * HH // 2 * KEYS],
                                  start=True, stop=True)
                    last.then_inc(s_done, 1)

                def scores_t(g, p, u):
                    n = UNITS * g + u
                    b, lo = u // 2, 64 * (u % 2)
                    if later(n, 2):
                        pe.wait_ge(exp_done, n - 1)
                    for c in range(CH - 1):
                        mm(psT[u % 2][:, c * 128:(c + 1) * 128], kbd[p][lo:lo + 64, b, c * 128:(c + 1) * 128],
                           qT[p][lo:lo + 64, b * S:(b + 1) * S], start=c == 0, stop=False, skip_group_check=True)

                def transpose_max(g, u):
                    n = UNITS * g + u
                    pe.wait_ge(max_done, n + 1)
                    nc.tensor.transpose(psMax[u % 2], negmax[u % 2][:], idb[:]).then_inc(maxT_done, 1)

                def subtract_max(g, p, u):
                    n = UNITS * g + u
                    b, lo, c = u // 2, 64 * (u % 2), CH - 1
                    pe.wait_ge(maxT_kept, n + 1)
                    mm(psT[u % 2][:, c * 128:(c + 1) * 128], kbd[p][lo:lo + 64, b, c * 128:(c + 1) * 128],
                       qT[p][lo:lo + 64, b * S:(b + 1) * S], start=True, stop=False, skip_group_check=True)
                    for c in range(CH):
                        last = mm(psT[u % 2][:, c * 128:(c + 1) * 128], selm[:, c * 128:(c + 1) * 128],
                                  negmaxT[u % 2][:], start=False, stop=True, skip_group_check=True)
                    last.then_inc(t_done, 1)

                def weigh(g, p, u):
                    n = UNITS * g + u
                    b, half = u // 2, u % 2
                    pe.wait_ge(exp_done, n + 1)
                    if half == 0:
                        if b == 0:
                            pe.wait_ge(v_kept, CH * g + CH)
                        if later(n, 1):
                            pe.wait_ge(o_done, GB * g + b)
                    for c in range(CH):
                        last = mm(psO[:, half * 128:(half + 1) * 128], probs[u % 2][:, c * 128:(c + 1) * 128],
                                  vx[p][:, c, 2 * b + half, :], start=c == 0, stop=c == CH - 1)
                    last.then_inc(pv_done, 1)

                def transpose_o(g):
                    pe.wait_ge(o_done, GB * g + GB)
                    for b in range(GB):
                        last = nc.tensor.transpose(psM[:, b * S:(b + 1) * S], o[:, b, :], P("ident"))
                    last.then_inc(oT_done, 1)

                def project(g):
                    pe.wait_ge(oT_kept, g + 1)
                    for b in range(GB):
                        last = mm(psM[:, b * D:(b + 1) * D], oT[:, b * S:(b + 1) * S], P("Wo0"), start=True, stop=True)
                    last.then_inc(wo_done, 1)

                pe.wait_ge(consts, 5)
                pe.wait_ge(ones_set, 2 * CH)
                transpose_x(0)
                queries(0)
                keys(0, 0, 0)
                project_values(0, 0)
                for part in range(3):
                    values(0, part)
                scores(0, 0, 0)

                def step(g, p, again_next, prev=True, nxt=True):
                    for u in range(UNITS):
                        scores_t(g, p, u)
                        if u:
                            weigh(g, p, u - 1)
                        elif prev:
                            weigh(g - 1, 1 - p, UNITS - 1)
                        transpose_max(g, u)
                        if u < UNITS - 1:
                            scores(g, p, u + 1)
                        elif nxt:
                            scores(g + 1, 1 - p, 0)
                        subtract_max(g, p, u)
                        if u == 1 and prev:
                            pe.wait_ge(v_kept, CH * g + CH)
                            transpose_o(g - 1)
                        if u == 2 and nxt:
                            if prev:
                                pe.wait_ge(oT_kept, g)
                            else:
                                pe.wait_ge(v_kept, CH)
                            transpose_x(g + 1)
                        if u == 3 and prev:
                            if nxt:
                                pe.wait_ge(xT_kept, g + 2)
                            project(g - 1)
                        if u == 4 and nxt:
                            if prev:
                                pe.wait_ge(x_done, g)
                            queries(g + 1)
                        if u == 5 and nxt:
                            keys(g + 1, 1 - p, again_next)
                            project_values(g + 1, 1 - p)
                        if u == 6 and nxt:
                            values(g + 1, 0)
                            values(g + 1, 1)
                        if u == 7 and nxt:
                            values(g + 1, 2)

                step(0, 0, 0, prev=False)
                with pe.Fori(0, G // 2 - 1) as h:
                    step(2 * h + 1, 1, h + 1)
                    step(2 * h + 2, 0, h + 1)
                step(G - 1, 1, 0, nxt=False)
                weigh(G - 1, 1, UNITS - 1)
                transpose_o(G - 1)
                project(G - 1)


def ternary(nc, sem, sb, P):
    absum = sb("t_absum", [128, 2])
    half = sb("t_half", [128, 2])
    neg = sb("t_neg", [128, 2])
    up = sb("t_up", [128, FF])
    down = sb("t_down", [128, FF])
    step_done = sem("t_step_done")
    summed = sem("t_summed")
    with ExitStack() as stack:
        total = stack.enter_context(nc.psum_tensor("t_total", [128, 2], F32))
        with nc.Block() as block:
            @block.tensor
            def _(pe):
                pe.wait_ge(step_done, 2)
                nc.tensor.matmul(total[:], P("ones"), absum[:], start=True, stop=True).then_inc(summed, 1)

            @block.vector
            def _(dve):
                for j, name in enumerate(("W1T", "W2T")):
                    nc.vector.tensor_reduce(absum[:, j:j + 1], P(name), AX_X, ALU.add,
                                            apply_absolute_value=True).then_inc(step_done, 1)
                dve.wait_ge(summed, 1)
                nc.vector.tensor_scalar(half[:], total[:], 1.0 / (D * FF), 1e-8, ALU.mult, ALU.max).then_inc(step_done, 1)
                dve.wait_ge(step_done, 3)
                nc.vector.tensor_scalar(neg[:], half[:], -0.5, None, ALU.mult).then_inc(step_done, 1)
                dve.wait_ge(step_done, 4)
                nc.vector.tensor_scalar(half[:], half[:], 0.5, None, ALU.mult).then_inc(step_done, 1)
                n = 5
                for j, name in enumerate(("W1T", "W2T")):
                    w = P(name)
                    dve.wait_ge(step_done, n)
                    nc.vector.tensor_scalar(up[:], w, half[:, j:j + 1], None, ALU.is_gt).then_inc(step_done, 1)
                    nc.vector.tensor_scalar(down[:], w, neg[:, j:j + 1], None, ALU.is_lt).then_inc(step_done, 1)
                    dve.wait_ge(step_done, n + 2)
                    nc.vector.tensor_tensor(up[:], up[:], down[:], ALU.subtract).then_inc(step_done, 1)
                    dve.wait_ge(step_done, n + 3)
                    nc.vector.tensor_tensor(up[:], up[:], w, ALU.subtract).then_inc(step_done, 1)
                    dve.wait_ge(step_done, n + 4)
                    nc.vector.tensor_tensor(w, w, up[:], ALU.add).then_inc(step_done, 1)
                    n += 5
                dve.wait_ge(step_done, n)


def feed_forward0(nc, sem, X, xg, P, halves, epsilons, passed):
    with ExitStack() as stack:
        def sb(name, shape, dt=F32):
            return stack.enter_context(nc.sbuf_tensor(name, shape, dt))

        def ps(name, shape, dt=F32):
            return stack.enter_context(nc.psum_tensor(name, shape, dt))

        ternary(nc, sem, sb, P)
        stats = sb("b_stats", [128, GB, 6])
        mv = sb("b_mv", [128, GB, 2])
        veps = sb("b_veps", [128, GB])
        rstd = sb("b_rstd", [128, GB])
        xn = sb("b_xn", [128, GB, D])
        xnT = [sb(f"b_xnT{p}", [128, GB * S]) for p in range(2)]
        hT = [sb(f"b_hT{p}", [128, FC, GB * S]) for p in range(2)]
        psX = ps("b_psX", [128, 512])
        psU = [ps(f"b_psU{c}", [128, 512]) for c in range(FC)]
        psY = [ps(f"b_psY{p}", [128, 512]) for p in range(2)]

        stats_done = sem("b_stats_done")
        aggr_done = sem("b_aggr_done")
        veps_done = sem("b_veps_done")
        rstd_done = sem("b_rstd_done")
        xn_done = sem("b_xn_done")
        b2_added = sem("b_b2_added")
        xT_done = sem("b_xT_done")
        xT_kept = sem("b_xT_kept")
        up_done = sem("b_up_done")
        gelu_done = sem("b_gelu_done")
        down_done = sem("b_down_done")
        x_done = sem("b_x_done")

        def over_groups(eng, step):
            step(0, 0)
            with eng.Fori(0, (G - 4) // 2) as h:
                step(2 * h + 1, 1)
                step(2 * h + 2, 0)
            for g in range(G - 3, G):
                step(g, g % 2)

        def has(g, ahead):
            return type(g) is not int or g + ahead < G

        with nc.Block() as block:
            @block.gpsimd
            def _(pool):
                def norm(g):
                    pool.wait_ge(aggr_done, GB * g + GB)
                    nc.gpsimd.tensor_tensor(veps[:], mv[:, :, 1], epsilons[:], ALU.add).then_inc(veps_done, 1)
                    pool.wait_ge(veps_done, g + 1)
                    nc.gpsimd.tensor_tensor(rstd[:], veps[:], halves[:], ALU.pow).then_inc(rstd_done, 1)
                    pool.wait_ge(xn_done, GB * g + GB)
                    nc.gpsimd.tensor_tensor(xg(g), xg(g), P("b2").unsqueeze(1).to_broadcast([128, GB, D]),
                                            ALU.add).then_inc(b2_added, 1)

                for g in range(3):
                    norm(g)
                over_groups(pool, lambda g, p: norm(g + 3) if has(g, 3) else None)

            @block.vector
            def _(dve):
                def stats_of(g):
                    for b in range(GB):
                        nc.vector.bn_stats(stats[:, b, :], xg(g, b)).then_inc(stats_done, 1)
                    hold(dve, stats_done, GB * g + GB, passed)
                    for b in range(GB):
                        nc.vector.bn_aggr(mv[:, b, :], stats[:, b, :]).then_inc(aggr_done, 1)

                def normalise(g):
                    dve.wait_ge(rstd_done, g + 1)
                    if later(g, 1):
                        dve.wait_ge(xT_done, g)
                    for b in range(GB):
                        nc.vector.tensor_scalar(xn[:, b, :], xg(g, b), mv[:, b, 0:1], rstd[:, b:b + 1],
                                                ALU.subtract, ALU.mult).then_inc(xn_done, 1)

                for g in range(2):
                    stats_of(g)
                    normalise(g)
                stats_of(2)

                def step(g, p):
                    if has(g, 2):
                        normalise(g + 2)
                    if has(g, 3):
                        stats_of(g + 3)
                    dve.wait_ge(down_done, g + 1)
                    dve.wait_ge(b2_added, g + 1)
                    nc.vector.tensor_tensor(xg(g), xg(g), psY[p][:].rearrange("p (b d) -> p b d", d=D),
                                            ALU.add).then_inc(x_done, 1)
                over_groups(dve, step)
                dve.wait_ge(x_done, G)

            @block.scalar
            def _(act):
                def keep_xT(g, p):
                    act.wait_ge(xT_done, g + 1)
                    if later(g, 2):
                        act.wait_ge(up_done, FC * (g - 1))
                    nc.scalar.copy(xnT[p][:], psX[:]).then_inc(xT_kept, 1)

                def gelu(g, p, c):
                    act.wait_ge(up_done, FC * g + c + 1)
                    if later(g, 2) and c == 0:
                        act.wait_ge(down_done, g - 1)
                    nc.scalar.activation(hT[p][:, c, :], psU[c][:], ACT.Gelu, bias=P("b1")[:, c:c + 1]).then_inc(gelu_done, 1)

                keep_xT(0, 0)
                for c in range(FC):
                    gelu(0, 0, c)
                keep_xT(1, 1)

                def step(g, p):
                    if has(g, 1):
                        for c in range(FC):
                            gelu(g + 1, 1 - p, c)
                    if has(g, 2):
                        keep_xT(g + 2, p)
                over_groups(act, step)

            @block.tensor
            def _(pe):
                mm = nc.tensor.matmul

                def transpose_x(g):
                    pe.wait_ge(xn_done, GB * g + GB)
                    if later(g, 1):
                        pe.wait_ge(xT_kept, g)
                    for b in range(GB):
                        last = nc.tensor.transpose(psX[:, b * S:(b + 1) * S], xn[:, b, :], P("ident"))
                    last.then_inc(xT_done, 1)

                def up(g, p, c):
                    if c == 0:
                        pe.wait_ge(xT_kept, g + 1)
                    if later(g, 1):
                        pe.wait_ge(gelu_done, FC * (g - 1) + c + 1)
                    mm(psU[c][:], P("W1T")[:, c * 128:(c + 1) * 128], xnT[p][:], start=True, stop=True).then_inc(up_done, 1)

                def down(g, p, b):
                    if b == 0:
                        pe.wait_ge(gelu_done, FC * g + FC)
                        if later(g, 2):
                            pe.wait_ge(x_done, g - 1)
                    for c in range(FC):
                        last = mm(psY[p][:, b * D:(b + 1) * D], hT[p][:, c, b * S:(b + 1) * S],
                                  P("W2T")[:, c * D:(c + 1) * D], start=c == 0, stop=c == FC - 1)
                    if b == GB - 1:
                        last.then_inc(down_done, 1)

                transpose_x(0)
                for c in range(FC):
                    up(0, 0, c)
                transpose_x(1)

                def step(g, p):
                    for k in range(FC):
                        if has(g, 1):
                            up(g + 1, 1 - p, k)
                        down(g, p, k)
                    if has(g, 2):
                        transpose_x(g + 2)
                over_groups(pe, step)


def attention1(nc, sem, ctxT, X, xg, P, halves, epsilons, passed, before, tokens, padding, rows, fill, out):
    with ExitStack() as stack:
        def sb(name, shape, dt=F32):
            return stack.enter_context(nc.sbuf_tensor(name, shape, dt))

        def ps(name, shape, dt=F32):
            return stack.enter_context(nc.psum_tensor(name, shape, dt))

        ctx = sb("c_ctx", [128, 2, GB, KEYS])
        bq = sb("c_bq", [128, 1])
        stats = sb("c_stats", [128, GB, 6])
        mv = sb("c_mv", [128, GB, 2])
        veps = sb("c_veps", [128, GB])
        rstd = sb("c_rstd", [128, GB])
        xn = sb("c_xn", [128, GB, D])
        xnT = sb("c_xnT", [128, GB * S])
        qT = sb("c_qT", [128, GB * S])
        kT = sb("c_kT", [128, GB, KEYS])
        v = [sb(f"c_v{p}", [KEYS, GB * D]) for p in range(2)]
        clipped = sb("c_clipped", [128, GB, KEYS])
        negmax = sb("c_negmax", [128, GB])
        probs = sb("c_probs", [128, GB, KEYS])
        den = sb("c_den", [128, GB])
        rden = sb("c_rden", [128, GB])
        probsT = sb("c_probsT", [KEYS, GB * S])
        stats2 = sb("c_stats2", [128, GB, 6])
        mv2 = sb("c_mv2", [128, GB, 2])
        veps2 = sb("c_veps2", [128, GB])
        rstd2 = sb("c_rstd2", [128, GB])
        drow = [[sb(f"c_drow{p}{j}", [128, GB, ROW]) for j in range(2)] for p in range(2)]
        earlier = sb("c_earlier", [128, 128], BF16)
        onesb = sb("c_onesb", [128, 128], BF16)
        number = sb("c_number", [128, B], I32)
        chosen = [sb(f"c_chosen{p}", [128, GB + 1, E], BF16) for p in range(2)]
        hots = [[sb(f"c_hot{p}{j}", [128, GB, E]) for j in range(2)] for p in range(2)]
        place = sb("c_place", [128, GB, E])
        picked = sb("c_picked", [128, 2, GB, E])
        slotf = sb("c_slotf", [128, 2, GB])
        slot = [sb(f"c_slot{p}", [128, 2, GB], U32) for p in range(2)]
        xn2T = sb("c_xn2T", [128, GB * S])
        logits = sb("c_logits", [128, GB, E])
        top = sb("c_top", [128, GB, 8])
        topi = sb("c_topi", [128, GB, 8], U32)
        topf = sb("c_topf", [128, GB, 8])
        gap = sb("c_gap", [128, GB])
        egap = sb("c_egap", [128, GB])
        egap1 = sb("c_egap1", [128, GB])

        psX = ps("c_psX", [128, 512])
        psQ = ps("c_psQ", [128, 512])
        psK = ps("c_psK", [128, 512])
        psV = ps("c_psV", [KEYS, 512])
        psS = ps("c_psS", [128, 512])
        psP = ps("c_psP", [KEYS, 512])
        psY = ps("c_psY", [128, 512])
        psL = ps("c_psL", [128, 512])
        psR = psL[:, 256:512]

        names = ("bq_done stats_done aggr_done veps_done rstd_done xn_done xT_done xT_kept q_done q_kept k_done k_kept "
                 "v_done v_kept s_done clip_done max_done exp_done rden_done pT_done pT_kept y_done x_done stats2_done "
                 "aggr2_done veps2_done rstd2_done xn2_done x2T_done x2T_kept l_done l_kept top_done topi_done topf_done "
                 "gap_done egap_done egap1_done w1_done w2_done hot_done chosen_done row_copied number_done setup rank_done place_done picked_done slotf_done slot_done fill_done x_kept consts_in setup2").split()
        (bq_done, stats_done, aggr_done, veps_done, rstd_done, xn_done, xT_done, xT_kept, q_done, q_kept, k_done,
         k_kept, v_done, v_kept, s_done, clip_done, max_done, exp_done, rden_done, pT_done, pT_kept, y_done, x_done,
         stats2_done, aggr2_done, veps2_done, rstd2_done, xn2_done, x2T_done, x2T_kept, l_done, l_kept, top_done,
         topi_done, topf_done, gap_done, egap_done, egap1_done, w1_done, w2_done, hot_done, chosen_done,
         row_copied, number_done, setup, rank_done, place_done, picked_done, slotf_done, slot_done, fill_done, x_kept,
         consts_in, setup2) = [sem("c_" + name) for name in names]
        ctx_in = [sem(f"c_ctx_in{p}") for p in range(2)]
        sent = [sem(f"c_sent{p}") for p in range(2)]

        def over_groups(eng, step):
            step(0, 0, True, False, False)
            step(1, 1, True, True, False)
            with eng.Fori(1, G // 2) as h:
                step(2 * h, 0, True, True, True)
                step(2 * h + 1, 1, True, True, True)
            step(G, 0, False, True, True)
            step(G + 1, 1, False, False, True)

        with nc.Block() as block:
            @block.sync
            def _(sp):
                def load(g, p, times):
                    if times is not None:
                        sp.wait_ge(ctx_in[p], 16 * times)
                        sp.wait_ge(v_done, g - 1)
                    sp.dma_start(ctx[:, p], ctxT[:, bass.ds(g * GB, GB), :]).then_inc(ctx_in[p], 16)

                def keep_x(g):
                    hold(sp, x_done, GB * g + GB, passed)
                    sp.dma_start(out[bass.ds(g * GB * S, GB * S)].rearrange("(b p) d -> p b d", p=128),
                                 xg(g)).then_inc(x_kept, 16)

                load(0, 0, None)
                load(1, 1, None)
                sp.dma_start(earlier[:], before).then_inc(consts_in, 16)
                sp.dma_start(number[:], tokens).then_inc(consts_in, 16)
                sp.dma_start(rows[SPARE:SPARE + TT], padding).then_inc(consts_in, 16)
                sp.dma_start(out[B * S:B * S + TT], padding[:, 0:D]).then_inc(consts_in, 16)
                with sp.Fori(1, G // 2) as h:
                    load(2 * h, 0, h)
                    load(2 * h + 1, 1, h)
                    keep_x(2 * h - 2)
                    keep_x(2 * h - 1)
                keep_x(G - 2)
                keep_x(G - 1)
                for p in range(2):
                    sp.wait_ge(ctx_in[p], 16 * (G // 2))
                sp.wait_ge(x_kept, 16 * G)
                sp.wait_ge(consts_in, 64)

            @block.gpsimd
            def _(pool):
                def step(g, p, here, last, older):
                    if here:
                        pool.wait_ge(aggr_done, GB * g + GB)
                        nc.gpsimd.tensor_tensor(veps[:], mv[:, :, 1], epsilons[:], ALU.add).then_inc(veps_done, 1)
                        pool.wait_ge(veps_done, g + 1)
                        nc.gpsimd.tensor_tensor(rstd[:], veps[:], halves[:], ALU.pow).then_inc(rstd_done, 1)
                    if last:
                        pool.wait_ge(aggr2_done, GB * g)
                        nc.gpsimd.tensor_tensor(veps2[:], mv2[:, :, 1], epsilons[:], ALU.add).then_inc(veps2_done, 1)
                        pool.wait_ge(veps2_done, g)
                        nc.gpsimd.tensor_tensor(rstd2[:], veps2[:], halves[:], ALU.pow).then_inc(rstd2_done, 1)
                    if older:
                        hold(pool, slot_done, g - 1, passed)
                        for b in range(GB):
                            for j in range(2):
                                nc.gpsimd.indirect_dma_start(
                                    rows, bass.IndirectOffsetOnAxis(ap=slot[p][:, j, b:b + 1], axis=0),
                                    drow[p][j][:, b, :], None).then_inc(sent[p], 16)
                pool.wait_ge(consts_in, 64)
                over_groups(pool, step)
                for p in range(2):
                    pool.wait_ge(sent[p], 16 * 2 * GB * G // 2)

            @block.vector
            def _(dve):
                nc.vector.tensor_scalar(bq[:], P("bq1"), SCALE, None, ALU.mult).then_inc(bq_done, 1)
                nc.vector.tensor_scalar(fill[:], P("eidx"), float(REGION), None, ALU.mult).then_inc(fill_done, 1)
                nc.vector.memset(onesb[:], 1.0).then_inc(setup, 1)
                for p in range(2):
                    nc.vector.memset(chosen[p][:, GB, :], 0.0).then_inc(setup, 1)
                dve.wait_ge(consts_in, 64)

                def stats_of(g):
                    for b in range(GB):
                        nc.vector.bn_stats(stats[:, b, :], xg(g, b)).then_inc(stats_done, 1)
                    hold(dve, stats_done, GB * g + GB, passed)
                    for b in range(GB):
                        nc.vector.bn_aggr(mv[:, b, :], stats[:, b, :]).then_inc(aggr_done, 1)

                def normalise(g):
                    dve.wait_ge(rstd_done, g + 1)
                    if later(g, 1):
                        dve.wait_ge(xT_done, g)
                    for b in range(GB):
                        nc.vector.tensor_scalar(xn[:, b, :], xg(g, b), mv[:, b, 0:1], rstd[:, b:b + 1],
                                                ALU.subtract, ALU.mult).then_inc(xn_done, 1)

                def finish_attention(g, p):
                    dve.wait_ge(exp_done, GB * g + GB)
                    nc.vector.reciprocal(rden[:], den[:]).then_inc(rden_done, 1)
                    dve.wait_ge(rden_done, g + 1)
                    dve.wait_ge(y_done, g + 1)
                    for b in range(GB):
                        nc.vector.scalar_tensor_tensor(xg(g, b), psY[:, b * D:(b + 1) * D], rden[:, b:b + 1], xg(g, b),
                                                       ALU.mult, ALU.add).then_inc(x_done, 1)

                def second_stats(g):
                    hold(dve, x_done, GB * g + GB, passed)
                    for b in range(GB):
                        nc.vector.bn_stats(stats2[:, b, :], xg(g, b)).then_inc(stats2_done, 1)
                    hold(dve, stats2_done, GB * g + GB, passed)
                    for b in range(GB):
                        nc.vector.bn_aggr(mv2[:, b, :], stats2[:, b, :]).then_inc(aggr2_done, 1)

                def second_normalise(g, p, reused):
                    dve.wait_ge(rstd2_done, g + 1)
                    if reused is not None:
                        dve.wait_ge(sent[p], 16 * 2 * GB * reused)
                    for j in range(2):
                        nc.vector.tensor_copy(drow[p][j][:, :, ROW - 1].bitcast(I32),
                                              number[:, bass.ds(g * GB, GB)]).then_inc(number_done, 1)
                    for b in range(GB):
                        nc.vector.tensor_scalar(drow[p][0][:, b, 0:D], xg(g, b), mv2[:, b, 0:1], rstd2[:, b:b + 1],
                                                ALU.subtract, ALU.mult).then_inc(xn2_done, 1)

                def route(g, p):
                    dve.wait_ge(l_done, g + 1)
                    nc.vector.tensor_copy(logits[:], psL[:, 0:GB * E].rearrange("p (b e) -> p b e", e=E)).then_inc(l_kept, 1)
                    hold(dve, l_kept, g + 1, passed)
                    for b in range(GB):
                        nc.vector.max(top[:, b, :], logits[:, b, :]).then_inc(top_done, 1)
                    hold(dve, top_done, GB * g + GB, passed)
                    for b in range(GB):
                        nc.vector.max_index(topi[:, b, :], top[:, b, :], logits[:, b, :]).then_inc(topi_done, 1)
                    nc.vector.tensor_tensor(gap[:], top[:, :, 1], top[:, :, 0], ALU.subtract).then_inc(gap_done, 1)
                    dve.wait_ge(topi_done, GB * g + GB)
                    nc.vector.tensor_copy(topf[:], topi[:]).then_inc(topf_done, 1)
                    dve.wait_ge(topf_done, g + 1)
                    for j in range(2):
                        nc.vector.tensor_tensor(hots[p][j][:], P("eidx").unsqueeze(1).to_broadcast([128, GB, E]),
                                                topf[:, :, j:j + 1].to_broadcast([128, GB, E]),
                                                ALU.is_equal).then_inc(hot_done, 1)
                    dve.wait_ge(hot_done, 2 * g + 2)
                    nc.vector.tensor_tensor(chosen[p][:, 0:GB, :], hots[p][0][:], hots[p][1][:],
                                            ALU.add).then_inc(chosen_done, 1)
                    dve.wait_ge(egap_done, g + 1)
                    nc.vector.tensor_scalar(egap1[:], egap[:], 1.0, None, ALU.add).then_inc(egap1_done, 1)
                    dve.wait_ge(egap1_done, g + 1)
                    nc.vector.reciprocal(drow[p][0][:, :, D], egap1[:]).then_inc(w1_done, 1)
                    dve.wait_ge(w1_done, g + 1)
                    nc.vector.tensor_tensor(drow[p][1][:, :, D], drow[p][0][:, :, D], egap[:], ALU.mult).then_inc(w2_done, 1)

                def find_places(g, p):
                    dve.wait_ge(rank_done, g + 1)
                    dve.wait_ge(fill_done, g + 1)
                    ranks = psR[:, 0:(GB + 1) * E].rearrange("p (b e) -> p b e", e=E)
                    nc.vector.tensor_tensor(place[:], ranks[:, 0:GB, :], fill[:].unsqueeze(1).to_broadcast([128, GB, E]),
                                            ALU.add).then_inc(place_done, 1)
                    dve.wait_ge(place_done, g + 1)
                    nc.vector.tensor_tensor(fill[:], fill[:], ranks[:, GB, :], ALU.add).then_inc(fill_done, 1)
                    for j in range(2):
                        nc.vector.tensor_tensor(picked[:, j], place[:], hots[p][j][:], ALU.mult).then_inc(picked_done, 1)
                    dve.wait_ge(picked_done, 2 * g + 2)
                    nc.vector.tensor_reduce(slotf[:], picked[:], AX_X, ALU.add).then_inc(slotf_done, 1)
                    dve.wait_ge(slotf_done, g + 1)
                    dve.wait_ge(row_copied, g + 1)
                    dve.wait_ge(w2_done, g + 1)
                    nc.vector.tensor_copy(slot[p][:], slotf[:]).then_inc(slot_done, 1)

                def step(g, p, here, last, older):
                    if here:
                        stats_of(g)
                    if older:
                        find_places(g - 2, p)
                    if last:
                        finish_attention(g - 1, 1 - p)
                    if here:
                        normalise(g)
                    if last:
                        second_stats(g - 1)
                    if here:
                        dve.wait_ge(k_done, g + 1)
                        nc.vector.tensor_scalar(kT[:], psK[:, 0:GB * KEYS].rearrange("p (b k) -> p b k", k=KEYS), P("bk1"),
                                                None, ALU.add).then_inc(k_kept, 1)
                        dve.wait_ge(v_done, g + 1)
                        nc.vector.tensor_tensor(v[p][:].rearrange("k (b d) -> k b d", d=D),
                                                psV[:].rearrange("k (b d) -> k b d", d=D),
                                                P("bv1")[0:KEYS, :].unsqueeze(1).to_broadcast([KEYS, GB, D]),
                                                ALU.add).then_inc(v_kept, 1)
                    if last:
                        second_normalise(g - 1, 1 - p, reused_of(g, p))
                    if here:
                        dve.wait_ge(s_done, g + 1)
                        nc.vector.tensor_scalar(clipped[:], psS[:, 0:GB * KEYS].rearrange("p (b k) -> p b k", k=KEYS),
                                                100.0, -100.0, ALU.min, ALU.max).then_inc(clip_done, 1)
                        dve.wait_ge(clip_done, g + 1)
                        nc.vector.tensor_reduce(negmax[:], clipped[:], AX_X, ALU.max, negate=True).then_inc(max_done, 1)
                    if last:
                        route(g - 1, 1 - p)

                loop = [None]

                def reused_of(g, p):
                    if type(g) is int:
                        return (g - 1) // 2 or None
                    return loop[0] - 1 + p

                step(0, 0, True, False, False)
                step(1, 1, True, True, False)
                step(2, 0, True, True, True)
                step(3, 1, True, True, True)
                with dve.Fori(2, G // 2) as h:
                    loop[0] = h
                    step(2 * h, 0, True, True, True)
                    step(2 * h + 1, 1, True, True, True)
                step(G, 0, False, True, True)
                step(G + 1, 1, False, False, True)
                dve.wait_ge(fill_done, G + 1)

            @block.scalar
            def _(act):
                act.wait_ge(bq_done, 1)

                def step(g, p, here, last, older):
                    if here:
                        act.wait_ge(xT_done, g + 1)
                        nc.scalar.copy(xnT[:], psX[:]).then_inc(xT_kept, 1)
                        act.wait_ge(q_done, g + 1)
                        nc.scalar.activation(qT[:], psQ[:], ACT.Identity, bias=bq[:], scale=SCALE).then_inc(q_kept, 1)
                    if last:
                        act.wait_ge(x2T_done, g)
                        nc.scalar.copy(xn2T[:], psX[:]).then_inc(x2T_kept, 1)
                        nc.scalar.copy(drow[1 - p][1][:, :, 0:D], drow[1 - p][0][:, :, 0:D]).then_inc(row_copied, 1)
                    if here:
                        act.wait_ge(max_done, g + 1)
                        for b in range(GB):
                            nc.scalar.activation(probs[:, b, :], clipped[:, b, :], ACT.Exp, bias=negmax[:, b:b + 1],
                                                 accum_out=den[:, b:b + 1]).then_inc(exp_done, 1)
                    if last:
                        act.wait_ge(gap_done, g)
                        nc.scalar.activation(egap[:], gap[:], ACT.Exp).then_inc(egap_done, 1)
                    if here:
                        act.wait_ge(pT_done, g + 1)
                        nc.scalar.copy(probsT[:], psP[:]).then_inc(pT_kept, 1)
                over_groups(act, step)
                act.wait_ge(row_copied, G)

            @block.tensor
            def _(pe):
                mm = nc.tensor.matmul

                def step(g, p, here, last, older):
                    if older:
                        pe.wait_ge(chosen_done, g - 1)
                        pe.wait_ge(l_kept, g - 1)
                        many = chosen[p]
                        mm(psR[:, 0:(GB + 1) * E], earlier[:], many[:], start=True, stop=False, skip_group_check=True)
                        for b in range(GB):
                            last_mm = mm(psR[:, (b + 1) * E:(GB + 1) * E].rearrange("p (b e) -> p b e", e=E), onesb[:],
                                         many[:, b:b + 1, :].to_broadcast([128, GB - b, E]), start=False,
                                         stop=b == GB - 1, skip_group_check=True)
                        last_mm.then_inc(rank_done, 1)
                    if last:
                        pe.wait_ge(pT_kept, g)
                        pe.wait_ge(v_kept, g)
                        for b in range(GB):
                            done = mm(psY[:, b * D:(b + 1) * D], probsT[:, b * S:(b + 1) * S],
                                      v[1 - p][:, b * D:(b + 1) * D], start=True, stop=True)
                        done.then_inc(y_done, 1)
                    if here:
                        pe.wait_ge(xn_done, GB * g + GB)
                        if last:
                            if later(g, 2):
                                pe.wait_ge(x2T_kept, g - 1)
                        for b in range(GB):
                            done = nc.tensor.transpose(psX[:, b * S:(b + 1) * S], xn[:, b, :], P("ident"))
                        done.then_inc(xT_done, 1)
                        pe.wait_ge(ctx_in[p], 16 * (half_of(g, p) + 1))
                        if last:
                            pe.wait_ge(k_kept, g)
                            pe.wait_ge(v_kept, g)
                        mm(psK[:, 0:GB * KEYS], P("Wk1"), ctx[:, p], start=True, stop=True).then_inc(k_done, 1)
                        for b in range(GB):
                            done = mm(psV[:, b * D:(b + 1) * D], ctx[:, p, b, :], P("Wv1"), start=True, stop=True)
                        done.then_inc(v_done, 1)
                        pe.wait_ge(xT_kept, g + 1)
                        mm(psQ[:], P("Wq1"), xnT[:], start=True, stop=True).then_inc(q_done, 1)
                    if last:
                        pe.wait_ge(xn2_done, GB * g)
                        if here:
                            pe.wait_ge(xT_kept, g + 1)
                        for b in range(GB):
                            done = nc.tensor.transpose(psX[:, b * S:(b + 1) * S], drow[1 - p][0][:, b, 0:D], P("ident"))
                        done.then_inc(x2T_done, 1)
                    if here:
                        pe.wait_ge(q_kept, g + 1)
                        pe.wait_ge(k_kept, g + 1)
                        if last:
                            pe.wait_ge(clip_done, g)
                        for b in range(GB):
                            done = mm(psS[:, b * KEYS:(b + 1) * KEYS], qT[:, b * S:(b + 1) * S], kT[:, b, :],
                                      start=True, stop=True)
                        done.then_inc(s_done, 1)
                    if last:
                        pe.wait_ge(x2T_kept, g)
                        if later(g, 2):
                            pe.wait_ge(l_kept, g - 1)
                        if older:
                            pe.wait_ge(fill_done, g)
                        for b in range(GB):
                            done = mm(psL[:, b * E:(b + 1) * E], xn2T[:, b * S:(b + 1) * S], P("router"),
                                      start=True, stop=True)
                        done.then_inc(l_done, 1)
                    if here:
                        pe.wait_ge(exp_done, GB * g + GB)
                        for b in range(GB):
                            done = nc.tensor.transpose(psP[:, b * S:(b + 1) * S], probs[:, b, :], P("ident"))
                        done.then_inc(pT_done, 1)

                def half_of(g, p):
                    return halfg[0] if type(g) is not int else g // 2

                halfg = [None]
                step(0, 0, True, False, False)
                step(1, 1, True, True, False)
                pe.wait_ge(consts_in, 64)
                pe.wait_ge(setup, 3)
                with pe.Fori(1, G // 2) as h:
                    halfg[0] = h
                    step(2 * h, 0, True, True, True)
                    step(2 * h + 1, 1, True, True, True)
                step(G, 0, False, True, True)
                step(G + 1, 1, False, False, True)


def experts(nc, sem, P, passed, weights, padding, rows, fill, out):
    with ExitStack() as stack:
        def sb(name, shape, dt=F32):
            return stack.enter_context(nc.sbuf_tensor(name, shape, dt))

        def ps(name, shape, dt=F32):
            return stack.enter_context(nc.psum_tensor(name, shape, dt))

        start_row = nc.dram_tensor("start_row", (128, 2), I32, kind="Internal").ap()
        first = sb("d_first", [128, E])
        filled = sb("d_filled", [128, E])
        over = sb("d_over", [128, E, KMAX])
        ntiles = sb("d_ntiles", [128, E])
        ones = sb("d_ones", [128, E])
        ends = sb("d_ends", [128, E])
        begins = sb("d_begins", [128, E])
        past = sb("d_past", [128, E])
        begun = sb("d_begun", [128, E])
        cand = sb("d_cand", [128, E])
        entry = sb("d_entry", [128, 2])
        spare = sb("d_spare", [128, 1])
        filli = sb("d_filli", [128, E], I32)
        entryi = sb("d_entryi", [128, 2], I32)
        table = sb("d_table", [1, 2 * 128], I32)
        w = [sb(f"d_w{p}", [128, WCOLS]) for p in range(4)]
        xt = [sb(f"d_xt{p}", [128, TB, ROW]) for p in range(4)]
        xT = [sb(f"d_xT{p}", [128, TT]) for p in range(2)]
        hT = [sb(f"d_hT{p}", [128, FC, TT]) for p in range(2)]
        yb = sb("d_yb", [128, TB, D])
        y = [sb(f"d_y{p}", [128, TB, D]) for p in range(2)]
        psX = ps("d_psX", [128, 512])
        psU = [ps(f"d_psU{c}", [128, 512]) for c in range(FC)]
        psY = [ps(f"d_psY{p}", [128, 512]) for p in range(2)]

        t_step = sem("d_t_step")
        table_out = sem("d_table_out")
        table_in = sem("d_table_in")
        padded = sem("d_padded")

        with nc.Block() as block:
            @block.vector
            def _(dve):
                n = [0]

                def do(ins):
                    n[0] += 1
                    ins.then_inc(t_step, 1)
                    dve.wait_ge(t_step, n[0])

                v = nc.vector
                do(v.tensor_copy(filli[:], fill[:]))
                do(v.tensor_scalar(first[:], P("eidx"), float(REGION), None, ALU.mult))
                do(v.tensor_tensor(filled[:], fill[:], first[:], ALU.subtract))
                do(v.tensor_tensor(over[:], filled[:].unsqueeze(2).to_broadcast([128, E, KMAX]),
                                   P("steps").unsqueeze(1).to_broadcast([128, E, KMAX]), ALU.is_gt))
                do(v.tensor_reduce(ntiles[:], over[:], AX_X, ALU.add))
                do(v.memset(ones[:], 1.0))
                do(v.tensor_tensor_scan(ends[:], ones[:], ntiles[:], 0.0, ALU.mult, ALU.add))
                do(v.tensor_tensor(begins[:], ends[:], ntiles[:], ALU.subtract))
                do(v.tensor_scalar(past[:], ends[:], P("part"), None, ALU.is_le))
                do(v.tensor_scalar(begun[:], begins[:], P("part"), None, ALU.is_le))
                do(v.tensor_reduce(entry[:, 0:1], past[:], AX_X, ALU.add))
                do(v.tensor_scalar(entry[:, 0:1], entry[:, 0:1], float(E - 1), None, ALU.min))
                do(v.tensor_tensor(begun[:], begun[:], past[:], ALU.subtract))
                do(v.tensor_scalar(cand[:], begins[:], P("part"), -float(TT), ALU.subtract, ALU.mult))
                do(v.tensor_tensor(cand[:], cand[:], first[:], ALU.add))
                do(v.tensor_tensor(cand[:], cand[:], begun[:], ALU.mult))
                do(v.tensor_reduce(entry[:, 1:2], cand[:], AX_X, ALU.add))
                do(v.tensor_scalar(spare[:], past[:, E - 1:E], float(SPARE), None, ALU.mult))
                do(v.tensor_tensor(entry[:, 1:2], entry[:, 1:2], spare[:], ALU.add))
                do(v.tensor_copy(entryi[:], entry[:]))

            @block.sync
            def _(sp):
                sp.wait_ge(t_step, 20)
                sp.dma_start(start_row, entryi[:]).then_inc(table_out, 16)
                sp.wait_ge(table_out, 16)
                sp.dma_start(table[:], start_row.rearrange("t c -> (t c)").unsqueeze(0)).then_inc(table_in, 16)
                for e in range(E):
                    row = sp.value_load(filli[0:1, e:e + 1], min_val=e * REGION, max_val=e * REGION + B * S)
                    sp.dma_start(rows[bass.ds(row, TT)], padding).then_inc(padded, 16)
                sp.wait_ge(table_in, 16)
                sp.wait_ge(padded, 16 * E)

        w_in = [sem(f"d_w_in{p}") for p in range(4)]
        rows_in = [sem(f"d_rows_in{p}") for p in range(4)]
        xT_done = sem("d_xT_done")
        xT_kept = sem("d_xT_kept")
        up_done = sem("d_up_done")
        gelu_done = sem("d_gelu_done")
        down_done = sem("d_down_done")
        yb_done = sem("d_yb_done")
        y_done = sem("d_y_done")
        added = sem("d_added")

        def over_tiles(eng, step):
            for t in range(4):
                step(t, t)
            with eng.Fori(1, TILES // 4 - 1) as q:
                for k in range(4):
                    step(4 * q + k, k)
            for k in range(4):
                step(TILES - 4 + k, k)

        def has(t, ahead):
            return type(t) is not int or t + ahead < TILES

        with nc.Block() as block:
            @block.sync
            def _(sp):
                def load(q, t, k, first):
                    expert = sp.value_load(table[0:1, bass.ds(2 * t, 1)], min_val=0, max_val=E - 1)
                    row = sp.value_load(table[0:1, bass.ds(2 * t + 1, 1)], min_val=0, max_val=SPARE)
                    if not first:
                        hold(sp, yb_done, t - 3, passed)
                        hold(sp, w_in[k], 16 * q, passed)
                    sp.dma_start(w[k][:], weights[bass.ds(expert, 1)].rearrange("e p c -> (e p) c")).then_inc(w_in[k], 16)
                    if not first:
                        hold(sp, rows_in[k], 16 * q, passed)
                        hold(sp, added, 32 * (t - 3), passed)
                    sp.dma_start(xt[k][:], rows[bass.ds(row, TT)].rearrange("(j p) c -> p j c", p=128)).then_inc(rows_in[k], 16)

                for k in range(4):
                    load(0, k, k, True)
                with sp.Fori(1, TILES // 4) as q:
                    for k in range(4):
                        load(q, 4 * q + k, k, False)

            @block.gpsimd
            def _(pool):
                def step(t, k):
                    hold(pool, y_done, TB * t + TB, passed)
                    if later(t, 1):
                        hold(pool, added, 32 * t, passed)
                    for j in range(TB):
                        nc.gpsimd.indirect_dma_start(
                            out, bass.IndirectOffsetOnAxis(ap=xt[k][:, j, ROW - 1:ROW].bitcast(U32), axis=0),
                            y[k % 2][:, j, :], None, compute_op=ALU.add).then_inc(added, 16)
                over_tiles(pool, step)
                pool.wait_ge(added, 32 * TILES)

            @block.vector
            def _(dve):
                def step(t, k):
                    dve.wait_ge(down_done, t + 1)
                    if later(t, 1):
                        dve.wait_ge(y_done, TB * t)
                    nc.vector.tensor_tensor(yb[:], psY[k % 2][:, 0:TT].rearrange("p (j d) -> p j d", d=D),
                                            w[k][:, WCOLS - D:].unsqueeze(1).to_broadcast([128, TB, D]),
                                            ALU.add).then_inc(yb_done, 1)
                    dve.wait_ge(yb_done, t + 1)
                    if later(t, 2):
                        dve.wait_ge(added, 32 * (t - 1))
                    for j in range(TB):
                        nc.vector.tensor_scalar(y[k % 2][:, j, :], yb[:, j, :], xt[k][:, j, D:D + 1], None,
                                                ALU.mult).then_inc(y_done, 1)
                over_tiles(dve, step)

            @block.scalar
            def _(act):
                def keep_xT(t, k):
                    act.wait_ge(xT_done, t + 1)
                    if later(t, 2):
                        act.wait_ge(up_done, FC * (t - 1))
                    nc.scalar.copy(xT[k % 2][:], psX[:, 0:TT]).then_inc(xT_kept, 1)

                def gelu(t, k, c):
                    act.wait_ge(up_done, FC * t + c + 1)
                    if later(t, 2) and c == 0:
                        act.wait_ge(down_done, t - 1)
                    nc.scalar.activation(hT[k % 2][:, c, :], psU[c][:, 0:TT], ACT.Gelu,
                                         bias=w[k][:, 2 * FF + c:2 * FF + c + 1]).then_inc(gelu_done, 1)

                keep_xT(0, 0)
                for c in range(FC):
                    gelu(0, 0, c)
                keep_xT(1, 1)

                def step(t, k):
                    if has(t, 1):
                        for c in range(FC):
                            gelu(t + 1, (k + 1) % 4, c)
                    if has(t, 2):
                        keep_xT(t + 2, k)
                over_tiles(act, step)

            @block.tensor
            def _(pe):
                mm = nc.tensor.matmul

                def times(t, k, ahead):
                    if type(t) is int:
                        return 16 * ((t + ahead) // 4 + 1)
                    return 16 * (loop[0] + (k + ahead) // 4 + 1)

                def transpose_x(t, k, ahead):
                    pe.wait_ge(rows_in[(k + ahead) % 4], times(t, k, ahead))
                    if later(t + ahead, 1):
                        pe.wait_ge(xT_kept, t + ahead)
                    for j in range(TB):
                        done = nc.tensor.transpose(psX[:, j * 128:(j + 1) * 128], xt[(k + ahead) % 4][:, j, 0:D], P("ident"))
                    done.then_inc(xT_done, 1)

                def up(t, k, c, ahead):
                    if c == 0:
                        pe.wait_ge(xT_kept, t + ahead + 1)
                        pe.wait_ge(w_in[(k + ahead) % 4], times(t, k, ahead))
                    if later(t + ahead, 1):
                        pe.wait_ge(gelu_done, FC * (t + ahead - 1) + c + 1)
                    mm(psU[c][:, 0:TT], w[(k + ahead) % 4][:, c * 128:(c + 1) * 128], xT[(k + ahead) % 2][:],
                       start=True, stop=True).then_inc(up_done, 1)

                def down(t, k, j):
                    if j == 0:
                        pe.wait_ge(gelu_done, FC * t + FC)
                        if later(t, 2):
                            pe.wait_ge(yb_done, t - 1)
                    for c in range(FC):
                        done = mm(psY[k % 2][:, j * D:(j + 1) * D], hT[k % 2][:, c, j * 128:(j + 1) * 128],
                                  w[k][:, FF + c * D:FF + (c + 1) * D], start=c == 0, stop=c == FC - 1)
                    if j == TB - 1:
                        done.then_inc(down_done, 1)

                loop = [None]
                transpose_x(0, 0, 0)
                for c in range(FC):
                    up(0, 0, c, 0)
                transpose_x(0, 0, 1)

                def step(t, k):
                    for j in range(TB):
                        if has(t, 1):
                            up(t, k, 2 * j, 1)
                            up(t, k, 2 * j + 1, 1)
                        down(t, k, j)
                    if has(t, 2):
                        transpose_x(t, k, 2)
                for t in range(4):
                    step(t, t)
                with pe.Fori(1, TILES // 4 - 1) as q:
                    loop[0] = q
                    for k in range(4):
                        step(4 * q + k, k)
                for k in range(4):
                    step(TILES - 4 + k, k)


def host_consts():
    f = np.arange(CH)[None, :] * 128 + np.arange(128)[:, None]
    head = f // KEYS
    vm = np.zeros((128, CH, SLOTS), np.float32)
    for c in range(CH):
        for slot in range(SLOTS):
            if first_head(c) + slot < HH:
                vm[:, c, slot] = head[:, c] == first_head(c) + slot
    rowsel = np.zeros((128, CH, 128), np.float32)
    rowsel[:KEYS] = (f.T % KEYS)[None] == np.arange(KEYS)[:, None, None]
    km = ((np.arange(128)[:, None] // DH) % HH == np.arange(HH)[None, :]).astype(np.float32)
    sel = (np.arange(FLAT)[None, :] // KEYS == np.arange(HH)[:, None]).astype(np.float32)
    return vm.reshape(128, -1), rowsel.reshape(128, -1), km, sel


def kernel(x, ctx_1024, L0_xattn_Wq, L0_xattn_bq, L0_xattn_Wk, L0_xattn_bk, L0_xattn_Wv, L0_xattn_bv, L0_xattn_Wo,
           L0_xattn_bo, L0_ffn_W1, L0_ffn_b1, L0_ffn_W2, L0_ffn_b2, L1_xattn_Wq, L1_xattn_bq, L1_xattn_Wk,
           L1_xattn_bk, L1_xattn_Wv, L1_xattn_bv, L1_ffn_w_up, L1_ffn_w_down, L1_ffn_b_up, L1_ffn_b_down,
           L1_ffn_w_router, _phases="ABCD", _raw=False):
    import ml_dtypes
    import concourse.bacc as _bacc
    from concourse import mybir as _mybir
    from concourse.bass_utils import run_bass_kernel_spmd as _run

    def f(a):
        return np.asarray(a)

    vm, rowsel, km, sel = host_consts()
    col = lambda v: f(v).reshape(-1, 128).T
    rows = lambda v: np.broadcast_to(f(v)[None, :], (128, f(v).shape[0]))
    cols = {
        "Wq0": f(L0_xattn_Wq), "Wk0": f(L0_xattn_Wk),
        "Wv0": f(L0_xattn_Wv), "Wo0": f(L0_xattn_Wo),
        "W1T": f(L0_ffn_W1).T, "W2T": f(L0_ffn_W2).T.reshape(FC, 128, D).transpose(1, 0, 2).reshape(128, FF),
        "Wq1": f(L1_xattn_Wq), "Wk1": f(L1_xattn_Wk), "Wv1": f(L1_xattn_Wv), "router": f(L1_ffn_w_router).T,
        "bq0": col(L0_xattn_bq), "bk0": col(L0_xattn_bk), "bv0": col(L0_xattn_bv), "b1": col(L0_ffn_b1),
        "bq1": col(L1_xattn_bq), "bk1": col(L1_xattn_bk), "ident": np.eye(128, dtype=np.float32),
        "kmask": km, "vmask": vm, "rowsel": rowsel, "ones": np.ones((128, 128), np.float32), "bo0": rows(L0_xattn_bo),
        "b2": rows(L0_ffn_b2), "bv1": rows(L1_xattn_bv),
        "eidx": rows(np.arange(E, dtype=np.float32)),
        "steps": rows(np.arange(KMAX, dtype=np.float32) * TT), "part": np.arange(128, dtype=np.float32)[:, None],
    }
    pack = np.concatenate([cols[n].reshape(128, PACK[n][1]) for n in PACK], 1)
    padding = np.zeros((TT, ROW), np.float32)
    padding[:, ROW - 1] = (B * S + np.arange(TT, dtype=np.int32)).view(np.float32)
    ctxT = f(ctx_1024).transpose(2, 0, 1)
    arrays = {
        "x_in": f(x), "ctxT": ctxT, "pack": pack,
        "sel": sel.astype(ml_dtypes.bfloat16), "identb": np.eye(128).astype(ml_dtypes.bfloat16),
        "weights": np.concatenate([
            f(L1_ffn_w_up).transpose(0, 2, 1),
            f(L1_ffn_w_down).transpose(0, 2, 1).reshape(E, FC, 128, D).transpose(0, 2, 1, 3).reshape(E, 128, FF),
            f(L1_ffn_b_up).reshape(E, FC, 128).transpose(0, 2, 1),
            np.broadcast_to(f(L1_ffn_b_down)[:, None, :], (E, 128, D))], 2),
        "before": (np.arange(128)[:, None] < np.arange(128)[None, :]).astype(ml_dtypes.bfloat16),
        "tokens": (np.arange(B)[None, :] * S + np.arange(128)[:, None]).astype(np.int32),
        "padding": padding,
    }
    arrays = {k: np.ascontiguousarray(v) for k, v in arrays.items()}
    nc = _bacc.Bacc("TRN2", target_bir_lowering=False, num_devices=1)
    aps = [nc.dram_tensor(k, v.shape, _mybir.dt.from_np(v.dtype), kind="ExternalInput").ap() for k, v in arrays.items()]
    out = nc.dram_tensor("out", (B * S + TT, D), F32, kind="ExternalOutput").ap()
    build(nc, *aps, out, phases=_phases)
    if _raw:
        return nc, arrays
    r = _run(nc, [arrays], core_ids=[0])
    return r.results[0]["out"][:B * S].reshape(B, S, D)
```

```python
from contextlib import ExitStack

import numpy as np
import concourse.bass as bass
from concourse import mybir

F32 = mybir.dt.float32
F32R = mybir.dt.float32r
BF16 = mybir.dt.bfloat16
U32 = mybir.dt.uint32
I32 = mybir.dt.int32
ALU = mybir.AluOpType
ACT = mybir.ActivationFunctionType
AX_X = mybir.AxisListType.X

B, S, D = 64, 128, 128
KEYS = 77
HEADS, DH = 16, 8
FF = 512
E = 8
GB = 4
G = B // GB
HH = HEADS // 2
CH = 5
UNITS = 2 * GB
FLAT = CH * 128
SLOTS = 3
FC = FF // 128
EPS = 1e-5
ROW = D + 2
TT = 256
TB = TT // 128
TILES = (2 * B * S + E * (TT - 1)) // TT // 2 * 2 + 2
REGION = B * S + TT
SPARE = E * REGION
COLUMNS = 4
KMAX = B * S // TT
WCOLS = 2 * FF + FC + D
HIGH = 0xFFFFF000
SCALE = 1.0 / float(np.sqrt(np.float32(128.0)))


def hold(engine, sem, value, passed):
    engine.wait_ge(sem, value)
    engine.sem_inc(passed)


def later(n, least):
    return type(n) is not int or n >= least


def first_head(c):
    return c * 128 // KEYS


PACK = {}
_at = 0
for _name, _n in (("Wq0", D), ("Wk0", D), ("Wv0", D), ("Wo0", D), ("bq0", 1), ("bk0", 1), ("bv0", 1), ("bo0", D),
                  ("ident", 128), ("kmask", HH), ("vmask", CH * SLOTS), ("rowsel", CH * 128),
                  ("W1T", FF), ("W2T", FF), ("Wq1", D), ("Wk1", D), ("Wv1", D), ("router", E), ("b1", FC), ("bq1", 1),
                  ("bk1", 1), ("ones", 128), ("b2", D), ("bv1", D), ("eidx", E), ("steps", KMAX), ("part", 1)):
    PACK[_name] = (_at, _n)
    _at += _n
PACK_COLS = _at
FIRST_COLS = PACK["W1T"][0]


def build(nc, x, ctxT, pack, weights, before, tokens, padding, out):
    with ExitStack() as stack:
        def sb(name, shape, dt=F32):
            return stack.enter_context(nc.sbuf_tensor(name, shape, dt))

        def sem(name):
            return stack.enter_context(nc.semaphore(name))

        X = sb("X", [128, B, D])
        par = sb("par", [128, PACK_COLS])

        def P(name):
            at, n = PACK[name]
            return par[:, at:at + n]

        halves = sb("halves", [128, 4 * GB])
        epsilons = sb("epsilons", [128, 4 * GB])
        passed = sem("passed")

        def xg(g, b=None):
            if b is None:
                return X[:, bass.ds(g * GB, GB), :]
            return X[:, bass.ds(g * GB + b, 1), :].rearrange("p a d -> p (a d)")

        W1r = sb("W1r", [128, FF], F32R)
        attention0(nc, sem, x, ctxT, X, xg, pack, par, P, halves, epsilons, passed, W1r)
        W = sb("W", [128, E, WCOLS])
        feed_forward0(nc, sem, X, xg, P, halves, epsilons, passed, weights, W, W1r)
        rows = nc.dram_tensor("rows", (SPARE + TT, ROW), F32, kind="Internal").ap()
        table = sb("table", [1, COLUMNS * 128], I32)
        attention1(nc, sem, ctxT, X, xg, P, halves, epsilons, passed, before, tokens, padding, rows, table, out)
        experts(nc, sem, P, passed, W, table, padding, rows, out)


def attention0(nc, sem, x, ctxT, X, xg, pack, par, P, halves, epsilons, passed, W1r):
    with ExitStack() as stack:
        def sb(name, shape, dt=F32):
            return stack.enter_context(nc.sbuf_tensor(name, shape, dt))

        def ps(name, shape, dt=F32):
            return stack.enter_context(nc.psum_tensor(name, shape, dt))

        ctx = sb("a_ctx", [128, 2, GB, KEYS])
        stats = sb("a_stats", [128, GB, 6])
        mv = sb("a_mv", [128, GB, 2])
        veps = sb("a_veps", [128, GB])
        rstd = sb("a_rstd", [128, GB])
        xn = sb("a_xn", [128, GB, D])
        xnT = sb("a_xnT", [128, GB * S])
        qT = sb("a_qT", [128, 2, GB * S])
        qcut = sb("a_qcut", [128, 2, GB * S])
        qh = [[sb(f"a_qh{p}{a}", [128, GB * S], F32R) for a in range(2)] for p in range(2)]
        ql = [[sb(f"a_ql{p}{a}", [128, GB * S], F32R) for a in range(2)] for p in range(2)]
        kT = sb("a_kT", [128, 2, GB, KEYS])
        kparts = sb("a_kparts", [128, 2, GB, KEYS])
        kbd = [sb(f"a_kbd{p}", [128, GB, 2, HH * KEYS], F32R) for p in range(2)]
        vals = sb("a_vals", [KEYS, GB, D + DH])
        vx = [sb(f"a_vx{p}", [128, CH, GB * 2, 128]) for p in range(2)]
        most = sb("a_most", [128, HH])
        shifted = [sb(f"a_shifted{p}", [128, HH * KEYS]) for p in range(2)]
        probs = [sb(f"a_probs{p}", [128, FLAT]) for p in range(2)]
        probsT = [sb(f"a_probsT{p}", [128, FLAT]) for p in range(2)]
        rden = sb("a_rden", [128, 2, HH])
        o = sb("a_o", [128, GB, D])
        oT = sb("a_oT", [128, GB * S])

        absum = sb("a_absum", [128, 2])
        half_mean = sb("a_half_mean", [128, 2])
        minus_half = sb("a_minus_half", [128, 2])
        above = [sb(f"a_above{j}", [128, FF]) for j in range(2)]
        below = [sb(f"a_below{j}", [128, FF]) for j in range(2)]
        absum_done = sem("a_absum_done")
        summed = sem("a_summed")
        half_done = sem("a_half_done")
        marks_done = sem("a_marks_done")
        ternary_done = sem("a_ternary_done")
        psS = ps("a_psS", [128, 2, 512])
        psT = [ps(f"a_psT{p}", [128, 1024]) for p in range(2)]
        psO = ps("a_psO", [128, 512])
        psM = ps("a_psM", [128, 512])

        half_rows = [slice(0, D // 2), slice(D // 2, D)]
        early = (psT[0][:, 512:1024], psT[1][:, 512:1024], psO)

        x_in = [sem(f"a_x_in{p}") for p in range(2)]
        ctx_in = [sem(f"a_ctx_in{p}") for p in range(2)]
        params_in = sem("a_params_in")
        later_params_in = sem("a_later_params_in")
        consts = sem("a_consts")
        vx_clear = sem("a_vx_clear")
        ones_set = sem("a_ones_set")
        vals_done = sem("a_vals_done")
        vals_kept = sem("a_vals_kept")
        stats_done = sem("a_stats_done")
        aggr_done = sem("a_aggr_done")
        veps_done = sem("a_veps_done")
        rstd_done = sem("a_rstd_done")
        xn_done = sem("a_xn_done")
        bo_added = sem("a_bo_added")
        xT_done = sem("a_xT_done")
        xT_kept = sem("a_xT_kept")
        q_done = sem("a_q_done")
        q_kept = sem("a_q_kept")
        k_done = sem("a_k_done")
        k_kept = sem("a_k_kept")
        k_twice = sem("a_k_twice")
        q_twice = sem("a_q_twice")
        kcut_done = sem("a_kcut_done")
        kparts_done = sem("a_kparts_done")
        qcut_done = sem("a_qcut_done")
        qh_done = sem("a_qh_done")
        ql_done = sem("a_ql_done")
        kbd_done = sem("a_kbd_done")
        v_done = sem("a_v_done")
        v_kept = sem("a_v_kept")
        s_done = sem("a_s_done")
        max_done = sem("a_max_done")
        shift_done = sem("a_shift_done")
        pT_done = sem("a_pT_done")
        pT_kept = sem("a_pT_kept")
        exp_done = sem("a_exp_done")
        pv_done = sem("a_pv_done")
        rden_done = sem("a_rden_done")
        o_done = sem("a_o_done")
        oT_done = sem("a_oT_done")
        oT_kept = sem("a_oT_kept")
        wo_done = sem("a_wo_done")
        x_done = sem("a_x_done")

        def over_groups(eng, first, step, last):
            first(0)
            with eng.Fori(0, G // 2 - 1) as h:
                step(2 * h + 1, 1)
                step(2 * h + 2, 0)
            last(G - 1)

        with nc.Block() as block:
            @block.sync
            def _(sp):
                def load(g, p, before):
                    if before is not None:
                        hold(sp, x_in[p], 16 * before, passed)
                        hold(sp, ctx_in[p], 16 * before, passed)
                        hold(sp, vals_done, g - 1, passed)
                    sp.dma_start(xg(g), x[bass.ds(g * GB, GB)].rearrange("b p d -> p b d")).then_inc(x_in[p], 16)
                    sp.dma_start(ctx[:, p], ctxT[:, bass.ds(g * GB, GB), :]).then_inc(ctx_in[p], 16)

                def repeat(t, kept, twice, g):
                    for a in range(2):
                        sp.wait_ge(kept, 2 * g + a + 1)
                        sp.dma_start(t[half_rows[1 - a], a], t[half_rows[a], a]).then_inc(twice, 16)

                load(0, 0, None)
                sp.dma_start(par[:, 0:FIRST_COLS], pack[:, 0:FIRST_COLS]).then_inc(params_in, 16)
                load(1, 1, None)
                sp.dma_start(par[:, FIRST_COLS:], pack[:, FIRST_COLS:]).then_inc(later_params_in, 16)

                def step(g, p, before):
                    repeat(kT, k_kept, k_twice, g)
                    repeat(qT, q_kept, q_twice, g)
                    if before is not None:
                        load(g + 2, p, before)
                step(0, 0, 1)
                step(1, 1, 1)
                with sp.Fori(1, G // 2 - 1) as h:
                    step(2 * h, 0, h + 1)
                    step(2 * h + 1, 1, h + 1)
                step(G - 2, 0, None)
                step(G - 1, 1, None)
                for p in range(2):
                    sp.wait_ge(x_in[p], 16 * (G // 2))
                    sp.wait_ge(ctx_in[p], 16 * (G // 2))
                sp.wait_ge(later_params_in, 16)
                sp.wait_ge(k_twice, 32 * G)
                sp.wait_ge(q_twice, 32 * G)

            @block.gpsimd
            def _(pool):
                nc.gpsimd.memset(halves[:], -0.5).then_inc(consts, 1)
                nc.gpsimd.memset(epsilons[:], EPS).then_inc(consts, 1)
                nc.gpsimd.memset(vals[:], 0.0).then_inc(consts, 1)
                for p in range(2):
                    nc.gpsimd.memset(probs[p][:, HH * KEYS:], 0.0).then_inc(consts, 1)
                pool.wait_ge(consts, 5)

                def norm(g):
                    pool.wait_ge(aggr_done, GB * g + GB)
                    nc.gpsimd.tensor_tensor(veps[:], mv[:, :, 1], epsilons[:, 0:GB], ALU.add).then_inc(veps_done, 1)
                    pool.wait_ge(veps_done, g + 1)
                    nc.gpsimd.tensor_tensor(rstd[:], veps[:], halves[:, 0:GB], ALU.pow).then_inc(rstd_done, 1)
                    if type(g) is int and g == 0:
                        pool.wait_ge(params_in, 16)
                    pool.wait_ge(xn_done, GB * g + GB)
                    nc.gpsimd.tensor_tensor(xg(g), xg(g), P("bo0").unsqueeze(1).to_broadcast([128, GB, D]),
                                            ALU.add).then_inc(bo_added, 1)

                def spread_keys(g, p):
                    if later(g, 2):
                        pool.wait_ge(s_done, UNITS * (g - 1))
                    for a in range(2):
                        for b in range(GB):
                            if b == 0:
                                pool.wait_ge(kparts_done, 2 * g + a + 1)
                            nc.gpsimd.tensor_tensor(
                                kbd[p][:, b, a, :].rearrange("p (h k) -> p h k", h=HH),
                                kparts[:, a, b, :].unsqueeze(1).to_broadcast([128, HH, KEYS]),
                                P("kmask").unsqueeze(2).to_broadcast([128, HH, KEYS]), ALU.mult).then_inc(kbd_done, 1)

                def rest_of_queries(g, p):
                    for a in range(2):
                        pool.wait_ge(qcut_done, 2 * g + a + 1)
                        if later(g, 2) and a == 0:
                            pool.wait_ge(s_done, UNITS * (g - 1))
                        nc.gpsimd.tensor_tensor(ql[p][a][:], qT[:, a], qcut[:, a], ALU.subtract).then_inc(ql_done, 1)

                norm(0)
                spread_keys(0, 0)
                pool.wait_ge(vx_clear, 1)
                nc.gpsimd.memset(vx[1][:], 0.0).then_inc(vx_clear, 1)

                def step(g, p):
                    norm(g + 1)
                    spread_keys(g + 1, 1 - p)
                    rest_of_queries(g + 1, 1 - p)
                over_groups(pool, lambda g: step(g, 0), step, lambda g: None)
                for j, name in enumerate(("W1T", "W2T")):
                    w = P(name)
                    pool.wait_ge(marks_done, 2 * j + 2)
                    nc.gpsimd.tensor_tensor(above[j][:], above[j][:], below[j][:], ALU.subtract).then_inc(ternary_done, 1)
                    pool.wait_ge(ternary_done, 3 * j + 1)
                    nc.gpsimd.tensor_tensor(above[j][:], above[j][:], w, ALU.subtract).then_inc(ternary_done, 1)
                    pool.wait_ge(ternary_done, 3 * j + 2)
                    nc.gpsimd.tensor_tensor(W1r[:] if j == 0 else w, w, above[j][:], ALU.add).then_inc(ternary_done, 1)
                pool.wait_ge(ternary_done, 6)

            @block.vector
            def _(dve):
                def set_ones(p):
                    dve.wait_ge(vx_clear, p + 1)
                    for c in range(CH):
                        at = (DH + 1) * first_head(c)
                        ones = vx[p][:, c, :, at:at + SLOTS * (DH + 1)].rearrange("p n (s e) -> p n s e", e=DH + 1)
                        nc.vector.tensor_copy(ones[:, :, :, DH], P("vmask")[:, c * SLOTS:(c + 1) * SLOTS].unsqueeze(1)
                                              .to_broadcast([128, GB * 2, SLOTS])).then_inc(ones_set, 1)

                def stats_of(g, p, again):
                    hold(dve, x_in[p], 16 * (again + 1), passed)
                    for b in range(GB):
                        nc.vector.bn_stats(stats[:, b, :], xg(g, b)).then_inc(stats_done, 1)
                    hold(dve, stats_done, GB * g + GB, passed)
                    for b in range(GB):
                        nc.vector.bn_aggr(mv[:, b, :], stats[:, b, :]).then_inc(aggr_done, 1)

                def normalise(g):
                    dve.wait_ge(rstd_done, g + 1)
                    if later(g, 1):
                        dve.wait_ge(xT_done, g)
                    for b in range(GB):
                        nc.vector.tensor_scalar(xn[:, b, :], xg(g, b), mv[:, b, 0:1], rstd[:, b:b + 1],
                                                ALU.subtract, ALU.mult).then_inc(xn_done, 1)

                def keep_values(g, p, part, bank=psM):
                    dve.wait_ge(v_done, 3 * g + part + 1)
                    if later(g, 2) and part == 0:
                        dve.wait_ge(pv_done, UNITS * (g - 1))
                    for k, c in enumerate(range(2 * part, min(2 * part + 2, CH))):
                        at = (DH + 1) * first_head(c)
                        nc.vector.tensor_tensor(
                            vx[p][:, c, :, at:at + SLOTS * (DH + 1)].rearrange("p n (s e) -> p n s e", e=DH + 1)[:, :, :, 0:DH],
                            bank[:, k * 192:(k + 1) * 192].rearrange("p (n s e) -> p n s e", s=SLOTS, e=DH),
                            P("vmask")[:, c * SLOTS:(c + 1) * SLOTS].unsqueeze(1).unsqueeze(3)
                            .to_broadcast([128, GB * 2, SLOTS, DH]), ALU.mult).then_inc(v_kept, 1)

                def split_keys(g, a):
                    dve.wait_ge(k_twice, 32 * g + 32)
                    if later(g, 1):
                        dve.wait_ge(kbd_done, 2 * GB * g)
                    nc.vector.tensor_scalar(kparts[:, a].bitcast(U32), kT[:, a].bitcast(U32), HIGH, None,
                                            ALU.bitwise_and).then_inc(kcut_done, 1)
                    dve.wait_ge(kcut_done, 2 * g + a + 1)
                    nc.vector.tensor_tensor(kparts[64:128, a], kT[64:128, a], kparts[64:128, a],
                                            ALU.subtract).then_inc(kparts_done, 1)

                def cut_queries(g, a):
                    dve.wait_ge(q_twice, 32 * g + 32)
                    if later(g, 1):
                        dve.wait_ge(qh_done, 2 * g + a - 1)
                        dve.wait_ge(ql_done, 2 * g + a - 1)
                    nc.vector.tensor_scalar(qcut[:, a].bitcast(U32), qT[:, a].bitcast(U32), HIGH, None,
                                            ALU.bitwise_and).then_inc(qcut_done, 1)

                def shift(g, u):
                    n = UNITS * g + u
                    scores = psS[:, :, 0:HH // 2 * KEYS].rearrange("p a (h k) -> p a h k", k=KEYS)
                    dve.wait_ge(s_done, n + 1)
                    nc.vector.tensor_reduce(most[:], scores, AX_X, ALU.max).then_inc(max_done, 1)
                    dve.wait_ge(max_done, n + 1)
                    if later(n, 2):
                        dve.wait_ge(exp_done, n - 1)
                    nc.vector.tensor_tensor(shifted[u % 2][:].rearrange("p (a h k) -> p a h k", a=2, k=KEYS), scores,
                                            most[:].rearrange("p (a h) -> p a h", a=2).unsqueeze(3)
                                            .to_broadcast([128, 2, HH // 2, KEYS]), ALU.subtract).then_inc(shift_done, 1)

                def divide(g, b):
                    k = GB * g + b
                    dve.wait_ge(pv_done, 2 * k + 2)
                    acc = psO[:, 0:256].rearrange("p (a c) -> p a c", a=2)[:, :, 0:HH * (DH + 1)].rearrange(
                        "p a (h e) -> p a h e", e=DH + 1)
                    nc.vector.reciprocal(rden[:], acc[:, :, :, DH]).then_inc(rden_done, 1)
                    dve.wait_ge(rden_done, k + 1)
                    if later(g, 1):
                        dve.wait_ge(oT_done, g)
                    nc.vector.tensor_tensor(o[:, b, :].rearrange("p (a h e) -> p a h e", a=2, e=DH),
                                            acc[:, :, :, 0:DH],
                                            rden[:].unsqueeze(3).to_broadcast([128, 2, HH, DH]),
                                            ALU.mult).then_inc(o_done, 1)

                def residual(g):
                    dve.wait_ge(wo_done, g + 1)
                    dve.wait_ge(bo_added, g + 1)
                    nc.vector.tensor_tensor(xg(g), xg(g), psM[:].rearrange("p (b d) -> p b d", d=D),
                                            ALU.add).then_inc(x_done, 1)

                stats_of(0, 0, 0)
                normalise(0)
                nc.vector.memset(vx[0][:], 0.0).then_inc(vx_clear, 1)
                dve.wait_ge(params_in, 16)
                set_ones(0)
                for a in range(2):
                    split_keys(0, a)
                for a in range(2):
                    cut_queries(0, a)
                    dve.wait_ge(qcut_done, a + 1)
                    nc.vector.tensor_tensor(ql[0][a][:], qT[:, a], qcut[:, a], ALU.subtract).then_inc(ql_done, 1)
                for part in range(3):
                    keep_values(0, 0, part, early[part])
                shift(0, 0)

                def sum_weights():
                    dve.wait_ge(later_params_in, 16)
                    for j, name in enumerate(("W1T", "W2T")):
                        nc.vector.tensor_reduce(absum[:, j:j + 1], P(name), AX_X, ALU.add,
                                                apply_absolute_value=True).then_inc(absum_done, 1)

                def halve_means():
                    dve.wait_ge(summed, 1)
                    nc.vector.tensor_scalar(half_mean[:], psM[:, 0:2], 0.5 / (D * FF), 0.5e-8, ALU.mult,
                                            ALU.max).then_inc(half_done, 1)
                    nc.vector.tensor_scalar(minus_half[:], psM[:, 0:2], -0.5 / (D * FF), -0.5e-8, ALU.mult,
                                            ALU.min).then_inc(half_done, 1)
                    dve.wait_ge(half_done, 2)

                def mark_weights(j):
                    w = P(("W1T", "W2T")[j])
                    nc.vector.tensor_scalar(above[j][:], w, half_mean[:, j:j + 1], None, ALU.is_gt).then_inc(marks_done, 1)
                    nc.vector.tensor_scalar(below[j][:], w, minus_half[:, j:j + 1], None, ALU.is_lt).then_inc(marks_done, 1)

                def step(g, p, again_next, prev=True, nxt=True):
                    for u in range(UNITS):
                        if prev and u == 0:
                            keep_values(g, p, 2)
                        if nxt and u >= UNITS - 2:
                            keep_values(g + 1, 1 - p, u - UNITS + 2)
                        if u < UNITS - 1:
                            shift(g, u + 1)
                        elif nxt:
                            shift(g + 1, 0)
                        if u % 2 == 0 and (prev or u):
                            divide(g if u else g - 1, (u // 2 - 1) % GB)
                        if u == 0 and nxt:
                            stats_of(g + 1, 1 - p, again_next)
                        if u == 3 and prev:
                            residual(g - 1)
                        if u in (2, 3) and nxt:
                            split_keys(g + 1, u - 2)
                        if u == 1 and nxt:
                            normalise(g + 1)
                        if not prev and u == 5:
                            set_ones(1)
                        if u in (5, 6) and nxt:
                            cut_queries(g + 1, u - 5)
                        if not nxt and u == 2:
                            sum_weights()
                        if not nxt and u == 4:
                            halve_means()
                        if not nxt and u in (4, 5):
                            mark_weights(u - 4)

                step(0, 0, 0, prev=False)
                with dve.Fori(0, G // 2 - 1) as h:
                    step(2 * h + 1, 1, h + 1)
                    step(2 * h + 2, 0, h + 1)
                step(G - 1, 1, 0, nxt=False)
                divide(G - 1, GB - 1)
                residual(G - 1)

            @block.scalar
            def _(act):
                def keep_xT(g):
                    act.wait_ge(xT_done, g + 1)
                    if later(g, 1):
                        act.wait_ge(q_done, g)
                    nc.scalar.copy(xnT[:], psM[:]).then_inc(xT_kept, 1)

                def keep_q(g, bank=psM):
                    act.wait_ge(q_done, g + 1)
                    if later(g, 1):
                        act.wait_ge(ql_done, 2 * g)
                    for a, rows in enumerate(half_rows):
                        nc.scalar.activation(qT[rows, a], bank[rows, 0:GB * S], ACT.Identity, bias=P("bq0")[rows]).then_inc(q_kept, 1)

                def keep_qh(g, p, a):
                    act.wait_ge(qcut_done, 2 * g + a + 1)
                    if later(g, 2) and a == 0:
                        act.wait_ge(s_done, UNITS * (g - 1))
                    nc.scalar.copy(qh[p][a][:], qcut[:, a]).then_inc(qh_done, 1)

                def keep_k(g, bank=psM):
                    act.wait_ge(k_done, g + 1)
                    if later(g, 1):
                        act.wait_ge(kparts_done, 2 * g)
                    for a, rows in enumerate(half_rows):
                        nc.scalar.activation(kT[rows, a], bank[rows, 0:GB * KEYS].rearrange("p (b k) -> p b k", k=KEYS),
                                             ACT.Identity, bias=P("bk0")[rows]).then_inc(k_kept, 1)

                def keep_vals(g):
                    act.wait_ge(vals_done, g + 1)
                    if later(g, 1):
                        act.wait_ge(v_done, 3 * g)
                    nc.scalar.copy(vals[:, :, 0:D], psM[0:KEYS, :].rearrange("p (b d) -> p b d", d=D)).then_inc(vals_kept, 1)

                def exponentials(g, u):
                    n = UNITS * g + u
                    act.wait_ge(shift_done, n + 1)
                    if later(n, 2):
                        act.wait_ge(pT_done, n - 1)
                    nc.scalar.activation(probs[u % 2][:, 0:HH * KEYS], shifted[u % 2][:], ACT.Exp,
                                         scale=SCALE).then_inc(exp_done, 1)

                def keep_pT(g, u):
                    n = UNITS * g + u
                    act.wait_ge(pT_done, n + 1)
                    if later(n, 2):
                        act.wait_ge(pv_done, n - 1)
                    nc.scalar.copy(probsT[u % 2][:], psT[u % 2][:, 0:FLAT]).then_inc(pT_kept, 1)

                def keep_oT(g):
                    act.wait_ge(oT_done, g + 1)
                    if later(g, 1):
                        act.wait_ge(wo_done, g)
                    nc.scalar.activation(oT[:], psM[:], ACT.Identity, bias=P("bv0")).then_inc(oT_kept, 1)

                act.wait_ge(consts, 5)
                act.wait_ge(params_in, 16)
                keep_k(0, psS[:, 0])
                keep_xT(0)
                keep_q(0, psT[0])
                keep_vals(0)
                for a in range(2):
                    keep_qh(0, 0, a)
                exponentials(0, 0)

                def step(g, p, prev=True, nxt=True):
                    for u in range(UNITS):
                        if nxt:
                            if u == 1:
                                keep_k(g + 1)
                            if u == 3:
                                keep_xT(g + 1)
                            if u == 4:
                                keep_q(g + 1)
                            if u == 5:
                                keep_vals(g + 1)
                        if prev and u == 2:
                            keep_oT(g - 1)
                        keep_pT(g, u)
                        if u >= 6 and nxt:
                            keep_qh(g + 1, 1 - p, u - 6)
                        if u < UNITS - 1:
                            exponentials(g, u + 1)
                        elif nxt:
                            exponentials(g + 1, 0)
                over_groups(act, lambda g: step(g, 0, prev=False), step, lambda g: step(g, 1, nxt=False))
                keep_oT(G - 1)

            @block.tensor
            def _(pe):
                mm = nc.tensor.matmul

                def transpose_x(g):
                    pe.wait_ge(xn_done, GB * g + GB)
                    for b in range(GB):
                        last = nc.tensor.transpose(psM[:, b * S:(b + 1) * S], xn[:, b, :], P("ident"))
                    last.then_inc(xT_done, 1)

                def queries(g, bank=psM):
                    pe.wait_ge(xT_kept, g + 1)
                    mm(bank[:, 0:GB * S], P("Wq0"), xnT[:], start=True, stop=True).then_inc(q_done, 1)

                def keys(g, p, again, bank=psM):
                    pe.wait_ge(ctx_in[p], 16 * (again + 1))
                    if later(g, 1):
                        pe.wait_ge(v_kept, CH * g)
                    mm(bank[:, 0:GB * KEYS], P("Wk0"), ctx[:, p], start=True, stop=True).then_inc(k_done, 1)

                def project_values(g, p):
                    if later(g, 1):
                        pe.wait_ge(q_kept, 2 * g + 2)
                    else:
                        pe.wait_ge(xT_kept, 1)
                    for b in range(GB):
                        last = mm(psM[0:KEYS, b * D:(b + 1) * D], ctx[:, p, b, :], P("Wv0"), start=True, stop=True)
                    last.then_inc(vals_done, 1)

                def values(g, part, bank=psM):
                    pe.wait_ge(vals_kept, g + 1)
                    if part and later(g, 1):
                        pe.wait_ge(v_kept, CH * g + 2 * part)
                    for k, c in enumerate(range(2 * part, min(2 * part + 2, CH))):
                        at, width = DH * first_head(c), SLOTS * DH
                        cols = bank[:, k * 192:(k + 1) * 192].rearrange("p (b a e) -> p b a e", b=GB, a=2)
                        rows_of_c = P("rowsel")[0:KEYS, c * 128:(c + 1) * 128]
                        if at + width <= D // 2:
                            last = mm(cols, rows_of_c, vals[:, :, 0:D].rearrange("k b (a r) -> k b a r", a=2)[:, :, :, at:at + width],
                                      start=True, stop=True)
                            continue
                        for half in range(2):
                            last = mm(cols[:, :, half, :], rows_of_c, vals[:, :, D // 2 * half + at:D // 2 * half + at + width],
                                      start=True, stop=True)
                    last.then_inc(v_done, 1)

                def scores(g, p, u):
                    n = UNITS * g + u
                    b, half = u // 2, u % 2
                    pe.wait_ge(kbd_done, 2 * GB * g + GB * half + b + 1)
                    if u < 2:
                        pe.wait_ge(qh_done, 2 * g + u + 1)
                        pe.wait_ge(ql_done, 2 * g + u + 1)
                    if later(n, 1):
                        pe.wait_ge(shift_done, n)
                    for part, q in enumerate((qh, ql)):
                        for a in range(2):
                            last = mm(psS[:, a, 0:HH // 2 * KEYS], q[p][half][:, b * S:(b + 1) * S],
                                      kbd[p][:, b, half, a * HH // 2 * KEYS:(a + 1) * HH // 2 * KEYS],
                                      start=part == 0, stop=part == 1)
                    last.then_inc(s_done, 1)

                def transpose_probs(g, u):
                    n = UNITS * g + u
                    pe.wait_ge(exp_done, n + 1)
                    if later(n, 2):
                        pe.wait_ge(pT_kept, n - 1)
                    for c in range(CH):
                        last = nc.tensor.transpose(psT[u % 2][:, c * 128:(c + 1) * 128],
                                                   probs[u % 2][:, c * 128:(c + 1) * 128], P("ident"))
                    last.then_inc(pT_done, 1)

                def weigh(g, p, u):
                    n = UNITS * g + u
                    b, half = u // 2, u % 2
                    pe.wait_ge(pT_kept, n + 1)
                    if half == 0:
                        if b == 0:
                            pe.wait_ge(v_kept, CH * g + CH)
                        if later(n, 1):
                            pe.wait_ge(o_done, GB * g + b)
                    for c in range(CH):
                        last = mm(psO[:, half * 128:(half + 1) * 128], probsT[u % 2][:, c * 128:(c + 1) * 128],
                                  vx[p][:, c, 2 * b + half, :], start=c == 0, stop=c == CH - 1)
                    last.then_inc(pv_done, 1)

                def transpose_o(g):
                    pe.wait_ge(o_done, GB * g + GB)
                    for b in range(GB):
                        last = nc.tensor.transpose(psM[:, b * S:(b + 1) * S], o[:, b, :], P("ident"))
                    last.then_inc(oT_done, 1)

                def project(g):
                    pe.wait_ge(oT_kept, g + 1)
                    for b in range(GB):
                        last = mm(psM[:, b * D:(b + 1) * D], oT[:, b * S:(b + 1) * S], P("Wo0"), start=True, stop=True)
                    last.then_inc(wo_done, 1)

                pe.wait_ge(params_in, 16)
                keys(0, 0, 0, psS[:, 0])
                transpose_x(0)
                queries(0, psT[0])
                project_values(0, 0)
                pe.wait_ge(consts, 5)
                for part in range(3):
                    values(0, part, early[part])
                pe.wait_ge(k_kept, 2)
                scores(0, 0, 0)
                pe.wait_ge(q_kept, 2)
                pe.wait_ge(v_kept, CH)
                pe.wait_ge(ones_set, CH)

                def step(g, p, again_next, prev=True, nxt=True):
                    for u in range(UNITS):
                        if u < UNITS - 1:
                            scores(g, p, u + 1)
                        elif nxt:
                            scores(g + 1, 1 - p, 0)
                        if not prev and u == UNITS - 1:
                            pe.wait_ge(ones_set, 2 * CH)
                        transpose_probs(g, u)
                        if prev and u == 3:
                            if nxt:
                                pe.wait_ge(xT_kept, g + 2)
                            project(g - 1)
                        if not nxt and u == 4:
                            pe.wait_ge(absum_done, 2)
                            pe.wait_ge(x_done, g)
                            mm(psM[:, 0:2], P("ones"), absum[:], start=True, stop=True).then_inc(summed, 1)
                        if u:
                            weigh(g, p, u - 1)
                        elif prev:
                            weigh(g - 1, 1 - p, UNITS - 1)
                        if prev and u == 1:
                            if nxt:
                                pe.wait_ge(k_kept, 2 * g + 4)
                            else:
                                pe.wait_ge(v_kept, CH * g + CH)
                            transpose_o(g - 1)
                        if nxt:
                            if u == 0:
                                keys(g + 1, 1 - p, again_next)
                            if u == 2:
                                if prev:
                                    pe.wait_ge(oT_kept, g)
                                else:
                                    pe.wait_ge(k_kept, 2 * g + 4)
                                transpose_x(g + 1)
                            if u == 3:
                                if prev:
                                    pe.wait_ge(x_done, g)
                                queries(g + 1)
                            if u == 4:
                                project_values(g + 1, 1 - p)
                            if u >= 5:
                                values(g + 1, u - 5)

                step(0, 0, 0, prev=False)
                with pe.Fori(0, G // 2 - 1) as h:
                    step(2 * h + 1, 1, h + 1)
                    step(2 * h + 2, 0, h + 1)
                step(G - 1, 1, 0, nxt=False)
                weigh(G - 1, 1, UNITS - 1)
                pe.wait_ge(half_done, 2)
                transpose_o(G - 1)
                project(G - 1)


def feed_forward0(nc, sem, X, xg, P, halves, epsilons, passed, weights, W, W1r):
    with ExitStack() as stack:
        def sb(name, shape, dt=F32):
            return stack.enter_context(nc.sbuf_tensor(name, shape, dt))

        def ps(name, shape, dt=F32):
            return stack.enter_context(nc.psum_tensor(name, shape, dt))

        stats = sb("b_stats", [128, GB, 6])
        mv = sb("b_mv", [128, GB, 2])
        veps = sb("b_veps", [128, GB])
        rstd = sb("b_rstd", [128, GB])
        xn = sb("b_xn", [128, GB, D])
        cut = sb("b_cut", [128, GB * S])
        xh = [sb(f"b_xh{p}", [128, GB * S], F32R) for p in range(2)]
        xl = [sb(f"b_xl{p}", [128, GB * S], F32R) for p in range(2)]
        hT = [sb(f"b_hT{p}", [128, FC, GB * S]) for p in range(2)]
        psX = ps("b_psX", [128, 512])
        psU = [ps(f"b_psU{c}", [128, 512]) for c in range(FC)]
        psY = [ps(f"b_psY{p}", [128, 512]) for p in range(2)]

        weights_in = sem("b_weights_in")
        stats_done = sem("b_stats_done")
        aggr_done = sem("b_aggr_done")
        veps_done = sem("b_veps_done")
        rstd_done = sem("b_rstd_done")
        xn_done = sem("b_xn_done")
        b2_added = sem("b_b2_added")
        xT_done = sem("b_xT_done")
        cut_done = sem("b_cut_done")
        xl_done = sem("b_xl_done")
        xh_done = sem("b_xh_done")
        up_done = sem("b_up_done")
        gelu_done = sem("b_gelu_done")
        down_done = sem("b_down_done")
        x_done = sem("b_x_done")

        def over_groups(eng, step):
            step(0, 0)
            with eng.Fori(0, (G - 6) // 2) as h:
                step(2 * h + 1, 1)
                step(2 * h + 2, 0)
            for g in range(G - 5, G):
                step(g, g % 2)

        def has(g, ahead):
            return type(g) is not int or g + ahead < G

        with nc.Block() as block:
            @block.sync
            def _(sp):
                for e in range(E):
                    sp.dma_start(W[:, e], weights[e]).then_inc(weights_in, 16)
                sp.wait_ge(weights_in, 16 * E)

            @block.gpsimd
            def _(pool):
                def norm(g):
                    pool.wait_ge(aggr_done, GB * g + GB)
                    nc.gpsimd.tensor_tensor(veps[:], mv[:, :, 1], epsilons[:, 0:GB], ALU.add).then_inc(veps_done, 1)
                    pool.wait_ge(veps_done, g + 1)
                    nc.gpsimd.tensor_tensor(rstd[:], veps[:], halves[:, 0:GB], ALU.pow).then_inc(rstd_done, 1)
                    pool.wait_ge(xn_done, GB * g + GB)
                    nc.gpsimd.tensor_tensor(xg(g), xg(g), P("b2").unsqueeze(1).to_broadcast([128, GB, D]),
                                            ALU.add).then_inc(b2_added, 1)

                for g in range(4):
                    norm(g)
                over_groups(pool, lambda g, p: norm(g + 4) if has(g, 4) else None)

            @block.vector
            def _(dve):
                def stats_of(g):
                    for b in range(GB):
                        nc.vector.bn_stats(stats[:, b, :], xg(g, b)).then_inc(stats_done, 1)
                    hold(dve, stats_done, GB * g + GB, passed)
                    for b in range(GB):
                        nc.vector.bn_aggr(mv[:, b, :], stats[:, b, :]).then_inc(aggr_done, 1)

                def normalise(g):
                    dve.wait_ge(rstd_done, g + 1)
                    if later(g, 1):
                        dve.wait_ge(xT_done, g)
                    for b in range(GB):
                        nc.vector.tensor_scalar(xn[:, b, :], xg(g, b), mv[:, b, 0:1], rstd[:, b:b + 1],
                                                ALU.subtract, ALU.mult).then_inc(xn_done, 1)

                def split(g, p):
                    dve.wait_ge(xT_done, g + 1)
                    if later(g, 1):
                        dve.wait_ge(xh_done, g)
                    nc.vector.tensor_scalar(cut[:].bitcast(U32), psX[:].bitcast(U32), HIGH, None,
                                            ALU.bitwise_and).then_inc(cut_done, 1)
                    dve.wait_ge(cut_done, g + 1)
                    if later(g, 2):
                        dve.wait_ge(up_done, FC * (g - 1))
                    nc.vector.tensor_tensor(xl[p][:], psX[:], cut[:], ALU.subtract).then_inc(xl_done, 1)

                stats_of(0)
                for g in range(3):
                    normalise(g)
                    stats_of(g + 1)
                    if g < 2:
                        split(g, g)

                def step(g, p):
                    if has(g, 2):
                        split(g + 2, p)
                    if has(g, 3):
                        normalise(g + 3)
                    if has(g, 4):
                        stats_of(g + 4)
                    dve.wait_ge(down_done, g + 1)
                    dve.wait_ge(b2_added, g + 1)
                    nc.vector.tensor_tensor(xg(g), xg(g), psY[p][:].rearrange("p (b d) -> p b d", d=D),
                                            ALU.add).then_inc(x_done, 1)
                over_groups(dve, step)
                dve.wait_ge(x_done, G)

            @block.scalar
            def _(act):
                def keep_high(g, p):
                    act.wait_ge(cut_done, g + 1)
                    if later(g, 2):
                        act.wait_ge(up_done, FC * (g - 1))
                    nc.scalar.copy(xh[p][:], cut[:]).then_inc(xh_done, 1)

                def gelu(g, p, c):
                    act.wait_ge(up_done, FC * g + c + 1)
                    if later(g, 2) and c == 0:
                        act.wait_ge(down_done, g - 1)
                    nc.scalar.activation(hT[p][:, c, :], psU[c][:], ACT.Gelu, bias=P("b1")[:, c:c + 1]).then_inc(gelu_done, 1)

                keep_high(0, 0)
                for c in range(FC):
                    gelu(0, 0, c)
                keep_high(1, 1)

                def step(g, p):
                    for c in range(FC):
                        if has(g, 1):
                            gelu(g + 1, 1 - p, c)
                        if c == 2 and has(g, 2):
                            keep_high(g + 2, p)
                over_groups(act, step)

            @block.tensor
            def _(pe):
                mm = nc.tensor.matmul

                def transpose_x(g):
                    pe.wait_ge(xn_done, GB * g + GB)
                    if later(g, 1):
                        pe.wait_ge(xl_done, g)
                    for b in range(GB):
                        last = nc.tensor.transpose(psX[:, b * S:(b + 1) * S], xn[:, b, :], P("ident"))
                    last.then_inc(xT_done, 1)

                def up(g, p, c):
                    if c == 0:
                        pe.wait_ge(xh_done, g + 1)
                        pe.wait_ge(xl_done, g + 1)
                    if later(g, 1):
                        pe.wait_ge(gelu_done, FC * (g - 1) + c + 1)
                    mm(psU[c][:], W1r[:, c * 128:(c + 1) * 128], xh[p][:], start=True, stop=False)
                    mm(psU[c][:], W1r[:, c * 128:(c + 1) * 128], xl[p][:], start=False, stop=True).then_inc(up_done, 1)

                def down(g, p, b):
                    if b == 0:
                        pe.wait_ge(gelu_done, FC * g + FC)
                        if later(g, 2):
                            pe.wait_ge(x_done, g - 1)
                    for c in range(FC):
                        last = mm(psY[p][:, b * D:(b + 1) * D], hT[p][:, c, b * S:(b + 1) * S],
                                  P("W2T")[:, c * D:(c + 1) * D], start=c == 0, stop=c == FC - 1)
                    if b == GB - 1:
                        last.then_inc(down_done, 1)

                transpose_x(0)
                for c in range(FC):
                    up(0, 0, c)
                transpose_x(1)

                def step(g, p):
                    for k in range(FC):
                        if has(g, 1):
                            up(g + 1, 1 - p, k)
                        down(g, p, k)
                        if k == 0 and has(g, 2):
                            transpose_x(g + 2)
                over_groups(pe, step)


def tile_table(nc, stack, sem, P, padding, rows, fill, table):
    def sb(name, shape, dt=F32):
        return stack.enter_context(nc.sbuf_tensor(name, shape, dt))

    in_dram = nc.dram_tensor("tile_table", (128, COLUMNS), I32, kind="Internal").ap()
    first = sb("t_first", [128, E])
    filled = sb("t_filled", [128, E])
    over = sb("t_over", [128, E, KMAX])
    ntiles = sb("t_ntiles", [128, E])
    ones = sb("t_ones", [128, E])
    ends = sb("t_ends", [128, E])
    begins = sb("t_begins", [128, E])
    past = sb("t_past", [128, E])
    begun = sb("t_begun", [128, E])
    cand = sb("t_cand", [128, E])
    entry = sb("t_entry", [128, 2])
    first_tile = sb("t_first_tile", [128, E + 1])
    before = sb("t_before", [128, 2])
    beforei = sb("t_beforei", [128, 2], I32)
    spare = sb("t_spare", [128, 1])
    filli = sb("t_filli", [128, E], I32)
    entryi = sb("t_entryi", [128, COLUMNS], I32)
    t_step = sem("t_step")
    table_out = sem("t_table_out")
    table_in = sem("t_table_in")
    padded = sem("t_padded")

    def work_out(dve):
        n = [0]

        def do(ins):
            n[0] += 1
            ins.then_inc(t_step, 1)
            dve.wait_ge(t_step, n[0])

        v = nc.vector
        do(v.tensor_copy(filli[:], fill[:]))
        do(v.tensor_scalar(first[:], P("eidx"), float(REGION), None, ALU.mult))
        do(v.tensor_tensor(filled[:], fill[:], first[:], ALU.subtract))
        do(v.tensor_tensor(over[:], filled[:].unsqueeze(2).to_broadcast([128, E, KMAX]),
                           P("steps").unsqueeze(1).to_broadcast([128, E, KMAX]), ALU.is_gt))
        do(v.tensor_reduce(ntiles[:], over[:], AX_X, ALU.add))
        do(v.memset(ones[:], 1.0))
        do(v.tensor_tensor_scan(ends[:], ones[:], ntiles[:], 0.0, ALU.mult, ALU.add))
        do(v.tensor_tensor(begins[:], ends[:], ntiles[:], ALU.subtract))
        do(v.tensor_scalar(past[:], ends[:], P("part"), None, ALU.is_le))
        do(v.tensor_scalar(begun[:], begins[:], P("part"), None, ALU.is_le))
        do(v.tensor_reduce(entry[:, 0:1], past[:], AX_X, ALU.add))
        do(v.tensor_scalar(entry[:, 0:1], entry[:, 0:1], float(E - 1), None, ALU.min))
        do(v.tensor_tensor(begun[:], begun[:], past[:], ALU.subtract))
        do(v.tensor_scalar(cand[:], begins[:], P("part"), -float(TT), ALU.subtract, ALU.mult))
        do(v.tensor_tensor(cand[:], cand[:], first[:], ALU.add))
        do(v.tensor_tensor(cand[:], cand[:], begun[:], ALU.mult))
        do(v.tensor_reduce(entry[:, 1:2], cand[:], AX_X, ALU.add))
        do(v.tensor_scalar(spare[:], past[:, E - 1:E], float(SPARE), None, ALU.mult))
        do(v.tensor_tensor(entry[:, 1:2], entry[:, 1:2], spare[:], ALU.add))
        do(v.tensor_copy(entryi[:, 0:2], entry[:]))
        do(v.tensor_tensor(first_tile[:, 0:E], begins[:], begun[:], ALU.mult))
        do(v.tensor_tensor(first_tile[:, E:E + 1], past[:, E - 1:E], P("part"), ALU.mult))
        do(v.tensor_reduce(before[:, 1:2], first_tile[:], AX_X, ALU.add))
        do(v.tensor_scalar(before[:, 0:1], before[:, 1:2], 1.0, None, ALU.add))
        do(v.tensor_copy(beforei[:], before[:]))
        do(v.tensor_scalar(beforei[:], beforei[:], 1, 5, ALU.logical_shift_right, ALU.logical_shift_left))
        do(v.tensor_scalar(entryi[:, 2:4], beforei[:], 16, None, ALU.add))

    def pad(eng, experts):
        eng.wait_ge(t_step, 1)
        for e in experts:
            row = eng.value_load(filli[0:1, e:e + 1], min_val=e * REGION, max_val=e * REGION + B * S)
            eng.dma_start(rows[bass.ds(row, TT)], padding).then_inc(padded, 16)

    def spread(sp):
        sp.wait_ge(t_step, 27)
        sp.dma_start(in_dram, entryi[:]).then_inc(table_out, 16)
        sp.wait_ge(table_out, 16)
        sp.dma_start(table[:], in_dram.rearrange("t c -> (t c)").unsqueeze(0)).then_inc(table_in, 16)
        sp.wait_ge(table_in, 16)
        sp.wait_ge(padded, 16 * E)

    return work_out, pad, spread


def attention1(nc, sem, ctxT, X, xg, P, halves, epsilons, passed, before, tokens, padding, rows, table, out):
    with ExitStack() as stack:
        def sb(name, shape, dt=F32):
            return stack.enter_context(nc.sbuf_tensor(name, shape, dt))

        def ps(name, shape, dt=F32):
            return stack.enter_context(nc.psum_tensor(name, shape, dt))

        ctx = sb("c_ctx", [128, 2, GB, KEYS])
        bq = sb("c_bq", [128, 1])
        stats = sb("c_stats", [128, B, 6])
        mv = sb("c_mv", [128, B, 2])
        veps = sb("c_veps", [128, B])
        rstd = sb("c_rstd", [128, B])
        moments = [sb(f"c_moments{p}", [128, GB, 2]) for p in range(2)]
        batches = [(max(4 * k - 2, 0), min(4 * k + 2, G)) for k in range(G // 4 + 1)]
        xn = sb("c_xn", [128, GB, D])
        xnT = sb("c_xnT", [128, GB * S])
        qT = sb("c_qT", [128, GB * S])
        kT = sb("c_kT", [128, GB, KEYS])
        v = [sb(f"c_v{p}", [KEYS, GB * D]) for p in range(2)]
        clipped = sb("c_clipped", [128, GB, KEYS])
        negmax = sb("c_negmax", [128, GB])
        probs = sb("c_probs", [128, GB, KEYS])
        den = [sb(f"c_den{p}", [128, GB]) for p in range(2)]
        rden = sb("c_rden", [128, GB])
        probsT = sb("c_probsT", [KEYS, GB * S])
        stats2 = sb("c_stats2", [128, GB, 6])
        mv2 = sb("c_mv2", [128, GB, 2])
        veps2 = sb("c_veps2", [128, GB])
        rstd2 = sb("c_rstd2", [128, GB])
        drow = [[sb(f"c_drow{p}{j}", [128, GB, ROW]) for j in range(2)] for p in range(2)]
        xn2 = sb("c_xn2", [128, GB, D])
        earlier = sb("c_earlier", [128, 128], BF16)
        fill = sb("c_fill", [128, E])
        onesb = sb("c_onesb", [128, 128], BF16)
        number = sb("c_number", [128, B], I32)
        chosen = [sb(f"c_chosen{p}", [128, GB + 1, E], BF16) for p in range(2)]
        hots = [[sb(f"c_hot{p}{j}", [128, GB, E]) for j in range(2)] for p in range(2)]
        place = sb("c_place", [128, GB, E])
        picked = sb("c_picked", [128, 2, GB, E])
        slotf = sb("c_slotf", [128, 2, GB])
        slot = [sb(f"c_slot{p}", [128, 2, GB], U32) for p in range(2)]
        xn2T = sb("c_xn2T", [128, GB * S])
        logits = sb("c_logits", [128, GB, E])
        top = sb("c_top", [128, GB, 8])
        topi = sb("c_topi", [128, GB, 8], U32)
        topf = sb("c_topf", [128, GB, 8])
        gap = sb("c_gap", [128, GB])
        egap = sb("c_egap", [128, GB])
        egap1 = sb("c_egap1", [128, GB])

        psX = ps("c_psX", [128, 512])
        psQ = ps("c_psQ", [128, 512])
        psK = ps("c_psK", [128, 512])
        psV = ps("c_psV", [KEYS, 512])
        psS = ps("c_psS", [128, 512])
        psP = ps("c_psP", [KEYS, 512])
        psY = ps("c_psY", [128, 512])
        psL = ps("c_psL", [128, 512])
        psR = psL[:, 256:512]

        names = ("moments_done bq_done stats_done aggr_done veps_done rstd_done xn_done xT_done xT_kept q_done q_kept k_done k_kept "
                 "v_done v_kept s_done clip_done max_done exp_done rden_done pT_done pT_kept y_done x_done stats2_done "
                 "aggr2_done veps2_done rstd2_done xn2_done x2T_done x2T_kept l_done l_kept top_done topi_done topf_done "
                 "gap_done egap_done egap1_done w1_done w2_done hot_done chosen_done row_copied number_done setup rank_done place_done picked_done slotf_done slot_done fill_done x_kept consts_in").split()
        (moments_done, bq_done, stats_done, aggr_done, veps_done, rstd_done, xn_done, xT_done, xT_kept, q_done, q_kept, k_done,
         k_kept, v_done, v_kept, s_done, clip_done, max_done, exp_done, rden_done, pT_done, pT_kept, y_done, x_done,
         stats2_done, aggr2_done, veps2_done, rstd2_done, xn2_done, x2T_done, x2T_kept, l_done, l_kept, top_done,
         topi_done, topf_done, gap_done, egap_done, egap1_done, w1_done, w2_done, hot_done, chosen_done,
         row_copied, number_done, setup, rank_done, place_done, picked_done, slotf_done, slot_done, fill_done, x_kept,
         consts_in) = [sem("c_" + name) for name in names]
        ctx_in = [sem(f"c_ctx_in{p}") for p in range(2)]
        sent = [sem(f"c_sent{p}") for p in range(2)]

        work_out, pad, spread = tile_table(nc, stack, sem, P, padding, rows, fill, table)

        def over_steps(eng, step, first=4, left=0):
            for g in range(first):
                step(g, g % 2, None)
            with eng.Fori(first // 2, (G - left) // 2) as h:
                step(2 * h, 0, h)
                step(2 * h + 1, 1, h)
            for g in range(G - left, G + 4):
                step(g, g % 2, None)

        def live(g, lag):
            return type(g) is not int or 0 <= g - lag < G

        with nc.Block() as block:
            @block.sync
            def _(sp):
                def load(g, p, times):
                    if times is not None:
                        sp.wait_ge(ctx_in[p], 16 * times)
                        sp.wait_ge(v_done, g - 1)
                    sp.dma_start(ctx[:, p], ctxT[:, bass.ds(g * GB, GB), :]).then_inc(ctx_in[p], 16)

                def keep_x(g):
                    hold(sp, x_done, GB * g + GB, passed)
                    sp.dma_start(out[bass.ds(g * GB * S, GB * S)].rearrange("(b p) d -> p b d", p=128),
                                 xg(g)).then_inc(x_kept, 16)

                load(0, 0, None)
                load(1, 1, None)
                sp.dma_start(earlier[:], before).then_inc(consts_in, 16)
                sp.dma_start(number[:], tokens).then_inc(consts_in, 16)
                sp.dma_start(rows[SPARE:SPARE + TT], padding).then_inc(consts_in, 16)
                with sp.Fori(1, G // 2) as h:
                    load(2 * h, 0, h)
                    load(2 * h + 1, 1, h)
                    keep_x(2 * h - 2)
                    keep_x(2 * h - 1)
                keep_x(G - 2)
                keep_x(G - 1)
                for p in range(2):
                    sp.wait_ge(ctx_in[p], 16 * (G // 2))
                pad(sp, range(E // 2))
                spread(sp)
                sp.wait_ge(x_kept, 16 * G)
                sp.wait_ge(consts_in, 48)

            @block.gpsimd
            def _(pool):
                def dispatch(g, p, b):
                    for j in range(2):
                        nc.gpsimd.indirect_dma_start(
                            rows, bass.IndirectOffsetOnAxis(ap=slot[p][:, j, b:b + 1], axis=0),
                            drow[p][j][:, b, :], None).then_inc(sent[p], 16)

                def norm(k):
                    at, end = GB * batches[k][0], GB * batches[k][1]
                    pool.wait_ge(aggr_done, end)
                    nc.gpsimd.tensor_tensor(veps[:, at:end], mv[:, at:end, 1], epsilons[:, 0:end - at], ALU.add).then_inc(veps_done, 1)
                    pool.wait_ge(veps_done, k + 1)
                    nc.gpsimd.tensor_tensor(rstd[:, at:end], veps[:, at:end], halves[:, 0:end - at], ALU.pow).then_inc(rstd_done, 1)

                def step(g, p, h):
                    if live(g, 4):
                        hold(pool, slot_done, g - 3, passed)
                        for b in range(3):
                            dispatch(g - 4, p, b)
                    if live(g, 2):
                        pool.wait_ge(aggr2_done, GB * (g - 1))
                        nc.gpsimd.tensor_tensor(veps2[:], mv2[:, :, 1], epsilons[:, 0:GB], ALU.add).then_inc(veps2_done, 1)
                        pool.wait_ge(veps2_done, g - 1)
                        nc.gpsimd.tensor_tensor(rstd2[:], veps2[:], halves[:, 0:GB], ALU.pow).then_inc(rstd2_done, 1)
                    if live(g, 4):
                        dispatch(g - 4, p, 3)
                    if type(g) is int and g + 1 < len(batches):
                        norm(g + 1)
                norm(0)
                over_steps(pool, step, left=2)
                for p in range(2):
                    pool.wait_ge(sent[p], 16 * 2 * GB * G // 2)

            @block.vector
            def _(dve):
                nc.vector.tensor_scalar(bq[:], P("bq1"), SCALE, None, ALU.mult).then_inc(bq_done, 1)
                nc.vector.tensor_scalar(fill[:], P("eidx"), float(REGION), None, ALU.mult).then_inc(fill_done, 1)
                nc.vector.memset(onesb[:], 1.0).then_inc(setup, 1)
                for p in range(2):
                    nc.vector.memset(chosen[p][:, GB, :], 0.0).then_inc(setup, 1)

                def measure(k):
                    at, end = GB * batches[k][0], GB * batches[k][1]
                    for n in range(at, end):
                        nc.vector.bn_stats(stats[:, n, :], X[:, n, :]).then_inc(stats_done, 1)
                    dve.wait_ge(stats_done, end)
                    for n in range(at, end):
                        nc.vector.bn_aggr(mv[:, n, :], stats[:, n, :]).then_inc(aggr_done, 1)

                def keep_moments(g, p):
                    taken = [k for k, (at, end) in enumerate(batches) if type(g) is not int or g >= at]
                    dve.wait_ge(rstd_done, len(taken))
                    if later(g, 2):
                        dve.wait_ge(xn_done, GB * (g - 1))
                    nc.vector.tensor_copy(moments[p][:, :, 0], mv[:, bass.ds(g * GB, GB), 0]).then_inc(moments_done, 1)
                    nc.vector.tensor_copy(moments[p][:, :, 1], rstd[:, bass.ds(g * GB, GB)]).then_inc(moments_done, 1)

                def normalise(g, p):
                    dve.wait_ge(moments_done, 2 * g + 2)
                    if later(g, 1):
                        dve.wait_ge(xT_done, g)
                    for b in range(GB):
                        nc.vector.tensor_scalar(xn[:, b, :], xg(g, b), moments[p][:, b, 0:1], moments[p][:, b, 1:2],
                                                ALU.subtract, ALU.mult).then_inc(xn_done, 1)

                def clip(g):
                    dve.wait_ge(s_done, g + 1)
                    if later(g, 1):
                        dve.wait_ge(exp_done, GB * g)
                    nc.vector.tensor_scalar(clipped[:], psS[:, 0:GB * KEYS].rearrange("p (b k) -> p b k", k=KEYS),
                                            100.0, -100.0, ALU.min, ALU.max).then_inc(clip_done, 1)

                def find_max(g):
                    dve.wait_ge(clip_done, g + 1)
                    nc.vector.tensor_reduce(negmax[:], clipped[:], AX_X, ALU.max, negate=True).then_inc(max_done, 1)

                def finish_attention(g, p):
                    dve.wait_ge(exp_done, GB * g + GB)
                    nc.vector.reciprocal(rden[:], den[p][:]).then_inc(rden_done, 1)
                    dve.wait_ge(rden_done, g + 1)
                    dve.wait_ge(y_done, g + 1)
                    for b in range(GB):
                        nc.vector.scalar_tensor_tensor(xg(g, b), psY[:, b * D:(b + 1) * D], rden[:, b:b + 1], xg(g, b),
                                                       ALU.mult, ALU.add).then_inc(x_done, 1)

                def second_stats(g):
                    hold(dve, x_done, GB * g + GB, passed)
                    for b in range(GB):
                        nc.vector.bn_stats(stats2[:, b, :], xg(g, b)).then_inc(stats2_done, 1)

                def second_aggregate(g):
                    hold(dve, stats2_done, GB * g + GB, passed)
                    for b in range(GB):
                        nc.vector.bn_aggr(mv2[:, b, :], stats2[:, b, :]).then_inc(aggr2_done, 1)

                def set_numbers(g, p, reused):
                    if reused is not None:
                        dve.wait_ge(sent[p], 16 * 2 * GB * reused)
                    if type(g) is int and g == 0:
                        dve.wait_ge(consts_in, 48)
                    for j in range(2):
                        nc.vector.tensor_copy(drow[p][j][:, :, ROW - 1].bitcast(I32),
                                              number[:, bass.ds(g * GB, GB)]).then_inc(number_done, 1)

                def second_normalise(g):
                    dve.wait_ge(rstd2_done, g + 1)
                    if later(g, 1):
                        dve.wait_ge(x2T_done, g)
                        dve.wait_ge(row_copied, 2 * g)
                    for b in range(GB):
                        nc.vector.tensor_scalar(xn2[:, b, :], xg(g, b), mv2[:, b, 0:1], rstd2[:, b:b + 1],
                                                ALU.subtract, ALU.mult).then_inc(xn2_done, 1)

                def keep_logits(g):
                    dve.wait_ge(l_done, g + 1)
                    nc.vector.tensor_copy(logits[:], psL[:, 0:GB * E].rearrange("p (b e) -> p b e", e=E)).then_inc(l_kept, 1)

                def two_largest(g):
                    hold(dve, l_kept, g + 1, passed)
                    for b in range(GB):
                        nc.vector.max(top[:, b, :], logits[:, b, :]).then_inc(top_done, 1)

                def their_experts(g):
                    hold(dve, top_done, GB * g + GB, passed)
                    for b in range(GB):
                        nc.vector.max_index(topi[:, b, :], top[:, b, :], logits[:, b, :]).then_inc(topi_done, 1)
                    nc.vector.tensor_tensor(gap[:], top[:, :, 1], top[:, :, 0], ALU.subtract).then_inc(gap_done, 1)

                def as_floats(g):
                    dve.wait_ge(topi_done, GB * g + GB)
                    nc.vector.tensor_copy(topf[:], topi[:]).then_inc(topf_done, 1)

                def mark(g, p):
                    dve.wait_ge(topf_done, g + 1)
                    for j in range(2):
                        nc.vector.tensor_tensor(hots[p][j][:], P("eidx").unsqueeze(1).to_broadcast([128, GB, E]),
                                                topf[:, :, j:j + 1].to_broadcast([128, GB, E]),
                                                ALU.is_equal).then_inc(hot_done, 1)

                def choose(g, p):
                    dve.wait_ge(hot_done, 2 * g + 2)
                    nc.vector.tensor_tensor(chosen[p][:, 0:GB, :], hots[p][0][:], hots[p][1][:],
                                            ALU.add).then_inc(chosen_done, 1)

                def gate(g, p):
                    dve.wait_ge(egap1_done, g + 1)
                    nc.vector.reciprocal(drow[p][0][:, :, D], egap1[:]).then_inc(w1_done, 1)
                    dve.wait_ge(w1_done, g + 1)
                    nc.vector.tensor_tensor(drow[p][1][:, :, D], drow[p][0][:, :, D], egap[:], ALU.mult).then_inc(w2_done, 1)

                ranks = psR[:, 0:(GB + 1) * E].rearrange("p (b e) -> p b e", e=E)

                def find_places(g):
                    dve.wait_ge(rank_done, g + 1)
                    dve.wait_ge(fill_done, g + 1)
                    nc.vector.tensor_tensor(place[:], ranks[:, 0:GB, :], fill[:].unsqueeze(1).to_broadcast([128, GB, E]),
                                            ALU.add).then_inc(place_done, 1)

                def count(g):
                    dve.wait_ge(place_done, g + 1)
                    nc.vector.tensor_tensor(fill[:], fill[:], ranks[:, GB, :], ALU.add).then_inc(fill_done, 1)

                def pick_places(g, p):
                    for j in range(2):
                        nc.vector.tensor_tensor(picked[:, j], place[:], hots[p][j][:], ALU.mult).then_inc(picked_done, 1)

                def add_picked(g):
                    dve.wait_ge(picked_done, 2 * g + 2)
                    nc.vector.tensor_reduce(slotf[:], picked[:], AX_X, ALU.add).then_inc(slotf_done, 1)

                def as_slots(g, p):
                    dve.wait_ge(slotf_done, g + 1)
                    dve.wait_ge(row_copied, 2 * g + 2)
                    dve.wait_ge(w2_done, g + 1)
                    nc.vector.tensor_copy(slot[p][:], slotf[:]).then_inc(slot_done, 1)

                def step(g, p, h):
                    first, middle, old, oldest, new = live(g, 1), live(g, 2), live(g, 3), live(g, 4), live(g, -1)
                    reused = h - 2 + p if h is not None else (g - 3) // 2 or None
                    if first:
                        clip(g - 1)
                    if oldest:
                        find_places(g - 4)
                    if first:
                        find_max(g - 1)
                    if oldest:
                        count(g - 4)
                        pick_places(g - 4, p)
                    if oldest:
                        add_picked(g - 4)
                    if old:
                        second_normalise(g - 3)
                    if oldest:
                        as_slots(g - 4, p)
                    if live(g, 0):
                        normalise(g, p)
                    if middle:
                        finish_attention(g - 2, p)
                        second_stats(g - 2)
                    if old:
                        keep_logits(g - 3)
                    if middle:
                        second_aggregate(g - 2)
                    if old:
                        two_largest(g - 3)
                    if type(g) is int and g + 1 < len(batches):
                        measure(g + 1)
                    if old:
                        their_experts(g - 3)
                    if new:
                        keep_moments(g + 1, 1 - p)
                    if old:
                        as_floats(g - 3)
                        dve.wait_ge(egap_done, g - 2)
                        nc.vector.tensor_scalar(egap1[:], egap[:], 1.0, None, ALU.add).then_inc(egap1_done, 1)
                        mark(g - 3, 1 - p)
                        set_numbers(g - 3, 1 - p, reused)
                        gate(g - 3, 1 - p)
                        choose(g - 3, 1 - p)

                measure(0)
                keep_moments(0, 0)
                over_steps(dve, step, first=6, left=2)
                dve.wait_ge(fill_done, G + 1)
                work_out(dve)

            @block.scalar
            def _(act):
                act.wait_ge(bq_done, 1)

                def step(g, p, h):
                    if live(g, 2):
                        act.wait_ge(pT_done, g - 1)
                        if later(g, 3):
                            act.wait_ge(y_done, g - 2)
                        nc.scalar.copy(probsT[:], psP[:]).then_inc(pT_kept, 1)
                    if live(g, 0):
                        act.wait_ge(k_done, g + 1)
                        if later(g, 1):
                            act.wait_ge(s_done, g)
                        nc.scalar.activation(kT[:], psK[:, 0:GB * KEYS].rearrange("p (b k) -> p b k", k=KEYS),
                                             ACT.Identity, bias=P("bk1")).then_inc(k_kept, 1)
                    if live(g, 1):
                        act.wait_ge(max_done, g)
                        if later(g, 2):
                            act.wait_ge(pT_done, g - 1)
                        if later(g, 3):
                            act.wait_ge(rden_done, g - 2)
                        for b in range(GB):
                            nc.scalar.activation(probs[:, b, :], clipped[:, b, :], ACT.Exp, bias=negmax[:, b:b + 1],
                                                 accum_out=den[1 - p][:, b:b + 1]).then_inc(exp_done, 1)
                    if live(g, 3):
                        act.wait_ge(x2T_done, g - 2)
                        if later(g, 4):
                            act.wait_ge(l_done, g - 3)
                        nc.scalar.copy(xn2T[:], psQ[:]).then_inc(x2T_kept, 1)
                    if live(g, 0):
                        act.wait_ge(xT_done, g + 1)
                        if later(g, 1):
                            act.wait_ge(q_done, g)
                        nc.scalar.copy(xnT[:], psX[:]).then_inc(xT_kept, 1)
                    if live(g, 0):
                        act.wait_ge(v_done, g + 1)
                        if later(g, 2):
                            act.wait_ge(y_done, g - 1)
                        nc.scalar.copy(v[p][:], psV[:]).then_inc(v_kept, 1)
                    if live(g, 0):
                        act.wait_ge(q_done, g + 1)
                        if later(g, 1):
                            act.wait_ge(s_done, g)
                        nc.scalar.activation(qT[:], psQ[:], ACT.Identity, bias=bq[:], scale=SCALE).then_inc(q_kept, 1)
                    if live(g, 3):
                        act.wait_ge(gap_done, g - 2)
                        nc.scalar.activation(egap[:], gap[:], ACT.Exp).then_inc(egap_done, 1)
                    if live(g, 3):
                        reused = h - 2 + p if h is not None else (g - 3) // 2 or None
                        if reused is not None:
                            act.wait_ge(sent[1 - p], 16 * 2 * GB * reused)
                        for j in range(2):
                            nc.scalar.copy(drow[1 - p][j][:, :, 0:D], xn2[:]).then_inc(row_copied, 1)
                over_steps(act, step, first=6)
                pad(act, range(E // 2, E))
                act.wait_ge(row_copied, 2 * G)

            @block.tensor
            def _(pe):
                mm = nc.tensor.matmul

                def step(g, p, h):
                    if live(g, 1):
                        pe.wait_ge(q_kept, g)
                        pe.wait_ge(k_kept, g)
                        if later(g, 2):
                            pe.wait_ge(clip_done, g - 1)
                        for b in range(GB):
                            done = mm(psS[:, b * KEYS:(b + 1) * KEYS], qT[:, b * S:(b + 1) * S], kT[:, b, :],
                                      start=True, stop=True)
                        done.then_inc(s_done, 1)
                    if live(g, 4):
                        pe.wait_ge(chosen_done, g - 3)
                        pe.wait_ge(l_kept, g - 3)
                        many = chosen[p]
                        mm(psR[:, 0:(GB + 1) * E], earlier[:], many[:], start=True, stop=False, skip_group_check=True)
                        for b in range(GB):
                            done = mm(psR[:, (b + 1) * E:(GB + 1) * E].rearrange("p (b e) -> p b e", e=E), onesb[:],
                                      many[:, b:b + 1, :].to_broadcast([128, GB - b, E]), start=False,
                                      stop=b == GB - 1, skip_group_check=True)
                        done.then_inc(rank_done, 1)
                    if live(g, 2):
                        pe.wait_ge(exp_done, GB * (g - 1))
                        if later(g, 3):
                            pe.wait_ge(pT_kept, g - 2)
                        for b in range(GB):
                            done = nc.tensor.transpose(psP[:, b * S:(b + 1) * S], probs[:, b, :], P("ident"))
                        done.then_inc(pT_done, 1)
                    if live(g, 0):
                        pe.wait_ge(ctx_in[p], 16 * (h + 1) if h is not None else 16 * (g // 2 + 1))
                        if later(g, 1):
                            pe.wait_ge(k_kept, g)
                        mm(psK[:, 0:GB * KEYS], P("Wk1"), ctx[:, p], start=True, stop=True).then_inc(k_done, 1)
                    if live(g, 2):
                        pe.wait_ge(pT_kept, g - 1)
                        pe.wait_ge(v_kept, g - 1)
                        if later(g, 3):
                            pe.wait_ge(x_done, GB * (g - 2))
                        for b in range(GB):
                            done = mm(psY[:, b * D:(b + 1) * D], probsT[:, b * S:(b + 1) * S],
                                      v[p][:, b * D:(b + 1) * D], start=True, stop=True)
                        done.then_inc(y_done, 1)
                    if live(g, 3):
                        pe.wait_ge(xn2_done, GB * (g - 2))
                        if live(g, 1):
                            pe.wait_ge(q_kept, g)
                        for b in range(GB):
                            done = nc.tensor.transpose(psQ[:, b * S:(b + 1) * S], xn2[:, b, :], P("ident"))
                        done.then_inc(x2T_done, 1)
                    if live(g, 0):
                        pe.wait_ge(xn_done, GB * g + GB)
                        if later(g, 1):
                            pe.wait_ge(xT_kept, g)
                        for b in range(GB):
                            done = nc.tensor.transpose(psX[:, b * S:(b + 1) * S], xn[:, b, :], P("ident"))
                        done.then_inc(xT_done, 1)
                    if live(g, 3):
                        pe.wait_ge(x2T_kept, g - 2)
                        if live(g, 4):
                            pe.wait_ge(fill_done, g - 2)
                    if later(g, 1) and live(g, 0):
                        pe.wait_ge(v_kept, g)
                    for b in range(GB):
                        if live(g, 3):
                            done = mm(psL[:, b * E:(b + 1) * E], xn2T[:, b * S:(b + 1) * S], P("router"),
                                      start=True, stop=True)
                            if b == GB - 1:
                                done.then_inc(l_done, 1)
                        if live(g, 0):
                            mm(psV[:, b * D:(b + 1) * D], ctx[:, p, b, :], P("Wv1"), start=b == 0, stop=False,
                               skip_group_check=True)
                    if live(g, 0):
                        mm(psV[:].rearrange("k (b d) -> k b d", d=D), P("ones")[0:1, 0:KEYS],
                           P("bv1")[0:1, :].unsqueeze(1).to_broadcast([1, GB, D]), start=False, stop=True,
                           skip_group_check=True).then_inc(v_done, 1)
                    if live(g, 0):
                        pe.wait_ge(xT_kept, g + 1)
                        if later(g, 1):
                            pe.wait_ge(q_kept, g)
                        mm(psQ[:], P("Wq1"), xnT[:], start=True, stop=True).then_inc(q_done, 1)
                    if type(g) is int and g == 3:
                        pe.wait_ge(consts_in, 48)
                        pe.wait_ge(setup, 3)

                over_steps(pe, step)


def experts(nc, sem, P, passed, W, table, padding, rows, out):
    with ExitStack() as stack:
        def sb(name, shape, dt=F32):
            return stack.enter_context(nc.sbuf_tensor(name, shape, dt))

        def ps(name, shape, dt=F32):
            return stack.enter_context(nc.psum_tensor(name, shape, dt))

        w = [sb(f"d_w{p}", [128, WCOLS]) for p in range(4)]
        xt = [sb(f"d_xt{p}", [128, TB, ROW]) for p in range(4)]
        gates = [sb(f"d_gates{p}", [128, TB]) for p in range(4)]
        numbers = [sb(f"d_numbers{p}", [128, TB], I32) for p in range(4)]
        xT = [sb(f"d_xT{p}", [128, TT]) for p in range(2)]
        hT = [sb(f"d_hT{p}", [128, FC, TT]) for p in range(2)]
        yb = sb("d_yb", [128, TB, D])
        y = [sb(f"d_y{p}", [128, TB, D]) for p in range(2)]
        psX = ps("d_psX", [128, 512])
        psU = [ps(f"d_psU{c}", [128, 512]) for c in range(FC)]
        psY = [ps(f"d_psY{p}", [128, 512]) for p in range(2)]

        w_kept = sem("d_w_kept")
        rows_in = [sem(f"d_rows_in{p}") for p in range(4)]
        xT_done = sem("d_xT_done")
        xT_kept = sem("d_xT_kept")
        up_done = sem("d_up_done")
        gelu_done = sem("d_gelu_done")
        down_done = sem("d_down_done")
        ends_kept = sem("d_ends_kept")
        yb_done = sem("d_yb_done")
        y_done = sem("d_y_done")
        added = [sem(f"d_added{p}") for p in range(2)]

        def over_tiles(eng, step):
            for t in range(4):
                step(t, t)
            with eng.Fori(1, TILES // 4 - 1) as q:
                for k in range(4):
                    step(4 * q + k, k)
            for k in range(4):
                step(TILES - 4 + k, k)

        def has(t, ahead):
            return type(t) is not int or t + ahead < TILES

        with nc.Block() as block:
            @block.sync
            def _(sp):
                def load(q, t, k, first):
                    row = sp.value_load(table[0:1, bass.ds(COLUMNS * t + 1, 1)], min_val=0, max_val=SPARE)
                    if not first:
                        hold(sp, rows_in[k], 16 * q, passed)
                        hold(sp, xT_done, t - 3, passed)
                        hold(sp, ends_kept, 2 * (t - 3), passed)
                    sp.dma_start(xt[k][:], rows[bass.ds(row, TT)].rearrange("(j p) c -> p j c", p=128)).then_inc(rows_in[k], 16)

                for k in range(4):
                    load(0, k, k, True)
                with sp.Fori(1, TILES // 4) as q:
                    for k in range(4):
                        load(q, 4 * q + k, k, False)

            @block.gpsimd
            def _(pool):
                for p in range(2):
                    pool.dma_start(out[B * S + p * TT // 2:B * S + (p + 1) * TT // 2],
                                   padding[p * TT // 2:(p + 1) * TT // 2, 0:D]).then_inc(added[p], 16)

                def step(t, k):
                    hold(pool, y_done, TB * t + TB, passed)
                    for p in range(2):
                        earlier = pool.value_load(table[0:1, bass.ds(COLUMNS * t + 2 + p, 1)], min_val=16,
                                                  max_val=16 * TB * TILES // 2 + 16)
                        hold(pool, added[p], earlier, passed)
                    for j in range(TB):
                        nc.gpsimd.indirect_dma_start(
                            out, bass.IndirectOffsetOnAxis(ap=numbers[k][:, j:j + 1].bitcast(U32), axis=0),
                            y[k % 2][:, j, :], None, compute_op=ALU.add).then_inc(added[k % 2], 16)
                over_tiles(pool, step)
                for p in range(2):
                    pool.wait_ge(added[p], 16 * TB * TILES // 2 + 16)

            @block.vector
            def _(dve):
                def keep_ends(k, loaded):
                    dve.wait_ge(rows_in[k], loaded)
                    nc.vector.tensor_copy(gates[k][:], xt[k][:, :, D]).then_inc(ends_kept, 1)
                    nc.vector.tensor_copy(numbers[k][:], xt[k][:, :, D + 1].bitcast(I32)).then_inc(ends_kept, 1)

                def keep_weights(t, k):
                    expert = dve.value_load(table[0:1, bass.ds(COLUMNS * t, 1)], min_val=0, max_val=E - 1)
                    if later(t, 4):
                        hold(dve, down_done, t - 3, passed)
                    nc.vector.tensor_copy(w[k][:], W[:, bass.ds(expert, 1), :].rearrange("p e c -> p (e c)")).then_inc(w_kept, 1)

                def step(t, k):
                    dve.wait_ge(down_done, t + 1)
                    dve.wait_ge(w_kept, t + 1)
                    if later(t, 1):
                        dve.wait_ge(y_done, TB * t)
                    nc.vector.tensor_tensor(yb[:], psY[k % 2][:, 0:TT].rearrange("p (j d) -> p j d", d=D),
                                            w[k][:, WCOLS - D:].unsqueeze(1).to_broadcast([128, TB, D]),
                                            ALU.add).then_inc(yb_done, 1)
                    dve.wait_ge(yb_done, t + 1)
                    if later(t, 2):
                        dve.wait_ge(added[k % 2], 16 * TB * ((t - k) // 2 + k // 2) + 16 if type(t) is int else
                                    16 * TB * (2 * loop[0] + k // 2) + 16)
                    for j in range(TB):
                        nc.vector.tensor_scalar(y[k % 2][:, j, :], yb[:, j, :], gates[k][:, j:j + 1], None,
                                                ALU.mult).then_inc(y_done, 1)
                    if has(t, 3):
                        keep_weights(t + 3, (k + 3) % 4)
                    if type(t) is not int:
                        keep_ends((k + 2) % 4, 16 * (loop[0] + (k + 2) // 4 + 1))
                    elif t + 2 < TILES:
                        keep_ends((k + 2) % 4, 16 * ((t + 2) // 4 + 1))
                loop = [None]
                for k in range(3):
                    keep_weights(k, k)
                for k in range(2):
                    keep_ends(k, 16)
                for t in range(4):
                    step(t, t)
                with dve.Fori(1, TILES // 4 - 1) as q:
                    loop[0] = q
                    for k in range(4):
                        step(4 * q + k, k)
                for k in range(4):
                    step(TILES - 4 + k, k)

            @block.scalar
            def _(act):
                def keep_xT(t, k):
                    act.wait_ge(xT_done, t + 1)
                    if later(t, 2):
                        act.wait_ge(up_done, FC * (t - 1))
                    nc.scalar.copy(xT[k % 2][:], psX[:, 0:TT]).then_inc(xT_kept, 1)

                def gelu(t, k, c):
                    act.wait_ge(up_done, FC * t + c + 1)
                    if later(t, 2) and c == 0:
                        act.wait_ge(down_done, t - 1)
                    nc.scalar.activation(hT[k % 2][:, c, :], psU[c][:, 0:TT], ACT.Gelu,
                                         bias=w[k][:, 2 * FF + c:2 * FF + c + 1]).then_inc(gelu_done, 1)

                keep_xT(0, 0)
                for c in range(FC):
                    gelu(0, 0, c)
                keep_xT(1, 1)

                def step(t, k):
                    for c in range(FC):
                        if has(t, 1):
                            gelu(t + 1, (k + 1) % 4, c)
                        if c == 1 and has(t, 2):
                            keep_xT(t + 2, k)
                over_tiles(act, step)

            @block.tensor
            def _(pe):
                mm = nc.tensor.matmul

                def times(t, k, ahead):
                    if type(t) is int:
                        return 16 * ((t + ahead) // 4 + 1)
                    return 16 * (loop[0] + (k + ahead) // 4 + 1)

                def transpose_x(t, k, ahead):
                    pe.wait_ge(rows_in[(k + ahead) % 4], times(t, k, ahead))
                    if later(t + ahead, 1):
                        pe.wait_ge(xT_kept, t + ahead)
                    for j in range(TB):
                        done = nc.tensor.transpose(psX[:, j * 128:(j + 1) * 128], xt[(k + ahead) % 4][:, j, 0:D], P("ident"))
                    done.then_inc(xT_done, 1)

                def up(t, k, c, ahead):
                    if c == 0:
                        pe.wait_ge(xT_kept, t + ahead + 1)
                        pe.wait_ge(w_kept, t + ahead + 1)
                    if later(t + ahead, 1):
                        pe.wait_ge(gelu_done, FC * (t + ahead - 1) + c + 1)
                    mm(psU[c][:, 0:TT], w[(k + ahead) % 4][:, c * 128:(c + 1) * 128], xT[(k + ahead) % 2][:],
                       start=True, stop=True).then_inc(up_done, 1)

                def down(t, k, j):
                    if j == 0:
                        pe.wait_ge(gelu_done, FC * t + FC)
                        if later(t, 2):
                            pe.wait_ge(yb_done, t - 1)
                    for c in range(FC):
                        done = mm(psY[k % 2][:, j * D:(j + 1) * D], hT[k % 2][:, c, j * 128:(j + 1) * 128],
                                  w[k][:, FF + c * D:FF + (c + 1) * D], start=c == 0, stop=c == FC - 1)
                    if j == TB - 1:
                        done.then_inc(down_done, 1)

                loop = [None]
                transpose_x(0, 0, 0)
                for c in range(FC):
                    up(0, 0, c, 0)
                transpose_x(0, 0, 1)

                def step(t, k):
                    for j in range(TB):
                        if has(t, 1):
                            up(t, k, 2 * j, 1)
                            up(t, k, 2 * j + 1, 1)
                        down(t, k, j)
                        if j == 0 and has(t, 2):
                            transpose_x(t, k, 2)
                for t in range(4):
                    step(t, t)
                with pe.Fori(1, TILES // 4 - 1) as q:
                    loop[0] = q
                    for k in range(4):
                        step(4 * q + k, k)
                for k in range(4):
                    step(TILES - 4 + k, k)


def host_consts():
    f = np.arange(CH)[None, :] * 128 + np.arange(128)[:, None]
    head = f // KEYS
    vm = np.zeros((128, CH, SLOTS), np.float32)
    for c in range(CH):
        for slot in range(SLOTS):
            if first_head(c) + slot < HH:
                vm[:, c, slot] = head[:, c] == first_head(c) + slot
    rowsel = np.zeros((128, CH, 128), np.float32)
    rowsel[:KEYS] = (f.T % KEYS)[None] == np.arange(KEYS)[:, None, None]
    km = ((np.arange(128)[:, None] // DH) % HH == np.arange(HH)[None, :]).astype(np.float32)
    return vm.reshape(128, -1), rowsel.reshape(128, -1), km


def kernel(x, ctx_1024, L0_xattn_Wq, L0_xattn_bq, L0_xattn_Wk, L0_xattn_bk, L0_xattn_Wv, L0_xattn_bv, L0_xattn_Wo,
           L0_xattn_bo, L0_ffn_W1, L0_ffn_b1, L0_ffn_W2, L0_ffn_b2, L1_xattn_Wq, L1_xattn_bq, L1_xattn_Wk,
           L1_xattn_bk, L1_xattn_Wv, L1_xattn_bv, L1_ffn_w_up, L1_ffn_w_down, L1_ffn_b_up, L1_ffn_b_down,
           L1_ffn_w_router):
    import ml_dtypes
    import concourse.bacc as _bacc
    from concourse import mybir as _mybir
    from concourse.bass_utils import run_bass_kernel_spmd as _run

    def f(a):
        return np.asarray(a)

    vm, rowsel, km = host_consts()
    col = lambda v: f(v).reshape(-1, 128).T
    rows = lambda v: np.broadcast_to(f(v)[None, :], (128, f(v).shape[0]))
    cols = {
        "Wq0": f(L0_xattn_Wq), "Wk0": f(L0_xattn_Wk),
        "Wv0": f(L0_xattn_Wv), "Wo0": f(L0_xattn_Wo),
        "W1T": f(L0_ffn_W1).T, "W2T": f(L0_ffn_W2).T.reshape(FC, 128, D).transpose(1, 0, 2).reshape(128, FF),
        "Wq1": f(L1_xattn_Wq), "Wk1": f(L1_xattn_Wk), "Wv1": f(L1_xattn_Wv), "router": f(L1_ffn_w_router).T,
        "bq0": col(L0_xattn_bq), "bk0": col(L0_xattn_bk), "bv0": col(L0_xattn_bv), "b1": col(L0_ffn_b1),
        "bq1": col(L1_xattn_bq), "bk1": col(L1_xattn_bk), "ident": np.eye(128, dtype=np.float32),
        "kmask": km, "vmask": vm, "rowsel": rowsel, "ones": np.ones((128, 128), np.float32), "bo0": rows(L0_xattn_bo),
        "b2": rows(L0_ffn_b2), "bv1": rows(L1_xattn_bv),
        "eidx": rows(np.arange(E, dtype=np.float32)),
        "steps": rows(np.arange(KMAX, dtype=np.float32) * TT), "part": np.arange(128, dtype=np.float32)[:, None],
    }
    pack = np.concatenate([cols[n].reshape(128, PACK[n][1]) for n in PACK], 1)
    padding = np.zeros((TT, ROW), np.float32)
    padding[:, ROW - 1] = (B * S + np.arange(TT, dtype=np.int32)).view(np.float32)
    ctxT = f(ctx_1024).transpose(2, 0, 1)
    arrays = {
        "x_in": f(x), "ctxT": ctxT, "pack": pack,
        "weights": np.concatenate([
            f(L1_ffn_w_up).transpose(0, 2, 1),
            f(L1_ffn_w_down).transpose(0, 2, 1).reshape(E, FC, 128, D).transpose(0, 2, 1, 3).reshape(E, 128, FF),
            f(L1_ffn_b_up).reshape(E, FC, 128).transpose(0, 2, 1),
            np.broadcast_to(f(L1_ffn_b_down)[:, None, :], (E, 128, D))], 2),
        "before": (np.arange(128)[:, None] < np.arange(128)[None, :]).astype(ml_dtypes.bfloat16),
        "tokens": (np.arange(B)[None, :] * S + np.arange(128)[:, None]).astype(np.int32),
        "padding": padding,
    }
    arrays = {k: np.ascontiguousarray(v) for k, v in arrays.items()}
    nc = _bacc.Bacc("TRN2", target_bir_lowering=False, num_devices=1)
    aps = [nc.dram_tensor(k, v.shape, _mybir.dt.from_np(v.dtype), kind="ExternalInput").ap() for k, v in arrays.items()]
    out = nc.dram_tensor("out", (B * S + TT, D), F32, kind="ExternalOutput").ap()
    build(nc, *aps, out)
    r = _run(nc, [arrays], core_ids=[0])
    return r.results[0]["out"][:B * S].reshape(B, S, D)
```
